# Optimizing a Trainium2 kernel written in Bass

```python
import numpy as np
import jax
import jax.numpy as jnp

def _softmax(x, axis=-1):
    return jax.nn.softmax(x, axis=axis)

def _gelu(x):
    return jax.nn.gelu(x, approximate=True)

def _silu(x):
    return jax.nn.silu(x)

def _sigmoid(x):
    return jax.nn.sigmoid(x)

def _layernorm(x, axis=-1, eps=1e-05):
    m = jnp.mean(x, axis=axis, keepdims=True)
    v = jnp.var(x, axis=axis, keepdims=True)
    return (x - m) / jnp.sqrt(v + eps)

def _scatter_add(tgt, idx, src, axis=0):
    return tgt.at[idx].add(src)

def _segment_sum(src, seg, n):
    return jax.ops.segment_sum(src, seg, n)
kernel_name = 'mk_gnn_resnorm_d2_gnn_r32_8faef9'

def setup_inputs(seed: int=0):
    np.random.seed(seed)
    _w = jnp.asarray

    def _rec_inputs():
        import jax
        import jax.numpy as jnp
        _gk = jax.random.key(seed)
        x = -0.0001126 + 1 * jax.random.normal(jax.random.fold_in(_gk, 1), (10000, 768), jnp.float32)
        src = jax.random.randint(jax.random.fold_in(_gk, 2), (10000,), 0, 10000, jnp.int32)
        dst = jax.random.randint(jax.random.fold_in(_gk, 3), (10000,), 0, 10000, jnp.int32)
        _o = jnp.argsort(dst, stable=True)
        src = src[_o]
        dst = dst[_o]
        return (x, src, dst)
    x, src, dst = _rec_inputs()

    def _L0_gnn_setup():
        import jax, jax.numpy as jnp
        import numpy as np
        NEG_SLOPE = 0.2

        def _gat_layer(x, W, a_src, a_dst, b, src, dst, n_nodes):
            h = x @ W
            e_src = h @ a_src
            e_dst = h @ a_dst
            e = jax.nn.leaky_relu(e_src[src] + e_dst[dst], NEG_SLOPE)
            m = jax.ops.segment_max(e, dst, num_segments=n_nodes)
            w = jnp.exp(e - m[dst])
            z = jax.ops.segment_sum(w, dst, num_segments=n_nodes)
            alpha = w / z[dst]
            out = jax.ops.segment_sum(h[src] * alpha[:, None], dst, num_segments=n_nodes)
            return out + b
        key = jax.random.key(seed)
        ks = jax.random.split(key, 10)
        N, E, D = (10000, 3125, 768)
        scale = 1.0 / np.sqrt(D)
        x = jax.random.normal(ks[0], (N, D), dtype=jnp.float32)
        edge_index = jax.random.randint(ks[1], (2, E), 0, N, dtype=jnp.int32)
        params = {}
        for i, nm in enumerate(['1', '2']):
            params[f'W{nm}'] = jax.random.normal(ks[2 + 4 * i], (D, D), jnp.float32) * scale
            params[f'att_src{nm}'] = jax.random.normal(ks[3 + 4 * i], (D,), jnp.float32) * scale
            params[f'att_dst{nm}'] = jax.random.normal(ks[4 + 4 * i], (D,), jnp.float32) * scale
            params[f'b{nm}'] = jnp.zeros((D,), jnp.float32)
        return {'x': x, 'edge_index': edge_index, **params}
    _L0_gnn_all = _L0_gnn_setup()
    _L0_gnn_in = {k: v for k, v in _L0_gnn_all.items() if k in ('W1', 'att_src1', 'att_dst1', 'b1', 'W2', 'att_src2', 'att_dst2', 'b2')}
    del _L0_gnn_all

    def _L1_gnn_setup():
        import jax, jax.numpy as jnp
        import numpy as np
        N = 625
        E_RAND = 10000
        NEG_SLOPE = 0.2

        def gat_layer(x, W, a_src, a_dst, bias, src, dst, heads, out_c, concat):
            n = x.shape[0]
            h = (x @ W).reshape(n, heads, out_c)
            al_s = jnp.einsum('nhc,hc->nh', h, a_src)
            al_d = jnp.einsum('nhc,hc->nh', h, a_dst)
            e = jax.nn.leaky_relu(al_s[src] + al_d[dst], NEG_SLOPE)
            m = jax.ops.segment_max(e, dst, num_segments=n)
            ex = jnp.exp(e - m[dst])
            z = jax.ops.segment_sum(ex, dst, num_segments=n)
            alpha = ex / (z[dst] + 1e-16)
            msg = h[src] * alpha[:, :, None]
            out = jax.ops.segment_sum(msg, dst, num_segments=n)
            out = out.reshape(n, heads * out_c) if concat else out.mean(axis=1)
            return out + bias
        key = jax.random.key(seed)
        ks = jax.random.split(key, 10)
        x = jax.random.normal(ks[0], (N, 768), dtype=jnp.float32)
        src = jax.random.randint(ks[1], (E_RAND,), 0, N)
        dst = jax.random.randint(ks[2], (E_RAND,), 0, N)
        loop = jnp.arange(N)
        edge_index = jnp.stack([jnp.concatenate([src, loop]), jnp.concatenate([dst, loop])])
        s = 1.0 / np.sqrt(768.0)
        W1 = jax.random.normal(ks[3], (768, 768), dtype=jnp.float32) * s
        a_src1 = jax.random.normal(ks[4], (8, 96), dtype=jnp.float32) * 0.1
        a_dst1 = jax.random.normal(ks[5], (8, 96), dtype=jnp.float32) * 0.1
        b1 = jnp.zeros((768,), dtype=jnp.float32)
        W2 = jax.random.normal(ks[6], (768, 768), dtype=jnp.float32) * s
        a_src2 = jax.random.normal(ks[7], (1, 768), dtype=jnp.float32) * 0.1
        a_dst2 = jax.random.normal(ks[8], (1, 768), dtype=jnp.float32) * 0.1
        b2 = jnp.zeros((768,), dtype=jnp.float32)
        return {'x': x, 'edge_index': edge_index, 'W1': W1, 'a_src1': a_src1, 'a_dst1': a_dst1, 'b1': b1, 'W2': W2, 'a_src2': a_src2, 'a_dst2': a_dst2, 'b2': b2}
    _L1_gnn_all = _L1_gnn_setup()
    _L1_gnn_in = {k: v for k, v in _L1_gnn_all.items() if k in ('W1', 'a_src1', 'a_dst1', 'b1', 'W2', 'a_src2', 'a_dst2', 'b2')}
    del _L1_gnn_all
    return {'x': x, 'src': src, 'dst': dst, 'L0_gnn_W1': _L0_gnn_in['W1'], 'L0_gnn_att_src1': _L0_gnn_in['att_src1'], 'L0_gnn_att_dst1': _L0_gnn_in['att_dst1'], 'L0_gnn_b1': _L0_gnn_in['b1'], 'L0_gnn_W2': _L0_gnn_in['W2'], 'L0_gnn_att_src2': _L0_gnn_in['att_src2'], 'L0_gnn_att_dst2': _L0_gnn_in['att_dst2'], 'L0_gnn_b2': _L0_gnn_in['b2'], 'L1_gnn_W1': _L1_gnn_in['W1'], 'L1_gnn_a_src1': _L1_gnn_in['a_src1'], 'L1_gnn_a_dst1': _L1_gnn_in['a_dst1'], 'L1_gnn_b1': _L1_gnn_in['b1'], 'L1_gnn_W2': _L1_gnn_in['W2'], 'L1_gnn_a_src2': _L1_gnn_in['a_src2'], 'L1_gnn_a_dst2': _L1_gnn_in['a_dst2'], 'L1_gnn_b2': _L1_gnn_in['b2']}

def reference(x, src, dst, L0_gnn_W1, L0_gnn_att_src1, L0_gnn_att_dst1, L0_gnn_b1, L0_gnn_W2, L0_gnn_att_src2, L0_gnn_att_dst2, L0_gnn_b2, L1_gnn_W1, L1_gnn_a_src1, L1_gnn_a_dst1, L1_gnn_b1, L1_gnn_W2, L1_gnn_a_src2, L1_gnn_a_dst2, L1_gnn_b2):
    import jax
    import jax.numpy as jnp

    def _L0_gnn_ref(x, edge_index, W1, att_src1, att_dst1, b1, W2, att_src2, att_dst2, b2):
        import jax, jax.numpy as jnp
        import numpy as np
        NEG_SLOPE = 0.2

        def _gat_layer(x, W, a_src, a_dst, b, src, dst, n_nodes):
            h = x @ W
            e_src = h @ a_src
            e_dst = h @ a_dst
            e = jax.nn.leaky_relu(e_src[src] + e_dst[dst], NEG_SLOPE)
            m = jax.ops.segment_max(e, dst, num_segments=n_nodes)
            w = jnp.exp(e - m[dst])
            z = jax.ops.segment_sum(w, dst, num_segments=n_nodes)
            alpha = w / z[dst]
            out = jax.ops.segment_sum(h[src] * alpha[:, None], dst, num_segments=n_nodes)
            return out + b
        n_nodes = x.shape[0]
        loops = jnp.arange(n_nodes, dtype=edge_index.dtype)
        src = jnp.concatenate([edge_index[0], loops])
        dst = jnp.concatenate([edge_index[1], loops])
        h = _gat_layer(x, W1, att_src1, att_dst1, b1, src, dst, n_nodes)
        h = jax.nn.relu(h)
        out = _gat_layer(h, W2, att_src2, att_dst2, b2, src, dst, n_nodes)
        return out

    def _L1_gnn_ref(x, edge_index, W1, a_src1, a_dst1, b1, W2, a_src2, a_dst2, b2):
        import jax, jax.numpy as jnp
        import numpy as np
        N = 625
        E_RAND = 10000
        NEG_SLOPE = 0.2

        def gat_layer(x, W, a_src, a_dst, bias, src, dst, heads, out_c, concat):
            n = x.shape[0]
            h = (x @ W).reshape(n, heads, out_c)
            al_s = jnp.einsum('nhc,hc->nh', h, a_src)
            al_d = jnp.einsum('nhc,hc->nh', h, a_dst)
            e = jax.nn.leaky_relu(al_s[src] + al_d[dst], NEG_SLOPE)
            m = jax.ops.segment_max(e, dst, num_segments=n)
            ex = jnp.exp(e - m[dst])
            z = jax.ops.segment_sum(ex, dst, num_segments=n)
            alpha = ex / (z[dst] + 1e-16)
            msg = h[src] * alpha[:, :, None]
            out = jax.ops.segment_sum(msg, dst, num_segments=n)
            out = out.reshape(n, heads * out_c) if concat else out.mean(axis=1)
            return out + bias
        src, dst = (edge_index[0], edge_index[1])
        h = gat_layer(x, W1, a_src1, a_dst1, b1, src, dst, heads=8, out_c=96, concat=True)
        h = jax.nn.elu(h)
        out = gat_layer(h, W2, a_src2, a_dst2, b2, src, dst, heads=1, out_c=768, concat=False)
        return out
    edge_index = jnp.stack([src, dst])
    x = _layernorm(x + _L0_gnn_ref(x, edge_index, L0_gnn_W1, L0_gnn_att_src1, L0_gnn_att_dst1, L0_gnn_b1, L0_gnn_W2, L0_gnn_att_src2, L0_gnn_att_dst2, L0_gnn_b2), axis=-1)
    x = _layernorm(x + _L1_gnn_ref(x, edge_index, L1_gnn_W1, L1_gnn_a_src1, L1_gnn_a_dst1, L1_gnn_b1, L1_gnn_W2, L1_gnn_a_src2, L1_gnn_a_dst2, L1_gnn_b2), axis=-1)
    return x

_drawn_inputs = setup_inputs


def setup_inputs(seed=0):
    import zlib

    import numpy as np

    out = dict(_drawn_inputs(seed))
    spreads = {'L0_gnn_b1': (0.0, 0.1),
     'L0_gnn_b2': (0.0, 0.1),
     'L1_gnn_b1': (0.0, 0.1),
     'L1_gnn_b2': (0.0, 0.1)}
    factors = {}
    for name, (base, spread) in spreads.items():
        noise = np.random.default_rng([zlib.crc32(name.encode()), seed]).standard_normal(out[name].shape)
        drawn = base * np.exp(spread * noise) if base else spread * noise
        out[name] = jnp.asarray(drawn.astype(out[name].dtype))
    for name, factor in factors.items():
        out[name] = (out[name] * factor).astype(out[name].dtype)
    return out
```

```python
from contextlib import ExitStack

import concourse.bass as bass
from concourse import mybir

F32 = mybir.dt.float32
I32 = mybir.dt.int32
BF16 = mybir.dt.bfloat16
ALU = mybir.AluOpType
ACT = mybir.ActivationFunctionType
AX = mybir.AxisListType

P = 128
D = 768
KT = D // P
TN = 125
HALF = 64
HN = [HALF, TN - HALF]
WIN = 128
BIG = 1e30
FAR = 1 << 20
SLOPE = 0.2
EPS = 1e-5
OB = 512
HC = D // 2
PEEL = 4


class Net:
    pass


def steps(eng, n_tiles, first, last, step):
    for s in range(first, PEEL):
        step(s, s % 2)
    n_loop = (n_tiles - PEEL - 2) // 2
    with eng.Fori(0, n_loop) as i:
        step(2 * i + PEEL, 0)
        step(2 * i + PEEL + 1, 1)
    for s in range(PEEL + 2 * n_loop, n_tiles + last):
        step(s, s % 2)


def has(s, n_tiles):
    return not isinstance(s, int) or 0 <= s < n_tiles


def nth(s):
    return s // 2 + 1


def bcast(ap, at, n):
    return ap.unsqueeze(at).to_broadcast([*ap.shape[:at], n, *ap.shape[at:]])


def prepare(nc, net, ext, sem):
    N, E, NT = net.N, net.E, net.NT
    NW = 2 * NT
    KE = E // TN
    src, dst = ext["src"], ext["dst"]
    with ExitStack() as ctx:
        def sb(name, shape, dt=F32):
            return ctx.enter_context(nc.sbuf_tensor(name, shape, dt))

        padding = sb("padding", [2, WIN], I32)
        dst_i = sb("dst_i", [TN, KE], I32)
        next_i = sb("next_i", [TN, KE], I32)
        dst_f = sb("dst_f", [TN, KE])
        next_f = sb("next_f", [TN, KE])
        falls = sb("falls", [TN, KE])
        any_fall = sb("any_fall", [TN, 1])
        starts_i = sb("starts_i", [P, NT, 2], I32)
        starts = sb("starts", [P, NT, 2])
        CK = 20
        before = sb("before", [TN, 2, CK, NW], BF16)
        ones_bf = sb("ones_bf", [TN, 1], BF16)
        lo = sb("lo", [1, NW + 1])
        over = sb("over", [1, NW])
        worst = sb("worst", [1, 2])
        lo_i = sb("lo_i", [1, NW], I32)
        win_i = sb("win_i", [NT, 2, 2, WIN], I32)
        win_f = sb("win_f", [NT, 2, 2, WIN])
        a_rows = sb("a_rows", [P, 8, D])
        prod = sb("prod", [P, KT, D])
        ident_i = sb("ident_i", [P, P], I32)
        cols = sb("cols", [P, 6, KT])

        s_pad = sem("p_pad"); s_edges = sem("p_edges"); s_dst = sem("p_dst"); s_w = sem("p_weights")
        s_iota = sem("p_iota"); s_chain = sem("p_chain"); s_cmp = sem("p_cmp"); s_cmp_used = sem("p_cmp_used")
        s_lo = sem("p_lo"); s_loi = sem("p_loi"); s_win = [sem("p_win0"), sem("p_win1")]
        s_load = sem("p_load"); s_winf = sem("p_winf"); s_tr = sem("p_tr"); s_viol = sem("p_viol")
        s_cols = sem("p_cols"); s_bc = sem("p_bc"); s_bce = sem("p_bce"); s_ones = sem("p_ones"); s_padm = sem("p_padm")

        n_chunks = -(-KE // CK)
        folds = [("v1s", net.w[0], 0), ("v1d", net.w[0], 1), ("v2s", net.w[1], 2), ("v2d", net.w[1], 3),
                 ("v4s", net.w[3], 6), ("v4d", net.w[3], 7)]

        with nc.Block() as block:
            @block.sync
            def _(sp):
                sp.dma_start(net.edges[0, 0:E], src).then_inc(s_edges, 16)
                sp.dma_start(net.edges[1, 0:E], dst).then_inc(s_edges, 16)
                sp.dma_start(dst_i[:, :], dst.rearrange("(p k) -> p k", k=KE)).then_inc(s_dst, 16)
                sp.wait_ge(s_padm, 1)
                sp.dma_start(net.edges[:, E:E + WIN], padding[:, :]).then_inc(s_edges, 16)
                sp.wait_ge(s_edges, 48)
                sp.dma_start(next_i[:, :], net.edges[1, 1:E + 1].rearrange("(p k) -> p k", k=KE)).then_inc(s_dst, 16)
                for j, name in enumerate(("L0_gnn_W1", "L0_gnn_W2", "L1_gnn_W2")):
                    sp.dma_start(net.w[(0, 1, 3)[j]][:, :, :], ext[name].rearrange("(k p) n -> p k n", p=P)).then_inc(s_w, 16)
                sp.dma_start(net.w[2][:, :, 0:D], ext["L1_gnn_W1"].rearrange("(k p) n -> p k n", p=P)).then_inc(s_w, 16)
                sp.wait_ge(s_loi, 1)
                with sp.Fori(0, NT) as t:
                    at = sp.value_load(lo_i[0:1, bass.ds(2 * t, 1)], min_val=0, max_val=E)
                    sp.dma_start(net.windows[2 * t], net.edges[:, bass.ds(at, WIN)]).then_inc(s_win[0], 16)
                sp.wait_ge(s_win[0], 16 * NT)
                sp.wait_ge(s_win[1], 16 * NT)
                sp.dma_start(win_i[:, :, :, :], net.windows.rearrange("(t h) s e -> t h s e", h=2)).then_inc(s_load, 16)

            @block.scalar
            def _(act):
                vectors = ("L0_gnn_att_src1", "L0_gnn_att_dst1", "L0_gnn_att_src2", "L0_gnn_att_dst2",
                           "L1_gnn_a_src1", "L1_gnn_a_dst1", "L1_gnn_a_src2", "L1_gnn_a_dst2")
                for j, name in enumerate(vectors):
                    v = ext[name] if len(ext[name].shape) == 1 else ext[name].rearrange("h c -> (h c)")
                    act.dma_start(a_rows[:, j, :], bcast(v, 0, P)).then_inc(s_w, 16)
                for j, name in enumerate(("L0_gnn_b1", "L0_gnn_b2", "L1_gnn_b1", "L1_gnn_b2")):
                    act.dma_start(net.bias[:, j, :], bcast(ext[name], 0, P)).then_inc(s_w, 16)
                act.wait_ge(s_loi, 1)
                with act.Fori(0, NT) as t:
                    at = act.value_load(lo_i[0:1, bass.ds(2 * t + 1, 1)], min_val=0, max_val=E)
                    act.dma_start(net.windows[2 * t + 1], net.edges[:, bass.ds(at, WIN)]).then_inc(s_win[1], 16)

            @block.gpsimd
            def _(pool):
                nc.gpsimd.iota(padding[:, :], pattern=[[0, WIN]], base=0, channel_multiplier=FAR).then_inc(s_padm, 1)
                nc.gpsimd.iota(starts_i[:, :, :], pattern=[[TN, NT], [HALF, 2]], base=0, channel_multiplier=0).then_inc(s_iota, 1)
                nc.gpsimd.iota(net.node_ids_i[:, :], pattern=[[TN, NT]], base=0, channel_multiplier=1).then_inc(s_iota, 1)
                nc.gpsimd.iota(net.node_i[:, :, :], pattern=[[0, 2], [1, HALF]], base=0, channel_multiplier=0).then_inc(s_iota, 1)
                nc.gpsimd.iota(ident_i[:, :], pattern=[[1, P]], base=0, channel_multiplier=-1).then_inc(s_iota, 1)

            @block.vector
            def _(dve):
                n = [0]

                def link(ins):
                    n[0] += 1
                    ins.then_inc(s_chain, 1)
                    dve.wait_ge(s_chain, n[0])

                nc.vector.memset(ones_bf[:, :], 1.0).then_inc(s_ones, 1)
                nc.vector.memset(net.ones[:, :], 1.0).then_inc(s_ones, 1)
                nc.vector.memset(net.minus_half[:, :], -0.5)
                nc.vector.memset(lo[0:1, NW:NW + 1], float(E))
                dve.wait_ge(s_iota, 4)
                nc.vector.tensor_copy(net.node_ids[:, :], net.node_ids_i[:, :])
                nc.vector.tensor_copy(starts[:, :, :], starts_i[:, :, :])
                nc.vector.tensor_copy(net.node[:, :, :], net.node_i[:, :, :])
                nc.vector.tensor_scalar(net.ident[:, :], ident_i[:, :], 0.0, None, ALU.is_equal).then_inc(s_ones, 1)
                dve.wait_ge(s_dst, 32)
                nc.vector.tensor_copy(next_f[:, :], next_i[:, :])
                link(nc.vector.tensor_copy(dst_f[:, :], dst_i[:, :]))
                for c in range(n_chunks):
                    k0, k1 = c * CK, min(KE, c * CK + CK)
                    if c >= 2:
                        dve.wait_ge(s_cmp_used, c - 1)
                    nc.vector.tensor_tensor(
                        before[:, c % 2, 0:k1 - k0, :], bcast(dst_f[:, k0:k1], 2, NW),
                        bcast(starts[0:TN, :, :].rearrange("p t h -> p (t h)"), 1, k1 - k0), ALU.is_lt).then_inc(s_cmp, 1)
                link(nc.vector.tensor_tensor(falls[:, :], dst_f[:, :], next_f[:, :], ALU.is_gt))
                nc.vector.tensor_reduce(any_fall[:, :], falls[:, :], AX.X, ALU.max).then_inc(s_viol, 1)
                dve.wait_ge(s_lo, 1)
                nc.vector.tensor_copy(lo_i[0:1, :], net.bank[0][0:1, 0:NW]).then_inc(s_loi, 1)
                link(nc.vector.tensor_copy(lo[0:1, 0:NW], net.bank[0][0:1, 0:NW]))
                link(nc.vector.tensor_tensor(over[:, :], lo[0:1, 1:NW + 1], lo[0:1, 0:NW], ALU.subtract))
                link(nc.vector.tensor_reduce(worst[0:1, 0:1], over[:, :], AX.X, ALU.max))
                link(nc.vector.tensor_scalar(worst[0:1, 1:2], worst[0:1, 0:1], float(WIN), None, ALU.is_gt))
                nc.vector.tensor_tensor(net.flag[0:1, 0:1], worst[0:1, 1:2], net.bank[1][0:1, 0:1], ALU.add)
                dve.wait_ge(s_w, 16 * 16)
                for j, (_, w, a) in enumerate(folds):
                    for k in range(KT):
                        ins = nc.vector.tensor_tensor_reduce(prod[:, k, :], w[:, k, :], a_rows[:, a, :], 1.0, 0.0,
                                                             ALU.mult, ALU.add, cols[:, j, k:k + 1])
                    link(ins)
                dve.sem_inc(s_cols, 1)
                for a, c in ((4, D), (5, D + 8)):
                    link(nc.vector.tensor_tensor(prod[:, :, :], net.w[2][:, :, 0:D], bcast(a_rows[:, a, :], 1, KT), ALU.mult))
                    link(nc.vector.tensor_reduce(net.w[2][:, :, c:c + 8], prod[:, :, :].rearrange("p k (h c) -> p k h c", h=8),
                                                 AX.X, ALU.add))
                for j in range(6):
                    dve.wait_ge(s_bc, j + 1)
                    nc.vector.tensor_copy(net.v[:, j, :].rearrange("p (b c) -> p b c", b=2),
                                          net.bank2(2)[:, :, 0:HC]).then_inc(s_bce, 1)
                dve.wait_ge(s_load, 16)
                nc.vector.tensor_copy(win_f[:, :, :, :], win_i[:, :, :, :]).then_inc(s_winf, 1)
                dve.wait_ge(s_tr, 4)
                for h in range(2):
                    nc.vector.tensor_copy(net.src_idx[:, :, h], net.bank[4][:, (2 * h) * NT:(2 * h + 1) * NT])
                    nc.vector.tensor_tensor(net.dst_rel[:, :, h], net.bank[4][:, (2 * h + 1) * NT:(2 * h + 2) * NT],
                                            starts[:, :, h], ALU.subtract)

            @block.tensor
            def _(pe):
                pe.wait_ge(s_ones, 3)
                for c in range(n_chunks):
                    pe.wait_ge(s_cmp, c + 1)
                    for k in range(c * CK, min(KE, c * CK + CK)):
                        ins = nc.tensor.matmul(net.bank[0][0:1, 0:NW], ones_bf[:, :], before[:, c % 2, k - c * CK, :],
                                               start=(k == 0), stop=(k == KE - 1))
                    ins.then_inc(s_cmp_used, 1)
                pe.wait_ge(s_viol, 1)
                nc.tensor.matmul(net.bank[1][0:1, 0:1], any_fall[:, :], net.ones[0:TN, 0:1], start=True, stop=True).then_inc(s_lo, 1)
                pe.wait_ge(s_cols, 1)
                for j in range(6):
                    if j >= 1:
                        pe.wait_ge(s_bce, j)
                    for k in range(KT):
                        c = (k % 3) * P
                        ins = nc.tensor.matmul(net.bank2(2)[:, k // 3, c:c + P], bcast(cols[:, j, k], 1, P), net.ident[:, :],
                                               start=(k % 3 == 0), stop=True, skip_group_check=True)
                    ins.then_inc(s_bc, 1)
                pe.wait_ge(s_winf, 1)
                for h in range(2):
                    for s in range(2):
                        nc.tensor.transpose(net.bank[4][:, (2 * h + s) * NT:(2 * h + s + 1) * NT], win_f[:, h, s, :],
                                            net.ident[0:NT, 0:NT]).then_inc(s_tr, 1)


def attention_phase(nc, net, name, sem, *, heads, own, table, row, weights, residual, bias, out_kind):
    NT, H = net.NT, heads
    kind = out_kind
    first_layer = kind == "A"
    lag = 1 if kind == "B" else 0
    with ExitStack() as ctx:
        def sb(n, shape, dt=F32):
            return ctx.enter_context(nc.sbuf_tensor(f"{name}_{n}", shape, dt))

        def two(n, shape, dt=F32):
            return [sb(f"{n}{i}", shape, dt) for i in range(2)]

        def s_(n):
            return sem(f"{name}_{n}")

        XW = D + 8
        idx = two("idx", [P, 2], I32)
        rows = two("rows", [P, 2, XW])
        mine = two("mine", [TN, D]) if own else None
        resid = two("resid", [TN, D]) if residual is not None else None
        onehot = two("onehot", [P, 2, HALF])
        neg = two("neg", [P, 2, HALF])
        masked = two("masked", [P, H, 2, HALF])
        onehot_t = two("onehot_t", [TN, WIN])
        smax = two("smax", [TN, H])
        msum = two("msum", [TN, H])
        nd = two("nd", [TN, 2 * H])
        eself = two("eself", [TN, 1]) if own else None
        us = two("us", [TN, 4]) if own else None
        xself = two("xself", [TN, 1]) if own else None
        diag = two("diag", [TN, TN + 1]) if own else None
        e1 = two("e1", [P, 2, H]); e2 = two("e2", [P, 2, H]); e3 = two("e3", [P, 2, H]); e4 = two("e4", [P, 2, H])
        ex = two("ex", [P, 2, H])
        coef = two("coef", [P, 2, HALF]) if H == 1 else None
        zsum = two("zsum", [TN, H]); rz = two("rz", [TN, H])
        yt = two("yt", [P, KT, TN + 1]) if weights is not None else None
        scaled = two("scaled", [P, 2, XW]) if H > 1 else None
        onehot_k = two("onehot_k", [P, 2, HALF]) if H > 1 else None
        junk = [sb(f"junk{i}", [P, D]) for i in range(6)]
        o1 = two("o1", [TN, D])
        o2 = two("o2", [TN, D + 2])
        o3 = two("o3", [TN, D]) if kind == "C" else None
        st6 = two("st6", [TN, 2, 6]); mv = two("mv", [TN, 2]); rs = two("rs", [TN, 8])
        x1t = two("x1t", [P, KT, TN + 1]) if kind == "B" else None
        hrow = two("hrow", [TN, D + 16]) if kind == "B" else None

        q_idx = s_("idx"); q_gather = [[s_("gather00"), s_("gather01")], [s_("gather10"), s_("gather11")]]
        q_own = [s_("own0"), s_("own1")]; q_res = [s_("res0"), s_("res1")]
        c_front = s_("c_front"); c_mid = s_("c_mid"); c_exp = s_("c_exp"); c_back = s_("c_back"); c_evac = s_("c_evac")
        q_masked = s_("masked"); q_mt = s_("mt"); q_nd = s_("nd"); q_g = s_("g"); q_dself = s_("dself"); q_xself = s_("xself")
        q_logit = s_("logit"); q_exp = s_("exp"); q_coef = s_("coef"); q_diag = s_("diag"); q_agg = s_("agg")
        q_y = s_("y"); q_rz = s_("rz"); q_o = s_("o"); q_oread = s_("oread"); q_pre = s_("pre"); q_out = s_("out"); q_e2 = s_("e2")
        q_store = [s_("store0"), s_("store1")]; q_ecopy = s_("ecopy"); q_resb = s_("resb"); q_var = s_("var"); q_pow = s_("pow")
        q_t1 = s_("t1"); q_t1e = s_("t1e"); q_h = s_("h"); q_he = s_("he"); q_hstore = [s_("hstore0"), s_("hstore1")]
        q_gath_free = q_agg
        q_scaled = s_("scaled"); q_neg = s_("negx"); q_zero = s_("zero"); q_ndin = s_("ndin")
        q_go = s_("go"); q_go2 = s_("go2")
        q_b = s_("b"); q_c1 = s_("c1"); q_c2 = s_("c2"); q_mvr = s_("mvr")

        bank = net.bank
        if kind == "C":
            ps_m = net.bank2(4)
            ps_g = bank[6]
            ps_o = [net.bank2(0), net.bank2(2)]
            ps_y = None
        else:
            ps_m = None
            ps_o = [net.bank2(0), net.bank2(0) if kind == "B" else net.bank2(2)]
            ps_h = net.bank2(2)
            ps_y = net.bank2(4)
            ps_g = bank[6]
        ps_mt = bank[7] if kind != "C" else None
        EC = 256
        ps_e = net.psum[:, 6:8, EC:EC + 2 * H]
        n_o = 1 if kind == "B" else 2
        ZC = 8

        def sources(p):
            return rows[p][:, :, D:D + H]

        with nc.Block() as block:
            @block.sync
            def _(sp):
                def step(s, p):
                    t = s + 2
                    if has(t, NT):
                        if own:
                            if not isinstance(s, int) or s >= 0:
                                sp.wait_ge(q_agg, t - 1)
                            sp.dma_start(mine[p][:, :], net.tiles(table)[t][:, 0:D]).then_inc(q_own[p], 16)
                    t = s + 1
                    if has(t, NT) and residual is not None:
                        if not isinstance(s, int) or s >= 1:
                            sp.wait_ge(q_pre, t - 1)
                        sp.dma_start(resid[1 - p][:, :], net.tiles(residual)[t]).then_inc(q_res[1 - p], 16)
                    t = s - 1
                    if has(t, NT):
                        sp.wait_ge(q_out, t + 1)
                        if kind in "AC":
                            sp.wait_ge(q_e2, t + 1)
                            sp.dma_start(net.tiles(net.g[kind])[t], o2[1 - p][:, :]).then_inc(q_store[1 - p], 16)
                        elif kind == "B":
                            sp.dma_start(net.tiles(net.x1)[t], o2[1 - p][:, 0:D]).then_inc(q_store[1 - p], 16)
                        else:
                            sp.dma_start(net.tiles(net.out)[t], o2[1 - p][:, 0:D]).then_inc(q_store[1 - p], 16)
                    t = s - 2
                    if kind == "B" and has(t, NT):
                        sp.wait_ge(q_he, t + 1)
                        sp.dma_start(net.tiles(net.h)[t], hrow[p][:, :]).then_inc(q_hstore[p], 16)
                steps(sp, NT, -2, 1 + lag, step)
                for q in q_store + (q_hstore if kind == "B" else []):
                    sp.wait_ge(q, 16 * (NT // 2))

            @block.gpsimd
            def _(pool):
                def step(s, p):
                    t = s + 2
                    if has(t, NT):
                        if not isinstance(s, int) or s >= 0:
                            for h in range(2):
                                pool.wait_ge(q_gather[p][h], 16 * nth(s))
                        nc.gpsimd.tensor_copy(idx[p][:, :], net.src_idx[:, t, :]).then_inc(q_idx, 1)
                        pool.wait_ge(q_idx, t + 1)
                        if not isinstance(s, int) or s >= 0:
                            pool.wait_ge(q_gath_free if kind != "C" else q_scaled, t - 1)
                        pool.sem_inc(q_go, 1)
                        for h in range(2):
                            nc.gpsimd.indirect_dma_start(
                                out=rows[p][:, h, 0:row], out_offset=None, in_=table[:, :],
                                in_offset=bass.IndirectOffsetOnAxis(ap=idx[p][:, h:h + 1], axis=0)).then_inc(q_gather[p][h], 16)
                    t = s + 1
                    if has(t, NT) and kind == "B":
                        pool.wait_ge(q_res[1 - p], 16 * nth(t))
                        nc.gpsimd.tensor_tensor(resid[1 - p][:, :], resid[1 - p][:, :], net.bias[0:TN, bias, :], ALU.add).then_inc(q_resb, 1)
                    if has(t, NT) and kind == "D":
                        pool.wait_ge(q_res[1 - p], 16 * nth(t))
                        nc.gpsimd.tensor_tensor(resid[1 - p][:, :], resid[1 - p][:, :], net.bias[0:TN, bias, :], ALU.add).then_inc(q_resb, 1)
                    t = s - 1
                    if has(t, NT) and kind in "BD":
                        pool.wait_ge(q_var, t + 1)
                        nc.gpsimd.tensor_tensor(rs[1 - p][:, 1:2], rs[1 - p][:, 0:1], net.minus_half[0:TN, :], ALU.pow).then_inc(q_pow, 1)
                    if has(t, NT) and kind in "AC":
                        pool.wait_ge(q_e2, t + 1)
                        nc.gpsimd.tensor_copy(net.e_own[:, t, :], o2[1 - p][:, D:D + 2]).then_inc(q_ecopy, 1)
                steps(pool, NT, -2, 1, step)
                pool.wait_ge(q_idx, NT)

            @block.scalar
            def _(act):
                def step(s, p):
                    t, q = s - 1, 1 - p
                    if has(t, NT):
                        if kind == "A":
                            act.wait_ge(q_pre, t + 1)
                            if not isinstance(t, int) or t >= 2:
                                act.wait_ge(q_store[q], 16 * (nth(t) - 1))
                            nc.scalar.activation(o2[q][:, 0:D], o1[q][:, :], ACT.Relu).then_inc(q_out, 1)
                        if kind in "BD":
                            act.wait_ge(q_mvr, t + 1)
                            if not isinstance(t, int) or t >= 2:
                                act.wait_ge(q_store[q], 16 * (nth(t) - 1))
                            nc.scalar.activation(o2[q][:, 0:D], o1[q][:, :], ACT.Identity, bias=rs[q][:, 6:7],
                                                 scale=rs[q][:, 5:6]).then_inc(q_out, 1)
                        if kind == "C":
                            act.wait_ge(q_b, t + 1)
                            nc.scalar.activation(o3[q][:, :], o1[q][:, :], ACT.Relu, scale=-1.0).then_inc(q_c1, 1)
                            act.wait_ge(q_c1, t + 1)
                            nc.scalar.activation(o3[q][:, :], o3[q][:, :], ACT.Exp, scale=-1.0).then_inc(q_c2, 1)
                    t, q = s + 1, 1 - p
                    if has(t, NT):
                        if own:
                            act.wait_ge(q_dself, t + 1)
                            nc.scalar.activation(xself[q][:, :], us[q][:, 2:3], ACT.Exp).then_inc(q_xself, 1)
                        act.wait_ge(q_logit, t + 1)
                        nc.scalar.activation(ex[q][:, :, :], e4[q][:, :, :], ACT.Exp).then_inc(q_exp, 1)
                        if weights is not None:
                            act.wait_ge(q_agg, t + 1)
                            if not isinstance(s, int) or s >= 1:
                                act.wait_ge(q_o, t - 1)
                            for b in range(2):
                                nc.scalar.copy(yt[q][:, 3 * b:3 * b + 3, :].rearrange("p k n -> p (k n)"),
                                               ps_y[:, b, 0:3 * (TN + 1)]).then_inc(q_y, 1)
                    t, q = s - 1, 1 - p
                    if kind == "B" and has(t, NT):
                        act.wait_ge(q_t1, t + 1)
                        if not isinstance(t, int) or t >= 2:
                            act.wait_ge(q_h, t - 1)
                        for b in range(2):
                            nc.scalar.copy(x1t[q][:, 3 * b:3 * b + 3, :].rearrange("p k n -> p (k n)"),
                                           ps_y[:, b, 0:3 * (TN + 1)]).then_inc(q_t1e, 1)
                        act.wait_ge(q_h, t + 1)
                        if not isinstance(t, int) or t >= 2:
                            act.wait_ge(q_hstore[q], 16 * (nth(t) - 1))
                        nc.scalar.copy(net.e_dst8[:, t, :], ps_h[0:TN, 1, HC + 8:HC + 16])
                        nc.scalar.copy(hrow[q][:, 0:HC], ps_h[0:TN, 0, 0:HC])
                        nc.scalar.copy(hrow[q][:, HC:D + 16], ps_h[0:TN, 1, 0:HC + 16]).then_inc(q_he, 1)
                steps(act, NT, -1, 1, step)

            @block.vector
            def _(dve):
                def chain(q, t, per_tile):
                    n = [0]

                    def link(ins):
                        n[0] += 1
                        assert n[0] <= per_tile
                        ins.then_inc(q, 1)
                        dve.wait_ge(q, per_tile * t + n[0])
                    return link

                def front(t, p):
                    link = chain(c_front, t, 3 if first_layer else 2)
                    for h in range(2):
                        dve.wait_ge(q_gather[p][h], 16 * nth(t))
                    nc_onehot = nc.vector.tensor_tensor(onehot[p][:, :, :], net.node[:, :, :], bcast(net.dst_rel[:, t, :], 2, HALF), ALU.is_equal)
                    link(nc_onehot)
                    ins = nc.vector.tensor_scalar(neg[p][:, :, :], onehot[p][:, :, :], -1.0, BIG, ALU.add, ALU.mult)
                    if first_layer:
                        ins.then_inc(c_front, 1)
                        for h in range(2):
                            ins = nc.vector.tensor_tensor_reduce(junk[h][:, :], rows[p][:, h, 0:D], net.v[:, 0, :], 1.0, 0.0,
                                                                 ALU.mult, ALU.add, rows[p][:, h, D:D + 1])
                        ins.then_inc(c_front, 1)
                        dve.wait_ge(q_own[p], 16 * nth(t))
                        nc.vector.tensor_tensor_reduce(junk[2][0:TN, :], mine[p][:, :], net.v[0:TN, 0, :], 1.0, 0.0,
                                                       ALU.mult, ALU.add, eself[p][:, :]).then_inc(q_ndin, 1)
                        nc.vector.tensor_tensor_reduce(junk[3][0:TN, :], mine[p][:, :], net.v[0:TN, 1, :], 1.0, 0.0,
                                                       ALU.mult, ALU.add, nd[p][:, 0:1]).then_inc(q_ndin, 1)
                        dve.wait_ge(c_front, 3 * t + 3)
                    else:
                        link(ins)
                        if own:
                            nc.vector.tensor_copy(eself[p][:, :], net.e_own[:, t, 0:1]).then_inc(q_ndin, 1)
                        if H == 1:
                            nc.vector.tensor_copy(nd[p][:, 0:1], net.e_own[:, t, 1:2]).then_inc(q_ndin, 1)
                        else:
                            nc.vector.tensor_copy(nd[p][:, 0:H], net.e_dst8[:, t, :]).then_inc(q_ndin, 1)
                    if has(t - 2, NT) and (not isinstance(t, int) or t >= 2):
                        dve.wait_ge(q_mt, t - 1)
                    for hh in range(2):
                        ins = nc.vector.tensor_tensor(masked[p][:, :, hh, :], bcast(neg[p][:, hh, :], 1, H),
                                                      bcast(rows[p][:, hh, D:D + H], 2, HALF), ALU.add)
                    ins.then_inc(q_masked, 1)

                n_ndin = 2 if own else 1

                def middle(t, p):
                    link = chain(c_mid, t, 4 if own else 2)
                    dve.wait_ge(q_mt, t + 1)
                    dve.wait_ge(q_ndin, n_ndin * t + n_ndin)
                    if H == 1:
                        m = ps_mt[0:TN, 0:WIN]
                        link(nc.vector.tensor_reduce(smax[p][:, :], m, AX.X, ALU.max))
                        first = m
                    else:
                        m = ps_m[0:TN, :, :].rearrange("p b (h e) -> p (b h) e", e=WIN)
                        link(nc.vector.tensor_reduce(smax[p][:, :], m, AX.X, ALU.max))
                        first = ps_m[0:TN, 0, 0:WIN]
                    nc.vector.tensor_scalar(onehot_t[p][:, :], first, -BIG / 2, None, ALU.is_gt)
                    if own:
                        link(nc.vector.scalar_tensor_tensor(out=msum[p][:, :], in0=smax[p][:, :], scalar=eself[p][:, 0:1],
                                                            in1=nd[p][:, 0:1], op0=ALU.max, op1=ALU.add))
                    else:
                        link(nc.vector.tensor_tensor(msum[p][:, :], smax[p][:, :], nd[p][:, 0:H], ALU.add))
                    ins = nc.vector.scalar_tensor_tensor(out=nd[p][:, H:2 * H], in0=msum[p][:, :], scalar=SLOPE,
                                                         in1=msum[p][:, :], op0=ALU.mult, op1=ALU.max)
                    ins.then_inc(q_nd, 1)
                    if own:
                        link(nc.vector.tensor_tensor(us[p][:, 0:1], eself[p][:, :], nd[p][:, 0:1], ALU.add))
                        link(nc.vector.scalar_tensor_tensor(out=us[p][:, 1:2], in0=us[p][:, 0:1], scalar=SLOPE,
                                                            in1=us[p][:, 0:1], op0=ALU.mult, op1=ALU.max))
                        dve.wait_ge(q_nd, t + 1)
                        nc.vector.tensor_tensor(us[p][:, 2:3], us[p][:, 1:2], nd[p][:, 1:2], ALU.subtract).then_inc(q_dself, 1)

                    link = chain(c_exp, t, 3)
                    g = ps_e
                    dve.wait_ge(q_g, t + 1)
                    link(nc.vector.tensor_tensor(e1[p][:, :, :], sources(p), g[:, :, 0:H], ALU.add))
                    link(nc.vector.scalar_tensor_tensor(out=e2[p][:, :, :], in0=e1[p][:, :, :], scalar=SLOPE,
                                                        in1=e1[p][:, :, :], op0=ALU.mult, op1=ALU.max))
                    link(nc.vector.tensor_tensor(e3[p][:, :, :], e2[p][:, :, :], g[:, :, H:2 * H], ALU.subtract))
                    nc.vector.tensor_scalar(e4[p][:, :, :], e3[p][:, :, :], 0.0, None, ALU.min).then_inc(q_logit, 1)
                    if own:
                        dve.wait_ge(q_xself, t + 1)
                        nc.vector.tensor_scalar(diag[p][:, :], net.ident[0:TN, 0:TN + 1], xself[p][:, 0:1], None,
                                                ALU.mult).then_inc(q_diag, 1)
                    dve.wait_ge(q_exp, t + 1)
                    if H == 1:
                        nc.vector.tensor_tensor(coef[p][:, :, :], onehot[p][:, :, :], bcast(ex[p][:, :, 0], 2, HALF),
                                                ALU.mult).then_inc(q_coef, 1)
                    else:
                        if not isinstance(t, int) or t >= 2:
                            dve.wait_ge(q_o, t - 1)
                        for w in range(2):
                            ins = nc.vector.tensor_tensor(scaled[p][:, w, 0:D].rearrange("p (h c) -> p h c", h=H),
                                                          rows[p][:, w, 0:D].rearrange("p (h c) -> p h c", h=H),
                                                          bcast(ex[p][:, w, :], 2, D // H), ALU.mult)
                        ins.then_inc(q_scaled, 1)
                        nc.vector.tensor_copy(onehot_k[p][:, :, :], onehot[p][:, :, :])
                        nc.vector.tensor_copy(scaled[p][:, :, D:D + H], ex[p][:, :, :]).then_inc(q_coef, 1)

                def sums(t, p):
                    dve.wait_ge(q_agg, t + 1)
                    if own:
                        ins = nc.vector.tensor_scalar(zsum[p][:, :], ps_g[0:TN, ZC:ZC + 1], xself[p][:, 0:1], None, ALU.add)
                    else:
                        ins = nc.vector.tensor_scalar(zsum[p][:, :], ps_g[0:TN, ZC:ZC + 1], 1e-16, None, ALU.add)
                    ins.then_inc(c_evac, 1)
                    dve.wait_ge(c_evac, t + 1)
                    nc.vector.reciprocal(rz[p][:, :], zsum[p][:, :]).then_inc(q_rz, 1)

                def back(t, p):
                    dve.wait_ge(q_o, t + 1)
                    o = ps_o[p][0:TN, :, 0:HC]
                    v = o1[p][:, :].rearrange("p (b c) -> p b c", b=2)
                    if kind == "C":
                        link = chain(c_back, t, 2)
                        link(nc.vector.tensor_scalar(zsum[p][:, :], ps_o[p][0:TN, 1, HC:HC + H], 1e-16, None, ALU.add))
                        link(nc.vector.reciprocal(rz[p][:, :], zsum[p][:, :]))
                        for b in range(2):
                            ins = nc.vector.tensor_tensor(
                                o1[p][:, b * HC:(b + 1) * HC].rearrange("p (h c) -> p h c", h=H // 2),
                                ps_o[p][0:TN, b, 0:HC].rearrange("p (h c) -> p h c", h=H // 2),
                                bcast(rz[p][:, b * H // 2:(b + 1) * H // 2], 2, D // H), ALU.mult)
                        ins.then_inc(q_oread, 1)
                        dve.wait_ge(q_oread, t + 1)
                        nc.vector.tensor_tensor(o1[p][:, :], o1[p][:, :], net.bias[0:TN, bias, :], ALU.add).then_inc(q_b, 1)
                        dve.wait_ge(q_b, t + 1)
                        nc.vector.tensor_scalar(junk[0][0:TN, :], o1[p][:, :], 0.0, None, ALU.max).then_inc(q_neg, 1)
                        dve.wait_ge(q_neg, t + 1)
                        dve.wait_ge(q_c2, t + 1)
                        if not isinstance(t, int) or t >= 2:
                            dve.wait_ge(q_store[p], 16 * (nth(t) - 1))
                            dve.wait_ge(q_ecopy, t - 1)
                        nc.vector.scalar_tensor_tensor(out=o2[p][:, 0:D], in0=o3[p][:, :], scalar=-1.0, in1=junk[0][0:TN, :],
                                                       op0=ALU.add, op1=ALU.add).then_inc(q_out, 1)
                    else:
                        dve.wait_ge(q_rz, t + 1)
                        if kind == "A":
                            nc.vector.scalar_tensor_tensor(out=v, in0=o, scalar=rz[p][:, 0:1],
                                                           in1=net.bias[0:TN, bias, :].rearrange("p (b c) -> p b c", b=2),
                                                           op0=ALU.mult, op1=ALU.add).then_inc(q_pre, 1)
                        else:
                            dve.wait_ge(q_resb, t + 1)
                            if not isinstance(t, int) or t >= 2:
                                dve.wait_ge(q_out, t - 1)
                            nc.vector.scalar_tensor_tensor(out=v, in0=o, scalar=rz[p][:, 0:1],
                                                           in1=resid[p][:, :].rearrange("p (b c) -> p b c", b=2),
                                                           op0=ALU.mult, op1=ALU.add).then_inc(q_pre, 1)
                            dve.wait_ge(q_pre, t + 1)
                            link = chain(c_back, t, 6)
                            nc.vector.bn_stats(st6[p][:, 0, :], o1[p][:, 0:HC])
                            link(nc.vector.bn_stats(st6[p][:, 1, :], o1[p][:, HC:D]))
                            dve.sem_inc(q_go2, 1)
                            link(nc.vector.bn_aggr(mv[p][:, :], st6[p][:, :, :]))
                            nc.vector.tensor_scalar(rs[p][:, 0:1], mv[p][:, 1:2], EPS, None, ALU.add).then_inc(q_var, 1)
                            dve.wait_ge(q_var, t + 1)
                            dve.wait_ge(q_pow, t + 1)
                            link(nc.vector.tensor_tensor(rs[p][:, 2:3], rs[p][:, 1:2], rs[p][:, 1:2], ALU.mult))
                            link(nc.vector.tensor_tensor(rs[p][:, 3:4], rs[p][:, 2:3], rs[p][:, 0:1], ALU.mult))
                            link(nc.vector.tensor_scalar(rs[p][:, 4:5], rs[p][:, 3:4], -0.5, 1.5, ALU.mult, ALU.add))
                            link(nc.vector.tensor_tensor(rs[p][:, 5:6], rs[p][:, 4:5], rs[p][:, 1:2], ALU.mult))
                            nc.vector.scalar_tensor_tensor(out=rs[p][:, 6:7], in0=mv[p][:, 0:1], scalar=-1.0,
                                                           in1=rs[p][:, 5:6], op0=ALU.mult, op1=ALU.mult).then_inc(q_mvr, 1)
                    if kind in "AC":
                        j = 2 if kind == "A" else 4
                        dve.wait_ge(q_out, t + 1)
                        if kind == "A" and (not isinstance(t, int) or t >= 2):
                            dve.wait_ge(q_ecopy, t - 1)
                        for a in range(2):
                            ins = nc.vector.tensor_tensor_reduce(junk[4 + a][0:TN, :], o2[p][:, 0:D], net.v[0:TN, j + a, :], 1.0, 0.0,
                                                                 ALU.mult, ALU.add, o2[p][:, D + a:D + a + 1])
                        ins.then_inc(q_e2, 1)

                def step(s, p):
                    if has(s - 1, NT):
                        back(s - 1, 1 - p)
                    if has(s + 1, NT):
                        middle(s + 1, 1 - p)
                    if has(s + 2, NT):
                        front(s + 2, p)
                    if kind != "C" and has(s + 1, NT):
                        sums(s + 1, 1 - p)
                steps(dve, NT, -2, 1, step)

            @block.tensor
            def _(pe):
                def mask_t(t, p):
                    pe.wait_ge(q_masked, t + 1)
                    if not isinstance(t, int) or t >= 1:
                        pe.wait_ge(q_nd, t)
                    for h in range(H):
                        dst_ = ps_mt if H == 1 else ps_m[:, h // 4, :]
                        c = (h % 4) * WIN
                        for w in range(2):
                            ins = nc.tensor.matmul(dst_[HALF * w:HALF * w + HN[w], c:c + WIN], masked[p][:, h, w, 0:HN[w]],
                                                   net.ident[:, :], start=True, stop=True)
                    ins.then_inc(q_mt, 1)

                def spread(t, p):
                    pe.wait_ge(q_nd, t + 1)
                    if not isinstance(t, int) or t >= 1:
                        if kind != "C":
                            pe.wait_ge(q_rz, t)
                        pe.wait_ge(q_logit, t)
                    for w in range(2):
                        a = HALF * w
                        ins = nc.tensor.matmul(ps_e[:, w, :], onehot_t[p][a:a + HN[w], :],
                                               nd[p][a:a + HN[w], :], start=True, stop=True)
                    ins.then_inc(q_g, 1)

                def aggregate(t, p):
                    pe.wait_ge(q_coef, t + 1)
                    if own:
                        pe.wait_ge(q_diag, t + 1)
                        if not first_layer:
                            pe.wait_ge(q_own[p], 16 * nth(t))
                    if not isinstance(t, int) or t >= 1:
                        pe.wait_ge(q_y, 2 * t)
                    if kind == "B" and (not isinstance(t, int) or t >= 3):
                        pe.wait_ge(q_t1e, 2 * (t - 2))
                    for k in range(KT):
                        y = ps_y[:, k // 3, (k % 3) * (TN + 1):(k % 3 + 1) * (TN + 1)]
                        new = k % 3 == 0
                        f = slice(k * P, (k + 1) * P)
                        if own:
                            nc.tensor.matmul(y[:, :], mine[p][:, f], diag[p][:, :], start=new, stop=False, skip_group_check=True)
                        nc.tensor.matmul(y[:, 0:HALF], rows[p][:, 0, f], coef[p][:, 0, :], start=new and not own, stop=True, skip_group_check=True)
                        nc.tensor.matmul(y[:, HALF:TN + 1], rows[p][:, 1, f], coef[p][:, 1, 0:TN + 1 - HALF], start=False, stop=True, skip_group_check=True)
                    for w in range(2):
                        ins = nc.tensor.matmul(ps_g[HALF * w:HALF * w + HN[w], ZC:ZC + 1], coef[p][:, w, 0:HN[w]], net.ones[:, 0:1],
                                               start=True, stop=True, skip_group_check=True)
                    ins.then_inc(q_agg, 1)

                def product(t, p, k0, k1):
                    o = ps_o[p]
                    if k0 == 0:
                        pe.wait_ge(q_y, 2 * t + 2)
                        if not isinstance(t, int) or t >= n_o:
                            pe.wait_ge(q_pre, t + 1 - n_o)
                    for k in range(k0, k1):
                        for b in range(2):
                            ins = nc.tensor.matmul(o[0:TN, b, 0:HC], yt[p][:, k, 0:TN], weights[:, k, b * HC:(b + 1) * HC],
                                                   start=(k == 0), stop=(k == KT - 1))
                    if k1 == KT:
                        ins.then_inc(q_o, 1)

                def step(s, p):
                    if kind == "C":
                        if has(s + 1, NT):
                            mask_t(s + 1, 1 - p)
                            spread(s + 1, 1 - p)
                            t, q = s + 1, 1 - p
                        if has(s, NT):
                            pe.wait_ge(q_coef, s + 1)
                            if not isinstance(s, int) or s >= 2:
                                pe.wait_ge(q_oread, s - 1)
                            for b, n in ((0, HC), (1, HC + H)):
                                for w in range(2):
                                    ins = nc.tensor.matmul(ps_o[p][HALF * w:HALF * w + HN[w], b, 0:n], onehot_k[p][:, w, 0:HN[w]],
                                                           scaled[p][:, w, b * HC:b * HC + n], start=True, stop=True)
                            ins.then_inc(q_o, 1)
                        return
                    if has(s, NT):
                        product(s, p, 0, 2)
                    if has(s + 1, NT):
                        mask_t(s + 1, 1 - p)
                    if has(s, NT):
                        product(s, p, 2, 4)
                    if has(s + 1, NT):
                        spread(s + 1, 1 - p)
                    if has(s, NT):
                        product(s, p, 4, 5)
                    if has(s + 1, NT):
                        aggregate(s + 1, 1 - p)
                    if has(s, NT):
                        product(s, p, 5, 6)
                    if kind == "B" and has(s - 1, NT):
                        t, q = s - 1, 1 - p
                        pe.wait_ge(q_out, t + 1)
                        if has(s + 1, NT):
                            pe.wait_ge(q_y, 2 * (s + 1) + 2)
                        for k in range(KT):
                            ins = nc.tensor.transpose(ps_y[:, k // 3, (k % 3) * (TN + 1):(k % 3) * (TN + 1) + TN],
                                                      o2[q][:, k * P:(k + 1) * P], net.ident[0:TN, 0:TN])
                        ins.then_inc(q_t1, 1)
                        pe.wait_ge(q_t1e, 2 * t + 2)
                        if not isinstance(t, int) or t >= 1:
                            pe.wait_ge(q_he, t)
                        for k in range(KT):
                            for b, n in ((0, HC), (1, HC + 16)):
                                ins = nc.tensor.matmul(ps_h[0:TN, b, 0:n], x1t[q][:, k, 0:TN], net.w[2][:, k, b * HC:b * HC + n],
                                                       start=(k == 0), stop=(k == KT - 1))
                        ins.then_inc(q_h, 1)
                steps(pe, NT, -1, 1, step)

def general_graph(nc, net, sem):
    NT = net.NT
    with ExitStack() as ctx:
        node_i = ctx.enter_context(nc.sbuf_tensor("self_i", [P, NT, 2], I32))
        edge_i = ctx.enter_context(nc.sbuf_tensor("edge_i", [P, NT, 2], I32))
        s_iota = sem("n_iota")
        with nc.Block() as block:
            @block.gpsimd
            def _(pool):
                nc.gpsimd.iota(node_i[:, :, :], pattern=[[TN, NT], [HALF, 2]], base=0, channel_multiplier=1).then_inc(s_iota, 1)
                nc.gpsimd.iota(edge_i[:, :, :], pattern=[[0, NT], [0, 2]], base=0, channel_multiplier=1).then_inc(s_iota, 1)

            @block.vector
            def _(dve):
                dve.wait_ge(s_iota, 2)
                nc.vector.tensor_scalar(net.src_idx[:, :, :], node_i[:, :, :], float(net.N - 1), None, ALU.min)
                nc.vector.tensor_copy(net.dst_rel[:, :, :], edge_i[:, :, :])


def general_sums(nc, net, name, sem, *, heads, own, table, row, first_layer):
    N, E, NT, H = net.N, net.E, net.NT, heads
    NC = E // TN
    C = D // H
    src_cols = net.src.rearrange("(c e) -> c e", e=TN)
    with ExitStack() as ctx:
        def sb(n, shape, dt=F32):
            return ctx.enter_context(nc.sbuf_tensor(f"{name}_{n}", shape, dt))

        def s_(n):
            return sem(f"{name}_{n}")

        idx = sb("idx", [TN, 1], I32)
        rows = sb("rows", [TN, D + 8])
        mine = sb("mine", [TN, D])
        prod = [sb(f"prod{i}", [TN, D]) for i in range(3)]
        pair = sb("pair", [TN, 2])
        s_idx = s_("idx"); s_row = s_("row"); s_cell = s_("cell"); s_store = s_("store"); s_own = s_("own"); s_pair = s_("pair"); s_kept = s_("kept"); s_turn = s_("turn")

        with nc.Block() as block:
            @block.sync
            def _(sp):
                with sp.Fori(0, NC) as c:
                    sp.dma_start(idx[:, :], src_cols[c].unsqueeze(1)).then_inc(s_idx, 16)
                    sp.wait_ge(s_cell, c + 1) if first_layer else sp.wait_ge(s_row, 16 * c + 16)
                    with nc.allow_non_contiguous_dma(reason="four bytes per edge and head, in the slow path only"):
                        sp.dma_start(net.esrc[0:H, bass.ds(c * TN, TN)].rearrange("h e -> e h"), rows[:, D:D + H]).then_inc(s_store, 16)
                    sp.wait_ge(s_store, 16 * c + 16)
                    sp.sem_inc(s_turn, 1)
                if first_layer:
                    with sp.Fori(0, NT) as t:
                        sp.dma_start(mine[:, :], net.tiles(table)[t]).then_inc(s_own, 16)
                        sp.wait_ge(s_kept, t + 1)
                        sp.sem_inc(s_turn, 1)

            @block.gpsimd
            def _(pool):
                with pool.Fori(0, NC) as c:
                    pool.wait_ge(s_idx, 16 * c + 16)
                    pool.sem_inc(s_pair, 1)
                    nc.gpsimd.indirect_dma_start(out=rows[:, 0:row], out_offset=None, in_=table[:, :],
                                                 in_offset=bass.IndirectOffsetOnAxis(ap=idx[:, 0:1], axis=0)).then_inc(s_row, 16)

            @block.vector
            def _(dve):
                if first_layer:
                    with dve.Fori(0, NC) as c:
                        dve.wait_ge(s_row, 16 * c + 16)
                        nc.vector.tensor_tensor_reduce(prod[0][:, :], rows[:, 0:D], net.v[0:TN, 0, :], 1.0, 0.0,
                                                       ALU.mult, ALU.add, rows[:, D:D + 1]).then_inc(s_cell, 1)
                        dve.wait_ge(s_cell, c + 1)
                    with dve.Fori(0, NT) as t:
                        dve.wait_ge(s_own, 16 * t + 16)
                        for a in range(2):
                            ins = nc.vector.tensor_tensor_reduce(prod[1 + a][:, :], mine[:, :], net.v[0:TN, a, :], 1.0, 0.0,
                                                                 ALU.mult, ALU.add, pair[:, a:a + 1])
                        ins.then_inc(s_cell, 1)
                        dve.wait_ge(s_cell, NC + t + 1)
                        nc.vector.tensor_copy(net.e_own[:, t, :], pair[:, :]).then_inc(s_kept, 1)
                        dve.wait_ge(s_kept, t + 1)

    with ExitStack() as ctx:
        name += "s"
        idx = sb("idx", [TN, 1], I32)
        rows = sb("rows", [TN, D + 8])
        mine = sb("mine", [TN, D])
        part = sb("part", [TN, E])
        w = sb("w", [TN, E])
        zeros = sb("zeros", [TN, 8])
        c_ = sb("cells", [TN, 12])
        piece = sb("piece", [TN, TN])
        piece_t = sb("piece_t", [TN, TN])
        res = sb("res", [TN, 3, D])
        acc = net.bank2(0)
        s_to = s_("to"); s_part = s_("part"); s_idx = s_("idx"); s_row = s_("row"); s_own = s_("own"); s_go = s_("go")
        s_chain = s_("chain"); s_m = s_("m"); s_exp = s_("exp"); s_piece = s_("piece"); s_t = s_("t"); s_pt = s_("pt")
        s_mm = s_("mm"); s_res = s_("res"); s_store = s_("store"); s_turn = s_("turn")
        LINKS = 17 + (3 if own else 0)

        with nc.Block() as block:
            @block.sync
            def _(sp):
                with sp.Fori(0, H) as h:
                    sp.dma_start(part[:, :], bcast(net.esrc[h], 0, TN)).then_inc(s_part, 16)
                    with sp.Fori(0, NT) as t:
                        r = h * NT + t
                        sp.dma_start(w[:, :].bitcast(I32), bcast(net.dst, 0, TN)).then_inc(s_to, 16)
                        if own:
                            sp.dma_start(mine[:, :], net.tiles(table)[t][:, 0:D]).then_inc(s_own, 16)
                        with sp.Fori(0, NC) as c:
                            sp.dma_start(idx[:, :], src_cols[c].unsqueeze(1)).then_inc(s_idx, 16)
                            sp.wait_ge(s_mm, r * NC + c + 1)
                            sp.sem_inc(s_turn, 1)
                        sp.wait_ge(s_res, r + 1)
                        sp.dma_start(net.tiles(net.agg)[t][:, bass.ds(h * C, C)], res[:, 2, 0:C]).then_inc(s_store, 16)
                        sp.dma_start(net.tiles(net.agg)[t][:, D:D + 8], zeros[:, :]).then_inc(s_store, 16)
                        sp.wait_ge(s_store, 32 * r + 32)
                        sp.sem_inc(s_turn, 1)

            @block.gpsimd
            def _(pool):
                with pool.Fori(0, H * NT * NC) as k:
                    pool.wait_ge(s_idx, 16 * k + 16)
                    pool.sem_inc(s_go, 1)
                    nc.gpsimd.indirect_dma_start(out=rows[:, 0:row], out_offset=None, in_=table[:, :],
                                                 in_offset=bass.IndirectOffsetOnAxis(ap=idx[:, 0:1], axis=0)).then_inc(s_row, 16)

            @block.scalar
            def _(act):
                with act.Fori(0, H * NT) as r:
                    act.wait_ge(s_m, r + 1)
                    if own:
                        nc.scalar.activation(c_[:, 7:8], c_[:, 6:7], ACT.Exp)
                    nc.scalar.activation(w[:, :], w[:, :], ACT.Exp, bias=c_[:, 4:5]).then_inc(s_exp, 1)

            @block.vector
            def _(dve):
                nc.vector.memset(zeros[:, :], 0.0)
                with dve.Fori(0, H) as h:
                    dve.wait_ge(s_part, 16 * h + 16)
                    dve.sem_inc(s_turn, 1)
                    with dve.Fori(0, NT) as t:
                        r = h * NT + t
                        n = [0]

                        def link(ins):
                            n[0] += 1
                            ins.then_inc(s_chain, 1)
                            dve.wait_ge(s_chain, r * LINKS + n[0])

                        dve.wait_ge(s_to, 16 * r + 16)
                        link(nc.vector.tensor_copy(w[:, :], w[:, :].bitcast(I32)))
                        link(nc.vector.tensor_scalar(w[:, :], w[:, :], net.node_ids[:, bass.ds(t, 1)], None, ALU.is_equal))
                        link(nc.vector.tensor_scalar(w[:, :], w[:, :], -1.0, BIG, ALU.add, ALU.mult))
                        link(nc.vector.tensor_tensor(w[:, :], w[:, :], part[:, :], ALU.add))
                        if H == 1:
                            link(nc.vector.tensor_copy(c_[:, 0:2], net.e_own[:, t, :]))
                        else:
                            link(nc.vector.tensor_copy(c_[:, 1:2], net.e_dst8.rearrange("p t h -> p (t h)")[:, bass.ds(t * 8 + h, 1)]))
                        link(nc.vector.tensor_reduce(c_[:, 2:3], w[:, :], AX.X, ALU.max))
                        if own:
                            link(nc.vector.scalar_tensor_tensor(out=c_[:, 2:3], in0=c_[:, 2:3], scalar=c_[:, 0:1], in1=c_[:, 1:2],
                                                                op0=ALU.max, op1=ALU.add))
                        else:
                            link(nc.vector.tensor_tensor(c_[:, 2:3], c_[:, 2:3], c_[:, 1:2], ALU.add))
                        link(nc.vector.scalar_tensor_tensor(out=c_[:, 3:4], in0=c_[:, 2:3], scalar=SLOPE, in1=c_[:, 2:3],
                                                            op0=ALU.mult, op1=ALU.max))
                        link(nc.vector.tensor_scalar(c_[:, 4:5], c_[:, 3:4], -BIG / 100, -1.0, ALU.max, ALU.mult))
                        if own:
                            link(nc.vector.tensor_tensor(c_[:, 5:6], c_[:, 0:1], c_[:, 1:2], ALU.add))
                            link(nc.vector.scalar_tensor_tensor(out=c_[:, 5:6], in0=c_[:, 5:6], scalar=SLOPE, in1=c_[:, 5:6],
                                                                op0=ALU.mult, op1=ALU.max))
                            link(nc.vector.tensor_tensor(c_[:, 6:7], c_[:, 5:6], c_[:, 4:5], ALU.add))
                        link(nc.vector.tensor_scalar(w[:, :], w[:, :], c_[:, 1:2], None, ALU.add))
                        link(nc.vector.scalar_tensor_tensor(out=w[:, :], in0=w[:, :], scalar=SLOPE, in1=w[:, :], op0=ALU.mult, op1=ALU.max))
                        dve.sem_inc(s_m, 1)
                        dve.wait_ge(s_exp, r + 1)
                        link(nc.vector.tensor_reduce(c_[:, 8:9], w[:, :], AX.X, ALU.add))
                        link(nc.vector.tensor_scalar(c_[:, 9:10], c_[:, 8:9], c_[:, 7:8] if own else 1e-16, None, ALU.add))
                        link(nc.vector.reciprocal(c_[:, 10:11], c_[:, 9:10]))
                        dve.sem_inc(s_turn, 1)
                        with dve.Fori(0, NC) as c:
                            nc.vector.tensor_copy(piece[:, :], w[:, bass.ds(c * TN, TN)]).then_inc(s_piece, 1)
                            dve.wait_ge(s_t, r * NC + c + 1)
                            nc.vector.tensor_copy(piece_t[:, :], net.bank[2][0:TN, 0:TN]).then_inc(s_pt, 1)
                            dve.wait_ge(s_mm, r * NC + c + 1)
                        if own:
                            dve.wait_ge(s_own, 16 * r + 16)
                            link(nc.vector.tensor_scalar(res[:, 0, :], mine[:, :], c_[:, 7:8], None, ALU.mult))
                        else:
                            link(nc.vector.memset(res[:, 0, :], 0.0))
                        o = acc[0:TN, :, 0:C // 2] if H == 1 else acc[0:TN, 0:1, 0:C]
                        nb = 2 if H == 1 else 1
                        link(nc.vector.tensor_tensor(res[:, 1, 0:C].rearrange("p (b c) -> p b c", b=nb), o,
                                                        res[:, 0, 0:C].rearrange("p (b c) -> p b c", b=nb), ALU.add))
                        link(nc.vector.tensor_scalar(res[:, 2, 0:C], res[:, 1, 0:C], c_[:, 10:11], None, ALU.mult))
                        dve.sem_inc(s_res, 1)
                        dve.wait_ge(s_store, 32 * r + 32)
                        assert n[0] == LINKS, n

            @block.tensor
            def _(pe):
                def chunk(k, h, first):
                    pe.wait_ge(s_piece, k + 1)
                    nc.tensor.transpose(net.bank[2][0:TN, 0:TN], piece[:, :], net.ident[0:TN, 0:TN]).then_inc(s_t, 1)
                    pe.wait_ge(s_pt, k + 1)
                    pe.wait_ge(s_row, 16 * k + 16)
                    if H == 1:
                        for b in range(2):
                            ins = nc.tensor.matmul(acc[0:TN, b, 0:HC], piece_t[:, :], rows[:, b * HC:(b + 1) * HC],
                                                   start=first, stop=True, skip_group_check=True)
                    else:
                        ins = nc.tensor.matmul(acc[0:TN, 0, 0:C], piece_t[:, :], rows[:, bass.ds(h * C, C)],
                                               start=first, stop=True, skip_group_check=True)
                    ins.then_inc(s_mm, 1)

                with pe.Fori(0, H) as h:
                    with pe.Fori(0, NT) as t:
                        k = (h * NT + t) * NC
                        chunk(k, h, True)
                        with pe.Fori(1, NC) as c:
                            chunk(k + c, h, False)


def gat_program(nc, ext, out, N, E):
    with ExitStack() as ctx:
        net = Net()
        net.N, net.E, net.NT = N, E, N // TN
        NT = net.NT

        def sb(name, shape, dt=F32):
            return ctx.enter_context(nc.sbuf_tensor(name, shape, dt))

        def dram(name, shape, dt=F32):
            return nc.dram_tensor(name, shape, dt, kind="Internal").ap()

        sems = []

        def sem(name):
            sems.append(nc.alloc_semaphore(name))
            return sems[-1]

        def retire():
            nc.clear_and_free_semaphores(list(sems))
            sems.clear()
            nc.all_engine_barrier()

        net.w = [sb("w_l0_1", [P, KT, D]), sb("w_l0_2", [P, KT, D]), sb("w_l1_1", [P, KT, D + 16]), sb("w_l1_2", [P, KT, D])]
        net.bias = sb("bias_rows", [P, 4, D])
        net.v = sb("attention_rows", [P, 6, D])
        net.ident = sb("ident", [P, P])
        net.ones = sb("ones", [P, 2])
        net.minus_half = sb("minus_half", [P, 1])
        net.node_i = sb("node_i", [P, 2, HALF], I32)
        net.node = sb("node", [P, 2, HALF])
        net.src_idx = sb("src_idx", [P, NT, 2], I32)
        net.dst_rel = sb("dst_rel", [P, NT, 2])
        net.e_own = sb("e_own", [TN, NT, 2])
        net.e_dst8 = sb("e_dst8", [TN, NT, 8])
        net.flag = sb("flag", [1, 1], I32)
        net.node_ids_i = sb("node_ids_i", [TN, NT], I32)
        net.node_ids = sb("node_ids", [TN, NT])
        psum = ctx.enter_context(nc.psum_tensor("psum", [P, 8, OB], F32))
        net.psum = psum
        net.bank = [psum[:, b, :] for b in range(8)]
        net.bank2 = lambda b: psum[:, b:b + 2, :]
        net.edges = dram("edges", [2, E + WIN], I32)
        net.windows = dram("windows", [2 * NT, 2, WIN], I32)
        net.g = {"A": dram("g1", [N, D + 2]), "C": dram("g3", [N, D + 2])}
        net.x1 = dram("x1", [N, D])
        net.h = dram("h", [N, D + 16])
        net.agg = dram("agg", [N, D + 8])
        net.esrc = dram("esrc", [8, E])
        net.src, net.dst = ext["src"], ext["dst"]
        net.out = out
        net.tiles = lambda a: a.rearrange("(t p) d -> t p d", p=TN)
        x = ext["x"]

        prepare(nc, net, ext, sem)
        retire()
        flag = nc.values_load(net.flag[0:1, 0:1], min_val=0, max_val=TN + 1)

        layers = [dict(heads=1, own=True, weights=net.w[0], residual=None, bias=0, out_kind="A"),
                  dict(heads=1, own=True, weights=net.w[1], residual=x, bias=1, out_kind="B"),
                  dict(heads=8, own=False, weights=None, residual=None, bias=2, out_kind="C"),
                  dict(heads=1, own=False, weights=net.w[3], residual=net.x1, bias=3, out_kind="D")]
        tables = [(x, D), (net.g["A"], D + 2), (net.h, D + 8), (net.g["C"], D + 2)]
        with nc.If(flag == 0):
            for layer, (table, row) in zip(layers, tables):
                attention_phase(nc, net, layer["out_kind"], sem, table=table, row=row, **layer)
                retire()
        with nc.Else():
            for layer, (table, row) in zip(layers, tables):
                kind = layer["out_kind"]
                general_sums(nc, net, f"s{kind}", sem, heads=layer["heads"], own=layer["own"], table=table, row=row,
                             first_layer=kind == "A")
                retire()
                if kind == "A":
                    general_graph(nc, net, sem)
                    retire()
                attention_phase(nc, net, f"g{kind}", sem, table=net.agg, row=D if kind == "A" else D + layer["heads"], **layer)
                retire()


_INS = ["x", "src", "dst", "L0_gnn_W1", "L0_gnn_att_src1", "L0_gnn_att_dst1", "L0_gnn_b1", "L0_gnn_W2", "L0_gnn_att_src2",
        "L0_gnn_att_dst2", "L0_gnn_b2", "L1_gnn_W1", "L1_gnn_a_src1", "L1_gnn_a_dst1", "L1_gnn_b1", "L1_gnn_W2",
        "L1_gnn_a_src2", "L1_gnn_a_dst2", "L1_gnn_b2"]


def kernel(**inputs):
    import numpy as _np
    import concourse.bacc as _bacc
    from concourse import mybir as _mybir
    from concourse.bass_utils import run_bass_kernel_spmd as _run

    nc = _bacc.Bacc("TRN2", target_bir_lowering=False, num_devices=1)
    arrays, ext = {}, {}
    for name in _INS:
        a = _np.ascontiguousarray(inputs[name])
        arrays[f"in_{name}"] = a
        ext[name] = nc.dram_tensor(f"in_{name}", a.shape, _mybir.dt.from_np(a.dtype), kind="ExternalInput").ap()
    shape = arrays["in_x"].shape
    out = nc.dram_tensor("out_0", shape, _mybir.dt.float32, kind="ExternalOutput").ap()
    gat_program(nc, ext, out, shape[0], arrays["in_src"].shape[0])
    r = _run(nc, [arrays], core_ids=[0])
    return r.results[0]["out_0"]
```

```python
from contextlib import ExitStack

import concourse.bass as bass
from concourse import mybir

F32 = mybir.dt.float32
I32 = mybir.dt.int32
BF16 = mybir.dt.bfloat16
F32R = mybir.dt.float32r
ALU = mybir.AluOpType
ACT = mybir.ActivationFunctionType
AX = mybir.AxisListType

P = 128
D = 768
KT = D // P
TN = 125
HALF = 64
HN = [HALF, TN - HALF]
WIN = 128
BIG = 1e30
FAR = 1 << 20
SLOPE = 0.2
EPS = 1e-5
OB = 512
HC = D // 2
PEEL = 4


class Net:
    pass


def steps(eng, n_tiles, first, last, step):
    for s in range(first, PEEL):
        step(s, s % 2)
    n_loop = (n_tiles - PEEL - 3) // 2
    with eng.Fori(0, n_loop) as i:
        step(2 * i + PEEL, 0)
        step(2 * i + PEEL + 1, 1)
    for s in range(PEEL + 2 * n_loop, n_tiles + last):
        step(s, s % 2)


def has(s, n_tiles):
    return not isinstance(s, int) or 0 <= s < n_tiles


def nth(s):
    return s // 2 + 1


def bcast(ap, at, n):
    return ap.unsqueeze(at).to_broadcast([*ap.shape[:at], n, *ap.shape[at:]])


def prepare(nc, net, ext, sem):
    N, E, NT = net.N, net.E, net.NT
    NW = 2 * NT
    KE = E // TN
    src, dst = ext["src"], ext["dst"]
    with ExitStack() as ctx:
        def sb(name, shape, dt=F32):
            return ctx.enter_context(nc.sbuf_tensor(name, shape, dt))

        padding = sb("padding", [2, WIN], I32)
        dst_i = sb("dst_i", [TN, KE], I32)
        next_i = sb("next_i", [TN, KE], I32)
        dst_f = sb("dst_f", [TN, KE])
        next_f = sb("next_f", [TN, KE])
        falls = sb("falls", [TN, KE])
        any_fall = sb("any_fall", [TN, 1])
        starts_i = sb("starts_i", [P, NT, 2], I32)
        starts = sb("starts", [P, NT, 2])
        CK = 20
        before = sb("before", [TN, 2, CK, NW], BF16)
        ones_bf = sb("ones_bf", [TN, 1], BF16)
        lo = sb("lo", [1, NW + 1])
        over = sb("over", [1, NW])
        worst = sb("worst", [1, 2])
        lo_i = sb("lo_i", [1, NW], I32)
        win_i = sb("win_i", [NT, 2, 2, WIN], I32)
        win_f = sb("win_f", [NT, 2, 2, WIN])
        a_rows = sb("a_rows", [P, 8, D])
        prod = sb("prod", [P, KT, D])
        ident_i = sb("ident_i", [P, P], I32)
        node_i = sb("node_i", [P, 2, HALF], I32)
        node_ids_i = sb("node_ids_i", [TN, NT], I32)
        weights = [sb(f"w{j}", [P, KT, D]) for j in range(4)]
        cols = sb("cols", [P, 6, KT])

        s_pad = sem("p_pad"); s_edges = sem("p_edges"); s_dst = sem("p_dst"); s_w = sem("p_weights")
        s_iota = sem("p_iota"); s_chain = sem("p_chain"); s_cmp = sem("p_cmp"); s_cmp_used = sem("p_cmp_used")
        s_lo = sem("p_lo"); s_loi = sem("p_loi"); s_win = [sem("p_win0"), sem("p_win1")]
        s_load = sem("p_load"); s_winf = sem("p_winf"); s_tr = sem("p_tr"); s_viol = sem("p_viol")
        s_cols = sem("p_cols"); s_bc = sem("p_bc"); s_bce = sem("p_bce"); s_ones = sem("p_ones"); s_padm = sem("p_padm")

        n_chunks = -(-KE // CK)
        folds = [(0, 0), (0, 1), (1, 2), (1, 3), (3, 6), (3, 7)]

        with nc.Block() as block:
            @block.sync
            def _(sp):
                sp.dma_start(net.edges[0, 0:E], src).then_inc(s_edges, 16)
                sp.dma_start(net.edges[1, 0:E], dst).then_inc(s_edges, 16)
                sp.dma_start(dst_i[:, :], dst.rearrange("(p k) -> p k", k=KE)).then_inc(s_dst, 16)
                sp.wait_ge(s_padm, 1)
                sp.dma_start(net.edges[:, E:E + WIN], padding[:, :]).then_inc(s_edges, 16)
                sp.wait_ge(s_edges, 48)
                sp.dma_start(next_i[:, :], net.edges[1, 1:E + 1].rearrange("(p k) -> p k", k=KE)).then_inc(s_dst, 16)
                for j in range(4):
                    sp.dma_start(weights[j][:, :, :], net.w[j].rearrange("(k p) n -> p k n", p=P)).then_inc(s_w, 16)
                sp.wait_ge(s_loi, 1)
                with sp.Fori(0, NT) as t:
                    at = sp.value_load(lo_i[0:1, bass.ds(2 * t, 1)], min_val=0, max_val=E)
                    sp.dma_start(net.windows[2 * t], net.edges[:, bass.ds(at, WIN)]).then_inc(s_win[0], 16)
                sp.wait_ge(s_win[0], 16 * NT)
                sp.wait_ge(s_win[1], 16 * NT)
                sp.dma_start(win_i[:, :, :, :], net.windows.rearrange("(t h) s e -> t h s e", h=2)).then_inc(s_load, 16)

            @block.scalar
            def _(act):
                vectors = ("L0_gnn_att_src1", "L0_gnn_att_dst1", "L0_gnn_att_src2", "L0_gnn_att_dst2",
                           "L1_gnn_a_src1", "L1_gnn_a_dst1", "L1_gnn_a_src2", "L1_gnn_a_dst2")
                for j, name in enumerate(vectors):
                    v = ext[name] if len(ext[name].shape) == 1 else ext[name].rearrange("h c -> (h c)")
                    act.dma_start(a_rows[:, j, :], bcast(v, 0, P)).then_inc(s_w, 16)
                act.wait_ge(s_loi, 1)
                with act.Fori(0, NT) as t:
                    at = act.value_load(lo_i[0:1, bass.ds(2 * t + 1, 1)], min_val=0, max_val=E)
                    act.dma_start(net.windows[2 * t + 1], net.edges[:, bass.ds(at, WIN)]).then_inc(s_win[1], 16)

            @block.gpsimd
            def _(pool):
                nc.gpsimd.iota(padding[:, :], pattern=[[0, WIN]], base=0, channel_multiplier=FAR).then_inc(s_padm, 1)
                nc.gpsimd.iota(starts_i[:, :, :], pattern=[[TN, NT], [HALF, 2]], base=0, channel_multiplier=0).then_inc(s_iota, 1)
                nc.gpsimd.iota(node_ids_i[:, :], pattern=[[TN, NT]], base=0, channel_multiplier=1).then_inc(s_iota, 1)
                nc.gpsimd.iota(node_i[:, :, :], pattern=[[0, 2], [1, HALF]], base=0, channel_multiplier=0).then_inc(s_iota, 1)
                nc.gpsimd.iota(ident_i[:, :], pattern=[[1, P]], base=0, channel_multiplier=-1).then_inc(s_iota, 1)

            @block.vector
            def _(dve):
                n = [0]

                def link(ins):
                    n[0] += 1
                    ins.then_inc(s_chain, 1)
                    dve.wait_ge(s_chain, n[0])

                nc.vector.memset(ones_bf[:, :], 1.0).then_inc(s_ones, 1)
                nc.vector.memset(net.ones[:, :], 1.0).then_inc(s_ones, 1)
                nc.vector.memset(net.minus_half[:, :], -0.5)
                nc.vector.memset(lo[0:1, NW:NW + 1], float(E))
                dve.wait_ge(s_iota, 4)
                nc.vector.tensor_copy(net.node_ids[:, :], node_ids_i[:, :])
                nc.vector.tensor_copy(starts[:, :, :], starts_i[:, :, :])
                nc.vector.tensor_copy(net.node[:, :, :], node_i[:, :, :])
                nc.vector.tensor_scalar(net.ident[:, :], ident_i[:, :], 0.0, None, ALU.is_equal).then_inc(s_ones, 1)
                dve.wait_ge(s_dst, 32)
                nc.vector.tensor_copy(next_f[:, :], next_i[:, :])
                link(nc.vector.tensor_copy(dst_f[:, :], dst_i[:, :]))
                for c in range(n_chunks):
                    k0, k1 = c * CK, min(KE, c * CK + CK)
                    if c >= 2:
                        dve.wait_ge(s_cmp_used, c - 1)
                    nc.vector.tensor_tensor(
                        before[:, c % 2, 0:k1 - k0, :], bcast(dst_f[:, k0:k1], 2, NW),
                        bcast(starts[0:TN, :, :].rearrange("p t h -> p (t h)"), 1, k1 - k0), ALU.is_lt).then_inc(s_cmp, 1)
                link(nc.vector.tensor_tensor(falls[:, :], dst_f[:, :], next_f[:, :], ALU.is_gt))
                nc.vector.tensor_reduce(any_fall[:, :], falls[:, :], AX.X, ALU.max).then_inc(s_viol, 1)
                dve.wait_ge(s_lo, 1)
                nc.vector.tensor_copy(lo_i[0:1, :], net.bank[0][0:1, 0:NW]).then_inc(s_loi, 1)
                link(nc.vector.tensor_copy(lo[0:1, 0:NW], net.bank[0][0:1, 0:NW]))
                link(nc.vector.tensor_tensor(over[:, :], lo[0:1, 1:NW + 1], lo[0:1, 0:NW], ALU.subtract))
                link(nc.vector.tensor_reduce(worst[0:1, 0:1], over[:, :], AX.X, ALU.max))
                link(nc.vector.tensor_scalar(worst[0:1, 1:2], worst[0:1, 0:1], float(WIN), None, ALU.is_gt))
                nc.vector.tensor_tensor(net.flag[0:1, 0:1], worst[0:1, 1:2], net.bank[1][0:1, 0:1], ALU.add)
                dve.wait_ge(s_w, 16 * 12)
                for j, (w, a) in enumerate(folds):
                    for k in range(KT):
                        ins = nc.vector.tensor_tensor_reduce(prod[:, k, :], weights[w][:, k, :], a_rows[:, a, :], 1.0, 0.0,
                                                             ALU.mult, ALU.add, cols[:, j, k:k + 1])
                    link(ins)
                dve.sem_inc(s_cols, 1)
                for a, c in ((4, 0), (5, 8)):
                    link(nc.vector.tensor_tensor(prod[:, :, :], weights[2][:, :, :], bcast(a_rows[:, a, :], 1, KT), ALU.mult))
                    link(nc.vector.tensor_reduce(net.w_att[:, :, c:c + 8], prod[:, :, :].rearrange("p k (h c) -> p k h c", h=8),
                                                 AX.X, ALU.add))
                for j in range(6):
                    dve.wait_ge(s_bc, j + 1)
                    nc.vector.tensor_copy(net.v[:, j, :].rearrange("p (b c) -> p b c", b=2),
                                          net.bank2(2)[:, :, 0:HC]).then_inc(s_bce, 1)
                dve.wait_ge(s_load, 16)
                nc.vector.tensor_copy(win_f[:, :, :, :], win_i[:, :, :, :]).then_inc(s_winf, 1)
                dve.wait_ge(s_tr, 4)
                for h in range(2):
                    nc.vector.tensor_copy(net.src_idx[:, :, h], net.bank[4][:, (2 * h) * NT:(2 * h + 1) * NT])
                    nc.vector.tensor_tensor(net.dst_rel[:, :, h], net.bank[4][:, (2 * h + 1) * NT:(2 * h + 2) * NT],
                                            starts[:, :, h], ALU.subtract)

            @block.tensor
            def _(pe):
                pe.wait_ge(s_ones, 3)
                for c in range(n_chunks):
                    pe.wait_ge(s_cmp, c + 1)
                    for k in range(c * CK, min(KE, c * CK + CK)):
                        ins = nc.tensor.matmul(net.bank[0][0:1, 0:NW], ones_bf[:, :], before[:, c % 2, k - c * CK, :],
                                               start=(k == 0), stop=(k == KE - 1))
                    ins.then_inc(s_cmp_used, 1)
                pe.wait_ge(s_viol, 1)
                nc.tensor.matmul(net.bank[1][0:1, 0:1], any_fall[:, :], net.ones[0:TN, 0:1], start=True, stop=True).then_inc(s_lo, 1)
                pe.wait_ge(s_cols, 1)
                for j in range(6):
                    if j >= 1:
                        pe.wait_ge(s_bce, j)
                    for k in range(KT):
                        c = (k % 3) * P
                        ins = nc.tensor.matmul(net.bank2(2)[:, k // 3, c:c + P], bcast(cols[:, j, k], 1, P), net.ident[:, :],
                                               start=(k % 3 == 0), stop=True, skip_group_check=True)
                    ins.then_inc(s_bc, 1)
                pe.wait_ge(s_winf, 1)
                for h in range(2):
                    for s in range(2):
                        nc.tensor.transpose(net.bank[4][:, (2 * h + s) * NT:(2 * h + s + 1) * NT], win_f[:, h, s, :],
                                            net.ident[0:NT, 0:NT]).then_inc(s_tr, 1)


def attention_phase(nc, net, name, sem, *, heads, own, table, row, weights, residual, bias, out_kind):
    NT, H = net.NT, heads
    kind = out_kind
    first_layer = kind == "A"
    lag = 1 if kind == "B" else 0
    BK = {"B": 0, "C": 2}.get(kind, 1)
    loads = [] if weights is None else [weights, net.w[2]] if kind == "B" else [weights]
    with ExitStack() as ctx:
        def sb(n, shape, dt=F32):
            return ctx.enter_context(nc.sbuf_tensor(f"{name}_{n}", shape, dt))

        def two(n, shape, dt=F32):
            return [sb(f"{n}{i}", shape, dt) for i in range(2)]

        def s_(n):
            return sem(f"{name}_{n}")

        XW = D + 8
        bias_row = sb("bias_row", [TN, D])
        q_bias = s_("bias")
        idx = two("idx", [P, 2], I32)
        rows = two("rows", [P, 2, XW])
        mine = two("mine", [TN, D]) if own else None
        resid = two("resid", [TN, D]) if residual is not None else None
        onehot = two("onehot", [P, 2, HALF])
        neg = two("neg", [P, 2, HALF])
        masked = two("masked", [P, H, 2, HALF])
        onehot_t = two("onehot_t", [TN, WIN])
        smax = two("smax", [TN, H])
        msum = two("msum", [TN, H])
        nd = two("nd", [TN, 2 * H])
        eself = two("eself", [TN, 1]) if own else None
        us = two("us", [TN, 4]) if own else None
        xself = two("xself", [TN, 1]) if own else None
        diag = two("diag", [TN, TN + 1]) if own else None
        e1 = two("e1", [P, 2, H]); e2 = two("e2", [P, 2, H]); e3 = two("e3", [P, 2, H]); e4 = two("e4", [P, 2, H])
        ex = two("ex", [P, 2, H])
        coef = two("coef", [P, 2, HALF]) if H == 1 else None
        zsum = two("zsum", [TN, H]); rz = two("rz", [TN, H])
        yt_hi = two("yt_hi", [P, KT, TN + 1], F32R) if weights is not None else None
        yt_lo = two("yt_lo", [P, KT, TN + 1], F32R) if weights is not None else None
        w_in = [sb(f"w_in{j}", [P, KT, D]) for j in range(len(loads))]
        hrow = [w_in[0][0:TN, :, :].rearrange("p k n -> p (k n)")[:, i * (D + 16):(i + 1) * (D + 16)] for i in range(2)] if kind == "B" else None
        w_hi = [sb(f"w_hi{j}", [P, KT, D + 16 * j], F32R) for j in range(len(loads))]
        w_lo = [sb(f"w_lo{j}", [P, KT, D + 16 * j], F32R) for j in range(len(loads))]
        scaled = two("scaled", [P, 2, XW]) if H > 1 else None
        onehot_k = two("onehot_k", [P, 2, HALF]) if H > 1 else None
        junk = [sb(f"junk{i}", [P, D]) for i in range({"A": 6, "C": 6}.get(kind, 0))]
        own_prod = sb("own_prod", [TN, 2, D]) if first_layer else None
        o1 = two("o1", [TN, D])
        o2 = two("o2", [TN, D + 2])
        o3 = two("o3", [TN, D]) if kind == "C" else None
        st6 = two("st6", [TN, 2, 6]); mv = two("mv", [TN, 2]); rs = two("rs", [TN, 8])
        x1t_hi = two("x1t_hi", [P, KT, TN + 1], F32R) if kind == "B" else None
        x1t_lo = two("x1t_lo", [P, KT, TN + 1], F32R) if kind == "B" else None

        q_idx = s_("idx"); q_gather = [[s_("gather00"), s_("gather01")], [s_("gather10"), s_("gather11")]]
        q_own = [s_("own0"), s_("own1")]; q_res = [s_("res0"), s_("res1")]
        c_front = s_("c_front"); c_mid = s_("c_mid"); c_exp = s_("c_exp"); c_back = s_("c_back"); c_back2 = s_("c_back2"); c_evac = s_("c_evac")
        q_masked = s_("masked"); q_mt = s_("mt"); q_nd = s_("nd"); q_g = s_("g"); q_dself = s_("dself"); q_xself = s_("xself")
        q_logit = s_("logit"); q_exp = s_("exp"); q_coef = s_("coef"); q_diag = s_("diag"); q_agg = s_("agg")
        q_y = s_("y"); q_rz = s_("rz"); q_o = s_("o"); q_oread = s_("oread"); q_pre = s_("pre"); q_out = s_("out"); q_e2 = s_("e2")
        q_store = [s_("store0"), s_("store1")]; q_ecopy = s_("ecopy"); q_resb = s_("resb"); q_var = s_("var"); q_pow = s_("pow")
        q_t1 = s_("t1"); q_t1e = s_("t1e"); q_h = s_("h"); q_he = s_("he"); q_hstore = [s_("hstore0"), s_("hstore1")]
        q_scaled = s_("scaled"); q_scaled2 = s_("scaled2"); q_ndin = s_("ndin")
        q_w = s_("w"); q_whi = s_("whi"); q_wlo = s_("wlo"); q_ylo = s_("ylo"); q_t1lo = s_("t1lo")
        q_go = s_("go"); q_go2 = s_("go2"); q_ownp = s_("ownp")
        q_b = s_("b"); q_c1 = s_("c1"); q_c2 = s_("c2"); q_mvr = s_("mvr")

        bank = net.bank
        if kind == "C":
            ps_m = net.bank2(4)
            ps_g = bank[6]
            ps_o = [net.bank2(0), net.bank2(2)]
            ps_y = None
        else:
            ps_m = None
            ps_o = [net.bank2(0), net.bank2(0) if kind == "B" else net.bank2(2)]
            ps_h = net.bank2(2)
            ps_y = net.bank2(4)
            ps_g = bank[6]
        ps_mt = bank[7] if kind != "C" else None
        EC = 256
        ps_e = net.psum[:, 6:8, EC:EC + 2 * H]
        n_o = 1 if kind == "B" else 2
        ZC = 8

        def sources(p):
            return rows[p][:, :, D:D + H]

        with nc.Block() as block:
            @block.sync
            def _(sp):
                def step(s, p):
                    t = s + 2
                    if has(t, NT):
                        if own:
                            if not isinstance(s, int) or s >= 0:
                                sp.wait_ge(q_agg, t - 1)
                            sp.dma_start(mine[p][:, :], net.tiles(table)[t][:, 0:D]).then_inc(q_own[p], 16)
                    t = s + 1
                    if has(t, NT) and residual is not None:
                        if not isinstance(s, int) or s >= 1:
                            sp.wait_ge(q_pre, t - 1)
                        sp.dma_start(resid[1 - p][:, :], net.tiles(residual)[t]).then_inc(q_res[1 - p], 16)
                    t = s - 1
                    if has(t, NT):
                        sp.wait_ge(q_out, t + 1)
                        if kind in "AC":
                            sp.wait_ge(q_e2, t + 1)
                            sp.dma_start(net.tiles(net.g[kind])[t], o2[1 - p][:, :]).then_inc(q_store[1 - p], 16)
                        elif kind == "B":
                            sp.dma_start(net.tiles(net.x1)[t], o2[1 - p][:, 0:D]).then_inc(q_store[1 - p], 16)
                        else:
                            sp.dma_start(net.tiles(net.out)[t], o2[1 - p][:, 0:D]).then_inc(q_store[1 - p], 16)
                    t = s - 2
                    if kind == "B" and has(t, NT):
                        sp.wait_ge(q_he, t + 1)
                        sp.dma_start(net.tiles(net.h)[t], hrow[p][:, :]).then_inc(q_hstore[p], 16)
                for j, w in enumerate(loads):
                    sp.dma_start(w_in[j][:, :, :], w.rearrange("(k p) n -> p k n", p=P)).then_inc(q_w, 16)
                steps(sp, NT, -2, 1 + lag, step)
                for q in q_store + (q_hstore if kind == "B" else []):
                    sp.wait_ge(q, 16 * (NT // 2))

            @block.gpsimd
            def _(pool):
                def gather(t, p):
                    if not isinstance(t, int) or t >= 2:
                        for h in range(2):
                            pool.wait_ge(q_gather[p][h], 16 * (nth(t) - 1))
                    nc.gpsimd.tensor_copy(idx[p][:, :], net.src_idx[:, t, :]).then_inc(q_idx, 1)
                    pool.wait_ge(q_idx, t + 1)
                    if not isinstance(t, int) or t >= 2:
                        if kind == "C":
                            pool.wait_ge(q_scaled, t - 1)
                            pool.wait_ge(q_scaled2, t - 1)
                        else:
                            pool.wait_ge(q_agg, t - 1)
                    pool.sem_inc(q_go, 1)
                    for h in range(2):
                        nc.gpsimd.indirect_dma_start(
                            out=rows[p][:, h, 0:row], out_offset=None, in_=table[:, :],
                            in_offset=bass.IndirectOffsetOnAxis(ap=idx[p][:, h:h + 1], axis=0)).then_inc(q_gather[p][h], 16)

                def step(s, p):
                    if isinstance(s, int) and s == -1 and kind != "A":
                        pool.wait_ge(q_bias, 16)
                    if has(s + 2, NT) and kind != "C":
                        gather(s + 2, p)
                    t = s - BK
                    if has(t, NT) and kind == "D":
                        r = rs[(p + BK) % 2]
                        pool.wait_ge(q_var, t + 1)
                        nc.gpsimd.tensor_tensor(r[:, 1:2], r[:, 0:1], net.minus_half[0:TN, :], ALU.pow).then_inc(q_pow, 1)
                    t = s + 1
                    if has(t, NT) and kind == "C":
                        pool.wait_ge(q_exp, t + 1)
                        q = 1 - p
                        nc.gpsimd.tensor_tensor(scaled[q][:, 1, 0:D].rearrange("p (h c) -> p h c", h=H),
                                                rows[q][:, 1, 0:D].rearrange("p (h c) -> p h c", h=H),
                                                bcast(scaled[q][:, 1, D:D + H], 2, D // H), ALU.mult).then_inc(q_scaled2, 1)
                    if has(s + 3, NT) and kind == "C":
                        gather(s + 3, 1 - p)
                    if has(t, NT) and kind == "B":
                        pool.wait_ge(q_res[1 - p], 16 * nth(t))
                        nc.gpsimd.tensor_tensor(resid[1 - p][:, :], resid[1 - p][:, :], bias_row[:, :], ALU.add).then_inc(q_resb, 1)
                    if has(t, NT) and kind == "D":
                        pool.wait_ge(q_res[1 - p], 16 * nth(t))
                        nc.gpsimd.tensor_tensor(resid[1 - p][:, :], resid[1 - p][:, :], bias_row[:, :], ALU.add).then_inc(q_resb, 1)
                    t = s - BK
                    if has(t, NT) and kind == "B":
                        r = rs[(p + BK) % 2]
                        pool.wait_ge(q_var, t + 1)
                        nc.gpsimd.tensor_tensor(r[:, 1:2], r[:, 0:1], net.minus_half[0:TN, :], ALU.pow).then_inc(q_pow, 1)
                    t = s - 1
                    if has(t, NT) and kind == "C":
                        pool.wait_ge(q_oread, t + 1)
                        nc.gpsimd.tensor_tensor(o1[1 - p][:, :], o1[1 - p][:, :], bias_row[:, :], ALU.add).then_inc(q_b, 1)
                    t = s + 2
                    if has(t, NT) and first_layer:
                        pool.wait_ge(q_own[p], 16 * nth(t))
                        if not isinstance(t, int) or t >= 1:
                            pool.wait_ge(q_ndin, 2 * t)
                        nc.gpsimd.tensor_tensor(own_prod[:, :, :], bcast(mine[p][:, :], 1, 2), net.v[0:TN, 0:2, :],
                                                ALU.mult).then_inc(q_ownp, 1)
                    t = s - BK - 1
                    if has(t, NT) and kind in "AC":
                        pool.wait_ge(q_e2, t + 1)
                        nc.gpsimd.tensor_copy(net.e_own[:, t, :], o2[(p + BK + 1) % 2][:, D:D + 2]).then_inc(q_ecopy, 1)
                steps(pool, NT, -3 if kind == "C" else -2, BK + 1, step)
                pool.wait_ge(q_idx, NT)

            @block.scalar
            def _(act):
                def weights_of(t, q):
                    if own:
                        act.wait_ge(q_dself, t + 1)
                        nc.scalar.activation(xself[q][:, :], us[q][:, 2:3], ACT.Exp).then_inc(q_xself, 1)
                    if kind == "C":
                        if not isinstance(t, int) or t >= 2:
                            act.wait_ge(q_o, t - 1)
                        act.wait_ge(q_masked, t + 1)
                        nc.scalar.copy(onehot_k[q][:, :, :], onehot[q][:, :, :])
                    act.wait_ge(q_logit, t + 1)
                    out_ = ex[q][:, :, :] if H == 1 else scaled[q][:, :, D:D + H]
                    nc.scalar.activation(out_, e4[q][:, :, :], ACT.Exp).then_inc(q_exp, 1)

                def copy_aggregate(t, q):
                    act.wait_ge(q_agg, t + 1)
                    if not isinstance(t, int) or t >= 2:
                        act.wait_ge(q_o, t - 1)
                    for b in range(2):
                        nc.scalar.copy(yt_hi[q][:, 3 * b:3 * b + 3, :].rearrange("p k n -> p (k n)"),
                                       ps_y[:, b, 0:3 * (TN + 1)]).then_inc(q_y, 1)

                def finish(t, q):
                    if kind == "A":
                        act.wait_ge(q_pre, t + 1)
                        if not isinstance(t, int) or t >= 2:
                            act.wait_ge(q_store[q], 16 * (nth(t) - 1))
                        nc.scalar.activation(o2[q][:, 0:D], o1[q][:, :], ACT.Relu).then_inc(q_out, 1)
                    if kind in "BD":
                        act.wait_ge(q_mvr, t + 1)
                        if not isinstance(t, int) or t >= 2:
                            act.wait_ge(q_store[q], 16 * (nth(t) - 1))
                            if kind == "B":
                                act.wait_ge(q_t1, t - 1)
                        nc.scalar.activation(o2[q][:, 0:D], o1[q][:, :], ACT.Identity, bias=rs[q][:, 6:7],
                                             scale=rs[q][:, 5:6]).then_inc(q_out, 1)
                    if kind == "C":
                        act.wait_ge(q_b, t + 1)
                        nc.scalar.activation(o3[q][:, :], o1[q][:, :], ACT.Relu, scale=-1.0).then_inc(q_c1, 1)
                        act.wait_ge(q_c1, t + 1)
                        nc.scalar.activation(o3[q][:, :], o3[q][:, :], ACT.Exp, scale=-1.0).then_inc(q_c2, 1)

                def copy_turned(t, q):
                    act.wait_ge(q_t1, t + 1)
                    if not isinstance(t, int) or t >= 2:
                        act.wait_ge(q_h, t - 1)
                    for b in range(2):
                        nc.scalar.copy(x1t_hi[q][:, 3 * b:3 * b + 3, :].rearrange("p k n -> p (k n)"),
                                       ps_y[:, b, 0:3 * (TN + 1)]).then_inc(q_t1e, 1)

                def copy_next(t, q):
                    act.wait_ge(q_h, t + 1)
                    if not isinstance(t, int) or t >= 2:
                        act.wait_ge(q_hstore[q], 16 * (nth(t) - 1))
                    nc.scalar.copy(net.e_dst8[:, t, :], ps_h[0:TN, 1, HC + 8:HC + 16])
                    nc.scalar.copy(hrow[q][:, 0:HC], ps_h[0:TN, 0, 0:HC])
                    nc.scalar.copy(hrow[q][:, HC:D + 16], ps_h[0:TN, 1, 0:HC + 16]).then_inc(q_he, 1)

                def own_parts(t, q):
                    act.wait_ge(q_ownp, t + 1)
                    nc.scalar.activation(junk[2][0:TN, :], own_prod[:, 0, :], ACT.Copy, accum_out=eself[q][:, :]).then_inc(q_ndin, 1)
                    nc.scalar.activation(junk[3][0:TN, :], own_prod[:, 1, :], ACT.Copy, accum_out=nd[q][:, 0:1]).then_inc(q_ndin, 1)

                def step(s, p):
                    if has(s + 1, NT):
                        weights_of(s + 1, 1 - p)
                    if kind == "B" and has(s - 1, NT):
                        copy_turned(s - 1, 1 - p)
                    if kind in "AC" and has(s - 1, NT):
                        finish(s - 1, 1 - p)
                    if kind != "C" and has(s + 1, NT):
                        copy_aggregate(s + 1, 1 - p)
                    if kind == "D" and has(s - 1, NT):
                        finish(s - 1, 1 - p)
                    if first_layer and has(s + 2, NT):
                        own_parts(s + 2, p)
                    if kind == "B" and has(s, NT):
                        finish(s, p)
                    if kind == "B" and has(s - 1, NT):
                        copy_next(s - 1, 1 - p)
                act.dma_start(bias_row[:, :], bcast(bias, 0, TN)).then_inc(q_bias, 16)
                if loads:
                    act.wait_ge(q_w, 16 * len(loads))
                    for j in range(len(loads)):
                        nc.scalar.copy(w_hi[j][:, :, 0:D], w_in[j][:, :, :]).then_inc(q_whi, 1)
                    if kind == "B":
                        nc.scalar.copy(w_hi[1][:, :, D:D + 16], net.w_att[:, :, :]).then_inc(q_whi, 1)
                steps(act, NT, -2, 1, step)

            @block.vector
            def _(dve):
                def chain(q, t, per_tile):
                    n = [0]

                    def link(ins):
                        n[0] += 1
                        assert n[0] <= per_tile
                        ins.then_inc(q, 1)
                        dve.wait_ge(q, per_tile * t + n[0])
                    return link

                def front(t, p):
                    link = chain(c_front, t, 3 if first_layer else 2)
                    for h in range(2):
                        dve.wait_ge(q_gather[p][h], 16 * nth(t))
                    nc_onehot = nc.vector.tensor_tensor(onehot[p][:, :, :], net.node[:, :, :], bcast(net.dst_rel[:, t, :], 2, HALF), ALU.is_equal)
                    link(nc_onehot)
                    ins = nc.vector.tensor_scalar(neg[p][:, :, :], onehot[p][:, :, :], -1.0, BIG, ALU.add, ALU.mult)
                    if first_layer:
                        ins.then_inc(c_front, 1)
                        for h in range(2):
                            ins = nc.vector.tensor_tensor_reduce(junk[h][:, :], rows[p][:, h, 0:D], net.v[:, 0, :], 1.0, 0.0,
                                                                 ALU.mult, ALU.add, rows[p][:, h, D:D + 1])
                        ins.then_inc(c_front, 1)
                        dve.wait_ge(c_front, 3 * t + 3)
                    else:
                        link(ins)
                        if own:
                            nc.vector.tensor_copy(eself[p][:, :], net.e_own[:, t, 0:1]).then_inc(q_ndin, 1)
                        if H == 1:
                            nc.vector.tensor_copy(nd[p][:, 0:1], net.e_own[:, t, 1:2]).then_inc(q_ndin, 1)
                        else:
                            nc.vector.tensor_copy(nd[p][:, 0:H], net.e_dst8[:, t, :]).then_inc(q_ndin, 1)

                def mask(t, p):
                    if not isinstance(t, int) or t >= 2:
                        dve.wait_ge(q_mt, t - 1)
                    for hh in range(2):
                        ins = nc.vector.tensor_tensor(masked[p][:, :, hh, :], bcast(neg[p][:, hh, :], 1, H),
                                                      bcast(rows[p][:, hh, D:D + H], 2, HALF), ALU.add)
                    ins.then_inc(q_masked, 1)

                n_ndin = 2 if own else 1

                def middle(t, p):
                    link = chain(c_mid, t, 4 if own else 2)
                    dve.wait_ge(q_mt, t + 1)
                    dve.wait_ge(q_ndin, n_ndin * t + n_ndin)
                    if H == 1:
                        m = ps_mt[0:TN, 0:WIN]
                        link(nc.vector.tensor_reduce(smax[p][:, :], m, AX.X, ALU.max))
                        first = m
                    else:
                        m = ps_m[0:TN, :, :].rearrange("p b (h e) -> p (b h) e", e=WIN)
                        link(nc.vector.tensor_reduce(smax[p][:, :], m, AX.X, ALU.max))
                        first = ps_m[0:TN, 0, 0:WIN]
                    nc.vector.tensor_scalar(onehot_t[p][:, :], first, -BIG / 2, None, ALU.is_gt)
                    if own:
                        link(nc.vector.scalar_tensor_tensor(out=msum[p][:, :], in0=smax[p][:, :], scalar=eself[p][:, 0:1],
                                                            in1=nd[p][:, 0:1], op0=ALU.max, op1=ALU.add))
                    else:
                        link(nc.vector.tensor_tensor(msum[p][:, :], smax[p][:, :], nd[p][:, 0:H], ALU.add))
                    ins = nc.vector.scalar_tensor_tensor(out=nd[p][:, H:2 * H], in0=msum[p][:, :], scalar=SLOPE,
                                                         in1=msum[p][:, :], op0=ALU.mult, op1=ALU.max)
                    ins.then_inc(q_nd, 1)
                    if own:
                        link(nc.vector.tensor_tensor(us[p][:, 0:1], eself[p][:, :], nd[p][:, 0:1], ALU.add))
                        link(nc.vector.scalar_tensor_tensor(out=us[p][:, 1:2], in0=us[p][:, 0:1], scalar=SLOPE,
                                                            in1=us[p][:, 0:1], op0=ALU.mult, op1=ALU.max))
                        dve.wait_ge(q_nd, t + 1)
                        nc.vector.tensor_tensor(us[p][:, 2:3], us[p][:, 1:2], nd[p][:, 1:2], ALU.subtract).then_inc(q_dself, 1)

                def logits(t, p):
                    link = chain(c_exp, t, 3)
                    g = ps_e
                    dve.wait_ge(q_g, t + 1)
                    link(nc.vector.tensor_tensor(e1[p][:, :, :], sources(p), g[:, :, 0:H], ALU.add))
                    link(nc.vector.scalar_tensor_tensor(out=e2[p][:, :, :], in0=e1[p][:, :, :], scalar=SLOPE,
                                                        in1=e1[p][:, :, :], op0=ALU.mult, op1=ALU.max))
                    link(nc.vector.tensor_tensor(e3[p][:, :, :], e2[p][:, :, :], g[:, :, H:2 * H], ALU.subtract))
                    nc.vector.tensor_scalar(e4[p][:, :, :], e3[p][:, :, :], 0.0, None, ALU.min).then_inc(q_logit, 1)

                def weigh(t, p):
                    if own:
                        dve.wait_ge(q_xself, t + 1)
                        nc.vector.tensor_scalar(diag[p][:, :], net.ident[0:TN, 0:TN + 1], xself[p][:, 0:1], None,
                                                ALU.mult).then_inc(q_diag, 1)
                    dve.wait_ge(q_exp, t + 1)
                    if H == 1:
                        nc.vector.tensor_tensor(coef[p][:, :, :], onehot[p][:, :, :], bcast(ex[p][:, :, 0], 2, HALF),
                                                ALU.mult).then_inc(q_coef, 1)
                    else:
                        nc.vector.tensor_tensor(scaled[p][:, 0, 0:D].rearrange("p (h c) -> p h c", h=H),
                                                rows[p][:, 0, 0:D].rearrange("p (h c) -> p h c", h=H),
                                                bcast(scaled[p][:, 0, D:D + H], 2, D // H), ALU.mult).then_inc(q_scaled, 1)

                def low_parts(lo, hi, q_hi, q_lo, t, p):
                    if not isinstance(t, int) or t >= 2:
                        dve.wait_ge(q_o if q_hi is q_y else q_h, t - 1)
                    for b in range(2):
                        dve.wait_ge(q_hi, 2 * t + 1 + b)
                        nc.vector.tensor_tensor(lo[p][:, 3 * b:3 * b + 3, :].rearrange("p k n -> p (k n)"), ps_y[:, b, 0:3 * (TN + 1)],
                                                hi[p][:, 3 * b:3 * b + 3, :].bitcast(F32).rearrange("p k n -> p (k n)"),
                                                ALU.subtract).then_inc(q_lo, 1)

                def weights_low():
                    dve.wait_ge(q_whi, len(loads) + (kind == "B"))
                    for j in range(len(loads)):
                        nc.vector.tensor_tensor(w_lo[j][:, :, 0:D], w_in[j][:, :, :], w_hi[j][:, :, 0:D].bitcast(F32),
                                                ALU.subtract).then_inc(q_wlo, 1)
                    if kind == "B":
                        nc.vector.tensor_tensor(w_lo[1][:, :, D:D + 16], net.w_att[:, :, :], w_hi[1][:, :, D:D + 16].bitcast(F32),
                                                ALU.subtract).then_inc(q_wlo, 1)

                def sums(t, p):
                    dve.wait_ge(q_agg, t + 1)
                    if own:
                        ins = nc.vector.tensor_scalar(zsum[p][:, :], ps_g[0:TN, ZC:ZC + 1], xself[p][:, 0:1], None, ALU.add)
                    else:
                        ins = nc.vector.tensor_scalar(zsum[p][:, :], ps_g[0:TN, ZC:ZC + 1], 1e-16, None, ALU.add)
                    ins.then_inc(c_evac, 1)
                    dve.wait_ge(c_evac, t + 1)
                    nc.vector.reciprocal(rz[p][:, :], zsum[p][:, :]).then_inc(q_rz, 1)

                def back(t, p):
                    dve.wait_ge(q_o, t + 1)
                    o = ps_o[p][0:TN, :, 0:HC]
                    v = o1[p][:, :].rearrange("p (b c) -> p b c", b=2)
                    if kind == "C":
                        link = chain(c_back, t, 2)
                        link(nc.vector.tensor_scalar(zsum[p][:, :], ps_o[p][0:TN, 1, HC:HC + H], 1e-16, None, ALU.add))
                        link(nc.vector.reciprocal(rz[p][:, :], zsum[p][:, :]))
                        for b in range(2):
                            ins = nc.vector.tensor_tensor(
                                o1[p][:, b * HC:(b + 1) * HC].rearrange("p (h c) -> p h c", h=H // 2),
                                ps_o[p][0:TN, b, 0:HC].rearrange("p (h c) -> p h c", h=H // 2),
                                bcast(rz[p][:, b * H // 2:(b + 1) * H // 2], 2, D // H), ALU.mult)
                        ins.then_inc(q_oread, 1)
                    else:
                        dve.wait_ge(q_rz, t + 1)
                        if kind == "A":
                            if isinstance(t, int) and t == 0:
                                dve.wait_ge(q_bias, 16)
                            nc.vector.scalar_tensor_tensor(out=v, in0=o, scalar=rz[p][:, 0:1],
                                                           in1=bias_row[:, :].rearrange("p (b c) -> p b c", b=2),
                                                           op0=ALU.mult, op1=ALU.add).then_inc(q_pre, 1)
                        else:
                            dve.wait_ge(q_resb, t + 1)
                            if not isinstance(t, int) or t >= 2:
                                dve.wait_ge(q_out, t - 1)
                            nc.vector.scalar_tensor_tensor(out=v, in0=o, scalar=rz[p][:, 0:1],
                                                           in1=resid[p][:, :].rearrange("p (b c) -> p b c", b=2),
                                                           op0=ALU.mult, op1=ALU.add).then_inc(q_pre, 1)
                            dve.wait_ge(q_pre, t + 1)
                            link = chain(c_back, t, 2)
                            nc.vector.bn_stats(st6[p][:, 0, :], o1[p][:, 0:HC])
                            link(nc.vector.bn_stats(st6[p][:, 1, :], o1[p][:, HC:D]))
                            dve.sem_inc(q_go2, 1)
                            link(nc.vector.bn_aggr(mv[p][:, :], st6[p][:, :, :]))
                            nc.vector.tensor_scalar(rs[p][:, 0:1], mv[p][:, 1:2], EPS, None, ALU.add).then_inc(q_var, 1)

                def back_end(t, p):
                    if kind in "BD":
                            link = chain(c_back2, t, 4)
                            dve.wait_ge(q_var, t + 1)
                            dve.wait_ge(q_pow, t + 1)
                            link(nc.vector.tensor_tensor(rs[p][:, 2:3], rs[p][:, 1:2], rs[p][:, 1:2], ALU.mult))
                            link(nc.vector.tensor_tensor(rs[p][:, 3:4], rs[p][:, 2:3], rs[p][:, 0:1], ALU.mult))
                            link(nc.vector.tensor_scalar(rs[p][:, 4:5], rs[p][:, 3:4], -0.5, 1.5, ALU.mult, ALU.add))
                            link(nc.vector.tensor_tensor(rs[p][:, 5:6], rs[p][:, 4:5], rs[p][:, 1:2], ALU.mult))
                            nc.vector.scalar_tensor_tensor(out=rs[p][:, 6:7], in0=mv[p][:, 0:1], scalar=-1.0,
                                                           in1=rs[p][:, 5:6], op0=ALU.mult, op1=ALU.mult).then_inc(q_mvr, 1)
                    if kind == "C":
                        dve.wait_ge(q_c2, t + 1)
                        if not isinstance(t, int) or t >= 2:
                            dve.wait_ge(q_store[p], 16 * (nth(t) - 1))
                            dve.wait_ge(q_ecopy, t - 1)
                        nc.vector.scalar_tensor_tensor(out=o2[p][:, 0:D], in0=o3[p][:, :], scalar=-1.0, in1=o1[p][:, :],
                                                       op0=ALU.add, op1=ALU.max).then_inc(q_out, 1)
                    if kind in "AC":
                        j = 2 if kind == "A" else 4
                        dve.wait_ge(q_out, t + 1)
                        if kind == "A" and (not isinstance(t, int) or t >= 2):
                            dve.wait_ge(q_ecopy, t - 1)
                        for a in range(2):
                            ins = nc.vector.tensor_tensor_reduce(junk[4 + a][0:TN, :], o2[p][:, 0:D], net.v[0:TN, j + a, :], 1.0, 0.0,
                                                                 ALU.mult, ALU.add, o2[p][:, D + a:D + a + 1])
                        ins.then_inc(q_e2, 1)

                def step_heads(s, p):
                    if has(s + 1, NT):
                        middle(s + 1, 1 - p)
                    if has(s + 2, NT):
                        front(s + 2, p)
                    if has(s + 1, NT):
                        logits(s + 1, 1 - p)
                    if has(s + 2, NT):
                        mask(s + 2, p)
                    if has(s + 1, NT):
                        weigh(s + 1, 1 - p)
                    if has(s - 1, NT):
                        back(s - 1, 1 - p)
                    if has(s - 2, NT):
                        back_end(s - 2, p)

                def step(s, p):
                    if has(s + 1, NT):
                        middle(s + 1, 1 - p)
                        logits(s + 1, 1 - p)
                        weigh(s + 1, 1 - p)
                    if kind != "B" and has(s - 1, NT):
                        back(s - 1, 1 - p)
                    if kind == "B" and has(s - 1, NT):
                        low_parts(x1t_lo, x1t_hi, q_t1e, q_t1lo, s - 1, 1 - p)
                    if has(s + 2, NT):
                        front(s + 2, p)
                        mask(s + 2, p)
                    if has(s + 1, NT):
                        sums(s + 1, 1 - p)
                        low_parts(yt_lo, yt_hi, q_y, q_ylo, s + 1, 1 - p)
                    if isinstance(s, int) and s == -1:
                        weights_low()
                    if kind != "B" and has(s - 1, NT):
                        back_end(s - 1, 1 - p)
                    if kind == "B" and has(s, NT):
                        back(s, p)
                        back_end(s, p)
                if kind == "C":
                    steps(dve, NT, -2, 2, step_heads)
                else:
                    steps(dve, NT, -2, 1, step)

            @block.tensor
            def _(pe):
                def mask_t(t, p):
                    pe.wait_ge(q_masked, t + 1)
                    if not isinstance(t, int) or t >= 1:
                        pe.wait_ge(q_nd, t)
                    for h in range(H):
                        dst_ = ps_mt if H == 1 else ps_m[:, h // 4, :]
                        c = (h % 4) * WIN
                        for w in range(2):
                            ins = nc.tensor.matmul(dst_[HALF * w:HALF * w + HN[w], c:c + WIN], masked[p][:, h, w, 0:HN[w]],
                                                   net.ident[:, :], start=True, stop=True)
                    ins.then_inc(q_mt, 1)

                def spread(t, p):
                    pe.wait_ge(q_nd, t + 1)
                    if not isinstance(t, int) or t >= 1:
                        if kind != "C":
                            pe.wait_ge(q_rz, t)
                        pe.wait_ge(q_logit, t)
                    for w in range(2):
                        a = HALF * w
                        ins = nc.tensor.matmul(ps_e[:, w, :], onehot_t[p][a:a + HN[w], :],
                                               nd[p][a:a + HN[w], :], start=True, stop=True)
                    ins.then_inc(q_g, 1)

                def aggregate(t, p):
                    pe.wait_ge(q_coef, t + 1)
                    if own:
                        pe.wait_ge(q_diag, t + 1)
                        if not first_layer:
                            pe.wait_ge(q_own[p], 16 * nth(t))
                    if not isinstance(t, int) or t >= 1:
                        pe.wait_ge(q_ylo, 2 * t)
                    if kind == "B" and (not isinstance(t, int) or t >= 2):
                        pe.wait_ge(q_t1lo, 2 * (t - 1))
                    for k in range(KT):
                        y = ps_y[:, k // 3, (k % 3) * (TN + 1):(k % 3 + 1) * (TN + 1)]
                        new = k % 3 == 0
                        f = slice(k * P, (k + 1) * P)
                        if own:
                            nc.tensor.matmul(y[:, :], mine[p][:, f], diag[p][:, :], start=new, stop=False, skip_group_check=True)
                        nc.tensor.matmul(y[:, 0:HALF], rows[p][:, 0, f], coef[p][:, 0, :], start=new and not own, stop=True, skip_group_check=True)
                        nc.tensor.matmul(y[:, HALF:TN + 1], rows[p][:, 1, f], coef[p][:, 1, 0:TN + 1 - HALF], start=False, stop=True, skip_group_check=True)
                    for w in range(2):
                        ins = nc.tensor.matmul(ps_g[HALF * w:HALF * w + HN[w], ZC:ZC + 1], coef[p][:, w, 0:HN[w]], net.ones[:, 0:1],
                                               start=True, stop=True, skip_group_check=True)
                    ins.then_inc(q_agg, 1)

                def split_product(out_, banks, a_hi, a_lo, b_hi, b_lo, k):
                    for a_, b_, first, last in ((a_hi, b_hi, k == 0, False), (a_hi, b_lo, False, False), (a_lo, b_hi, False, k == KT - 1)):
                        for b, n in banks:
                            ins = nc.tensor.matmul(out_[0:TN, b, 0:n], a_[:, k, 0:TN], b_[:, k, b * HC:b * HC + n],
                                                   start=first, stop=last)
                    return ins

                def product(t, p, k0, k1):
                    o = ps_o[p]
                    if k0 == 0:
                        pe.wait_ge(q_ylo, 2 * t + 2)
                        if isinstance(t, int) and t == 0:
                            pe.wait_ge(q_wlo, len(loads) + (kind == "B"))
                        if not isinstance(t, int) or t >= n_o:
                            pe.wait_ge(q_pre, t + 1 - n_o)
                    for k in range(k0, k1):
                        ins = split_product(o, [(0, HC), (1, HC)], yt_hi[p], yt_lo[p], w_hi[0], w_lo[0], k)
                    if k1 == KT:
                        ins.then_inc(q_o, 1)

                def turn(t, q, s):
                    pe.wait_ge(q_out, t + 1)
                    if has(s, NT):
                        pe.wait_ge(q_ylo, 2 * s + 2)
                    for k in range(KT):
                        ins = nc.tensor.transpose(ps_y[:, k // 3, (k % 3) * (TN + 1):(k % 3) * (TN + 1) + TN],
                                                  o2[q][:, k * P:(k + 1) * P], net.ident[0:TN, 0:TN])
                    ins.then_inc(q_t1, 1)

                def next_product(t, q):
                    pe.wait_ge(q_t1lo, 2 * t + 2)
                    if not isinstance(t, int) or t >= 1:
                        pe.wait_ge(q_he, t)
                    for k in range(KT):
                        ins = split_product(ps_h, [(0, HC), (1, HC + 16)], x1t_hi[q], x1t_lo[q], w_hi[1], w_lo[1], k)
                    ins.then_inc(q_h, 1)

                def step(s, p):
                    if kind == "C":
                        if has(s + 1, NT):
                            mask_t(s + 1, 1 - p)
                            spread(s + 1, 1 - p)
                            t, q = s + 1, 1 - p
                        if has(s, NT):
                            pe.wait_ge(q_scaled, s + 1)
                            pe.wait_ge(q_scaled2, s + 1)
                            if not isinstance(s, int) or s >= 2:
                                pe.wait_ge(q_oread, s - 1)
                            for b, n in ((0, HC), (1, HC + H)):
                                for w in range(2):
                                    ins = nc.tensor.matmul(ps_o[p][HALF * w:HALF * w + HN[w], b, 0:n], onehot_k[p][:, w, 0:HN[w]],
                                                           scaled[p][:, w, b * HC:b * HC + n], start=True, stop=True)
                            ins.then_inc(q_o, 1)
                        return
                    if has(s + 1, NT):
                        mask_t(s + 1, 1 - p)
                    if has(s, NT):
                        product(s, p, 0, 2)
                    if has(s + 1, NT):
                        spread(s + 1, 1 - p)
                    if kind == "B" and has(s - 1, NT):
                        turn(s - 1, 1 - p, s)
                    if has(s, NT):
                        product(s, p, 2, 4)
                    if has(s + 1, NT):
                        aggregate(s + 1, 1 - p)
                    if has(s, NT):
                        product(s, p, 4, 6)
                    if kind == "B" and has(s - 1, NT):
                        next_product(s - 1, 1 - p)
                steps(pe, NT, -1, 1, step)

def general_graph(nc, net, sem):
    NT = net.NT
    with ExitStack() as ctx:
        node_i = ctx.enter_context(nc.sbuf_tensor("self_i", [P, NT, 2], I32))
        edge_i = ctx.enter_context(nc.sbuf_tensor("edge_i", [P, NT, 2], I32))
        s_iota = sem("n_iota")
        with nc.Block() as block:
            @block.gpsimd
            def _(pool):
                nc.gpsimd.iota(node_i[:, :, :], pattern=[[TN, NT], [HALF, 2]], base=0, channel_multiplier=1).then_inc(s_iota, 1)
                nc.gpsimd.iota(edge_i[:, :, :], pattern=[[0, NT], [0, 2]], base=0, channel_multiplier=1).then_inc(s_iota, 1)

            @block.vector
            def _(dve):
                dve.wait_ge(s_iota, 2)
                nc.vector.tensor_scalar(net.src_idx[:, :, :], node_i[:, :, :], float(net.N - 1), None, ALU.min)
                nc.vector.tensor_copy(net.dst_rel[:, :, :], edge_i[:, :, :])


def general_sums(nc, net, name, sem, *, heads, own, table, row, first_layer):
    N, E, NT, H = net.N, net.E, net.NT, heads
    NC = E // TN
    C = D // H
    src_cols = net.src.rearrange("(c e) -> c e", e=TN)
    with ExitStack() as ctx:
        def sb(n, shape, dt=F32):
            return ctx.enter_context(nc.sbuf_tensor(f"{name}_{n}", shape, dt))

        def s_(n):
            return sem(f"{name}_{n}")

        idx = sb("idx", [TN, 1], I32)
        rows = sb("rows", [TN, D + 8])
        mine = sb("mine", [TN, D])
        prod = [sb(f"prod{i}", [TN, D]) for i in range(3)]
        pair = sb("pair", [TN, 2])
        s_idx = s_("idx"); s_row = s_("row"); s_cell = s_("cell"); s_store = s_("store"); s_own = s_("own"); s_pair = s_("pair"); s_kept = s_("kept"); s_turn = s_("turn")

        with nc.Block() as block:
            @block.sync
            def _(sp):
                with sp.Fori(0, NC) as c:
                    sp.dma_start(idx[:, :], src_cols[c].unsqueeze(1)).then_inc(s_idx, 16)
                    sp.wait_ge(s_cell, c + 1) if first_layer else sp.wait_ge(s_row, 16 * c + 16)
                    with nc.allow_non_contiguous_dma(reason="four bytes per edge and head, in the slow path only"):
                        sp.dma_start(net.esrc[0:H, bass.ds(c * TN, TN)].rearrange("h e -> e h"), rows[:, D:D + H]).then_inc(s_store, 16)
                    sp.wait_ge(s_store, 16 * c + 16)
                    sp.sem_inc(s_turn, 1)
                if first_layer:
                    with sp.Fori(0, NT) as t:
                        sp.dma_start(mine[:, :], net.tiles(table)[t]).then_inc(s_own, 16)
                        sp.wait_ge(s_kept, t + 1)
                        sp.sem_inc(s_turn, 1)

            @block.gpsimd
            def _(pool):
                with pool.Fori(0, NC) as c:
                    pool.wait_ge(s_idx, 16 * c + 16)
                    pool.sem_inc(s_pair, 1)
                    nc.gpsimd.indirect_dma_start(out=rows[:, 0:row], out_offset=None, in_=table[:, :],
                                                 in_offset=bass.IndirectOffsetOnAxis(ap=idx[:, 0:1], axis=0)).then_inc(s_row, 16)

            @block.vector
            def _(dve):
                if first_layer:
                    with dve.Fori(0, NC) as c:
                        dve.wait_ge(s_row, 16 * c + 16)
                        nc.vector.tensor_tensor_reduce(prod[0][:, :], rows[:, 0:D], net.v[0:TN, 0, :], 1.0, 0.0,
                                                       ALU.mult, ALU.add, rows[:, D:D + 1]).then_inc(s_cell, 1)
                        dve.wait_ge(s_cell, c + 1)
                    with dve.Fori(0, NT) as t:
                        dve.wait_ge(s_own, 16 * t + 16)
                        for a in range(2):
                            ins = nc.vector.tensor_tensor_reduce(prod[1 + a][:, :], mine[:, :], net.v[0:TN, a, :], 1.0, 0.0,
                                                                 ALU.mult, ALU.add, pair[:, a:a + 1])
                        ins.then_inc(s_cell, 1)
                        dve.wait_ge(s_cell, NC + t + 1)
                        nc.vector.tensor_copy(net.e_own[:, t, :], pair[:, :]).then_inc(s_kept, 1)
                        dve.wait_ge(s_kept, t + 1)

    with ExitStack() as ctx:
        name += "s"
        idx = sb("idx", [TN, 1], I32)
        rows = sb("rows", [TN, D + 8])
        mine = sb("mine", [TN, D])
        part = sb("part", [TN, E])
        w = sb("w", [TN, E])
        zeros = sb("zeros", [TN, 8])
        c_ = sb("cells", [TN, 12])
        piece = sb("piece", [TN, TN])
        piece_t = sb("piece_t", [TN, TN])
        res = sb("res", [TN, 3, D])
        acc = net.bank2(0)
        s_to = s_("to"); s_part = s_("part"); s_idx = s_("idx"); s_row = s_("row"); s_own = s_("own"); s_go = s_("go")
        s_chain = s_("chain"); s_m = s_("m"); s_exp = s_("exp"); s_piece = s_("piece"); s_t = s_("t"); s_pt = s_("pt")
        s_mm = s_("mm"); s_res = s_("res"); s_store = s_("store"); s_turn = s_("turn")
        LINKS = 17 + (3 if own else 0)

        with nc.Block() as block:
            @block.sync
            def _(sp):
                with sp.Fori(0, H) as h:
                    sp.dma_start(part[:, :], bcast(net.esrc[h], 0, TN)).then_inc(s_part, 16)
                    with sp.Fori(0, NT) as t:
                        r = h * NT + t
                        sp.dma_start(w[:, :].bitcast(I32), bcast(net.dst, 0, TN)).then_inc(s_to, 16)
                        if own:
                            sp.dma_start(mine[:, :], net.tiles(table)[t][:, 0:D]).then_inc(s_own, 16)
                        with sp.Fori(0, NC) as c:
                            sp.dma_start(idx[:, :], src_cols[c].unsqueeze(1)).then_inc(s_idx, 16)
                            sp.wait_ge(s_mm, r * NC + c + 1)
                            sp.sem_inc(s_turn, 1)
                        sp.wait_ge(s_res, r + 1)
                        sp.dma_start(net.tiles(net.agg)[t][:, bass.ds(h * C, C)], res[:, 2, 0:C]).then_inc(s_store, 16)
                        sp.dma_start(net.tiles(net.agg)[t][:, D:D + 8], zeros[:, :]).then_inc(s_store, 16)
                        sp.wait_ge(s_store, 32 * r + 32)
                        sp.sem_inc(s_turn, 1)

            @block.gpsimd
            def _(pool):
                with pool.Fori(0, H * NT * NC) as k:
                    pool.wait_ge(s_idx, 16 * k + 16)
                    pool.sem_inc(s_go, 1)
                    nc.gpsimd.indirect_dma_start(out=rows[:, 0:row], out_offset=None, in_=table[:, :],
                                                 in_offset=bass.IndirectOffsetOnAxis(ap=idx[:, 0:1], axis=0)).then_inc(s_row, 16)

            @block.scalar
            def _(act):
                with act.Fori(0, H * NT) as r:
                    act.wait_ge(s_m, r + 1)
                    if own:
                        nc.scalar.activation(c_[:, 7:8], c_[:, 6:7], ACT.Exp)
                    nc.scalar.activation(w[:, :], w[:, :], ACT.Exp, bias=c_[:, 4:5]).then_inc(s_exp, 1)

            @block.vector
            def _(dve):
                nc.vector.memset(zeros[:, :], 0.0)
                with dve.Fori(0, H) as h:
                    dve.wait_ge(s_part, 16 * h + 16)
                    dve.sem_inc(s_turn, 1)
                    with dve.Fori(0, NT) as t:
                        r = h * NT + t
                        n = [0]

                        def link(ins):
                            n[0] += 1
                            ins.then_inc(s_chain, 1)
                            dve.wait_ge(s_chain, r * LINKS + n[0])

                        dve.wait_ge(s_to, 16 * r + 16)
                        link(nc.vector.tensor_copy(w[:, :], w[:, :].bitcast(I32)))
                        link(nc.vector.tensor_scalar(w[:, :], w[:, :], net.node_ids[:, bass.ds(t, 1)], None, ALU.is_equal))
                        link(nc.vector.tensor_scalar(w[:, :], w[:, :], -1.0, BIG, ALU.add, ALU.mult))
                        link(nc.vector.tensor_tensor(w[:, :], w[:, :], part[:, :], ALU.add))
                        if H == 1:
                            link(nc.vector.tensor_copy(c_[:, 0:2], net.e_own[:, t, :]))
                        else:
                            link(nc.vector.tensor_copy(c_[:, 1:2], net.e_dst8.rearrange("p t h -> p (t h)")[:, bass.ds(t * 8 + h, 1)]))
                        link(nc.vector.tensor_reduce(c_[:, 2:3], w[:, :], AX.X, ALU.max))
                        if own:
                            link(nc.vector.scalar_tensor_tensor(out=c_[:, 2:3], in0=c_[:, 2:3], scalar=c_[:, 0:1], in1=c_[:, 1:2],
                                                                op0=ALU.max, op1=ALU.add))
                        else:
                            link(nc.vector.tensor_tensor(c_[:, 2:3], c_[:, 2:3], c_[:, 1:2], ALU.add))
                        link(nc.vector.scalar_tensor_tensor(out=c_[:, 3:4], in0=c_[:, 2:3], scalar=SLOPE, in1=c_[:, 2:3],
                                                            op0=ALU.mult, op1=ALU.max))
                        link(nc.vector.tensor_scalar(c_[:, 4:5], c_[:, 3:4], -BIG / 100, -1.0, ALU.max, ALU.mult))
                        if own:
                            link(nc.vector.tensor_tensor(c_[:, 5:6], c_[:, 0:1], c_[:, 1:2], ALU.add))
                            link(nc.vector.scalar_tensor_tensor(out=c_[:, 5:6], in0=c_[:, 5:6], scalar=SLOPE, in1=c_[:, 5:6],
                                                                op0=ALU.mult, op1=ALU.max))
                            link(nc.vector.tensor_tensor(c_[:, 6:7], c_[:, 5:6], c_[:, 4:5], ALU.add))
                        link(nc.vector.tensor_scalar(w[:, :], w[:, :], c_[:, 1:2], None, ALU.add))
                        link(nc.vector.scalar_tensor_tensor(out=w[:, :], in0=w[:, :], scalar=SLOPE, in1=w[:, :], op0=ALU.mult, op1=ALU.max))
                        dve.sem_inc(s_m, 1)
                        dve.wait_ge(s_exp, r + 1)
                        link(nc.vector.tensor_reduce(c_[:, 8:9], w[:, :], AX.X, ALU.add))
                        link(nc.vector.tensor_scalar(c_[:, 9:10], c_[:, 8:9], c_[:, 7:8] if own else 1e-16, None, ALU.add))
                        link(nc.vector.reciprocal(c_[:, 10:11], c_[:, 9:10]))
                        dve.sem_inc(s_turn, 1)
                        with dve.Fori(0, NC) as c:
                            nc.vector.tensor_copy(piece[:, :], w[:, bass.ds(c * TN, TN)]).then_inc(s_piece, 1)
                            dve.wait_ge(s_t, r * NC + c + 1)
                            nc.vector.tensor_copy(piece_t[:, :], net.bank[2][0:TN, 0:TN]).then_inc(s_pt, 1)
                            dve.wait_ge(s_mm, r * NC + c + 1)
                        if own:
                            dve.wait_ge(s_own, 16 * r + 16)
                            link(nc.vector.tensor_scalar(res[:, 0, :], mine[:, :], c_[:, 7:8], None, ALU.mult))
                        else:
                            link(nc.vector.memset(res[:, 0, :], 0.0))
                        o = acc[0:TN, :, 0:C // 2] if H == 1 else acc[0:TN, 0:1, 0:C]
                        nb = 2 if H == 1 else 1
                        link(nc.vector.tensor_tensor(res[:, 1, 0:C].rearrange("p (b c) -> p b c", b=nb), o,
                                                        res[:, 0, 0:C].rearrange("p (b c) -> p b c", b=nb), ALU.add))
                        link(nc.vector.tensor_scalar(res[:, 2, 0:C], res[:, 1, 0:C], c_[:, 10:11], None, ALU.mult))
                        dve.sem_inc(s_res, 1)
                        dve.wait_ge(s_store, 32 * r + 32)
                        assert n[0] == LINKS, n

            @block.tensor
            def _(pe):
                def chunk(k, h, first):
                    pe.wait_ge(s_piece, k + 1)
                    nc.tensor.transpose(net.bank[2][0:TN, 0:TN], piece[:, :], net.ident[0:TN, 0:TN]).then_inc(s_t, 1)
                    pe.wait_ge(s_pt, k + 1)
                    pe.wait_ge(s_row, 16 * k + 16)
                    if H == 1:
                        for b in range(2):
                            ins = nc.tensor.matmul(acc[0:TN, b, 0:HC], piece_t[:, :], rows[:, b * HC:(b + 1) * HC],
                                                   start=first, stop=True, skip_group_check=True)
                    else:
                        ins = nc.tensor.matmul(acc[0:TN, 0, 0:C], piece_t[:, :], rows[:, bass.ds(h * C, C)],
                                               start=first, stop=True, skip_group_check=True)
                    ins.then_inc(s_mm, 1)

                with pe.Fori(0, H) as h:
                    with pe.Fori(0, NT) as t:
                        k = (h * NT + t) * NC
                        chunk(k, h, True)
                        with pe.Fori(1, NC) as c:
                            chunk(k + c, h, False)


def gat_program(nc, ext, out, N, E):
    with ExitStack() as ctx:
        net = Net()
        net.N, net.E, net.NT = N, E, N // TN
        NT = net.NT

        def sb(name, shape, dt=F32):
            return ctx.enter_context(nc.sbuf_tensor(name, shape, dt))

        def dram(name, shape, dt=F32):
            return nc.dram_tensor(name, shape, dt, kind="Internal").ap()

        sems = []

        def sem(name):
            sems.append(nc.alloc_semaphore(name))
            return sems[-1]

        def retire():
            nc.clear_and_free_semaphores(list(sems))
            sems.clear()
            nc.all_engine_barrier()

        net.w = [ext[n] for n in ("L0_gnn_W1", "L0_gnn_W2", "L1_gnn_W1", "L1_gnn_W2")]
        net.w_att = sb("w_att", [P, KT, 16])
        net.v = sb("attention_rows", [P, 6, D])
        net.ident = sb("ident", [P, P])
        net.ones = sb("ones", [P, 2])
        net.minus_half = sb("minus_half", [P, 1])
        net.node = sb("node", [P, 2, HALF])
        net.src_idx = sb("src_idx", [P, NT, 2], I32)
        net.dst_rel = sb("dst_rel", [P, NT, 2])
        net.e_own = sb("e_own", [TN, NT, 2])
        net.e_dst8 = sb("e_dst8", [TN, NT, 8])
        net.flag = sb("flag", [1, 1], I32)
        net.node_ids = sb("node_ids", [TN, NT])
        psum = ctx.enter_context(nc.psum_tensor("psum", [P, 8, OB], F32))
        net.psum = psum
        net.bank = [psum[:, b, :] for b in range(8)]
        net.bank2 = lambda b: psum[:, b:b + 2, :]
        net.edges = dram("edges", [2, E + WIN], I32)
        net.windows = dram("windows", [2 * NT, 2, WIN], I32)
        net.g = {"A": dram("g1", [N, D + 2]), "C": dram("g3", [N, D + 2])}
        net.x1 = dram("x1", [N, D])
        net.h = dram("h", [N, D + 16])
        net.agg = dram("agg", [N, D + 8])
        net.esrc = dram("esrc", [8, E])
        net.src, net.dst = ext["src"], ext["dst"]
        net.out = out
        net.tiles = lambda a: a.rearrange("(t p) d -> t p d", p=TN)
        x = ext["x"]

        prepare(nc, net, ext, sem)
        retire()
        flag = nc.values_load(net.flag[0:1, 0:1], min_val=0, max_val=TN + 1)

        layers = [dict(heads=1, own=True, weights=net.w[0], residual=None, bias=ext["L0_gnn_b1"], out_kind="A"),
                  dict(heads=1, own=True, weights=net.w[1], residual=x, bias=ext["L0_gnn_b2"], out_kind="B"),
                  dict(heads=8, own=False, weights=None, residual=None, bias=ext["L1_gnn_b1"], out_kind="C"),
                  dict(heads=1, own=False, weights=net.w[3], residual=net.x1, bias=ext["L1_gnn_b2"], out_kind="D")]
        tables = [(x, D), (net.g["A"], D + 2), (net.h, D + 8), (net.g["C"], D + 2)]
        with nc.If(flag == 0):
            for layer, (table, row) in zip(layers, tables):
                attention_phase(nc, net, layer["out_kind"], sem, table=table, row=row, **layer)
                retire()
        with nc.Else():
            for layer, (table, row) in zip(layers, tables):
                kind = layer["out_kind"]
                general_sums(nc, net, f"s{kind}", sem, heads=layer["heads"], own=layer["own"], table=table, row=row,
                             first_layer=kind == "A")
                retire()
                if kind == "A":
                    general_graph(nc, net, sem)
                    retire()
                attention_phase(nc, net, f"g{kind}", sem, table=net.agg, row=D if kind == "A" else D + layer["heads"], **layer)
                retire()


_INS = ["x", "src", "dst", "L0_gnn_W1", "L0_gnn_att_src1", "L0_gnn_att_dst1", "L0_gnn_b1", "L0_gnn_W2", "L0_gnn_att_src2",
        "L0_gnn_att_dst2", "L0_gnn_b2", "L1_gnn_W1", "L1_gnn_a_src1", "L1_gnn_a_dst1", "L1_gnn_b1", "L1_gnn_W2",
        "L1_gnn_a_src2", "L1_gnn_a_dst2", "L1_gnn_b2"]


def kernel(**inputs):
    import numpy as _np
    import concourse.bacc as _bacc
    from concourse import mybir as _mybir
    from concourse.bass_utils import run_bass_kernel_spmd as _run

    nc = _bacc.Bacc("TRN2", target_bir_lowering=False, num_devices=1)
    arrays, ext = {}, {}
    for name in _INS:
        a = _np.ascontiguousarray(inputs[name])
        arrays[f"in_{name}"] = a
        ext[name] = nc.dram_tensor(f"in_{name}", a.shape, _mybir.dt.from_np(a.dtype), kind="ExternalInput").ap()
    shape = arrays["in_x"].shape
    out = nc.dram_tensor("out_0", shape, _mybir.dt.float32, kind="ExternalOutput").ap()
    gat_program(nc, ext, out, shape[0], arrays["in_src"].shape[0])
    r = _run(nc, [arrays], core_ids=[0])
    return r.results[0]["out_0"]
```

```python
from contextlib import ExitStack

import concourse.bass as bass
from concourse import mybir

F32 = mybir.dt.float32
I32 = mybir.dt.int32
BF16 = mybir.dt.bfloat16
F32R = mybir.dt.float32r
ALU = mybir.AluOpType
ACT = mybir.ActivationFunctionType
AX = mybir.AxisListType

P = 128
D = 768
KT = D // P
TN = 125
HALF = 64
HN = [HALF, TN - HALF]
WIN = 128
BIG = 1e30
FAR = 1 << 20
SLOPE = 0.2
EPS = 1e-5
OB = 512
HC = D // 2
PEEL = 4


class Net:
    pass


def steps(eng, n_tiles, first, last, step, nb):
    for s in range(first, PEEL):
        step(s, s % nb)
    n_loop = (n_tiles - PEEL - 3) // nb
    with eng.Fori(0, n_loop) as i:
        for j in range(nb):
            step(nb * i + PEEL + j, j)
    for s in range(PEEL + nb * n_loop, n_tiles + last):
        step(s, s % nb)


def has(s, n_tiles):
    return not isinstance(s, int) or 0 <= s < n_tiles


def nth(s):
    return s // 2 + 1


def bcast(ap, at, n):
    return ap.unsqueeze(at).to_broadcast([*ap.shape[:at], n, *ap.shape[at:]])


def prepare(nc, net, ext, sem):
    N, E, NT = net.N, net.E, net.NT
    NW = 2 * NT
    KE = E // TN
    src, dst = ext["src"], ext["dst"]
    with ExitStack() as ctx:
        def sb(name, shape, dt=F32):
            return ctx.enter_context(nc.sbuf_tensor(name, shape, dt))

        padding = sb("padding", [2, WIN], I32)
        dst_i = sb("dst_i", [TN, KE], I32)
        next_i = sb("next_i", [TN, KE], I32)
        dst_f = sb("dst_f", [TN, KE])
        next_f = sb("next_f", [TN, KE])
        falls = sb("falls", [TN, KE])
        any_fall = sb("any_fall", [TN, 1])
        starts_i = sb("starts_i", [P, NT, 2], I32)
        starts = net.starts
        CK = 20
        before = sb("before", [TN, 2, CK, NW], BF16)
        ones_bf = sb("ones_bf", [TN, 1], BF16)
        lo = sb("lo", [1, NW + 1])
        over = sb("over", [1, NW])
        worst = sb("worst", [1, 2])
        a_rows = sb("a_rows", [P, 2, D])
        prod = sb("prod", [P, KT, D])
        ident_i = sb("ident_i", [P, P], I32)
        node_i = sb("node_i", [P, 2, HALF], I32)
        node_ids_i = sb("node_ids_i", [TN, NT], I32)

        s_edges = sem("p_edges"); s_dst = sem("p_dst"); s_w = sem("p_weights")
        s_iota = sem("p_iota"); s_chain = sem("p_chain"); s_cmp = sem("p_cmp"); s_cmp_used = sem("p_cmp_used")
        s_lo = sem("p_lo"); s_viol = sem("p_viol")
        s_ones = sem("p_ones"); s_padm = sem("p_padm")

        n_chunks = -(-KE // CK)
        with nc.Block() as block:
            @block.sync
            def _(sp):
                sp.dma_start(net.edges[0, 0:E], src).then_inc(s_edges, 16)
                sp.dma_start(net.edges[1, 0:E], dst).then_inc(s_edges, 16)
                sp.dma_start(dst_i[:, :], dst.rearrange("(p k) -> p k", k=KE)).then_inc(s_dst, 16)
                sp.wait_ge(s_padm, 1)
                sp.dma_start(net.edges[:, E:E + WIN], padding[:, :]).then_inc(s_edges, 16)
                sp.wait_ge(s_edges, 48)
                sp.dma_start(next_i[:, :], net.edges[1, 1:E + 1].rearrange("(p k) -> p k", k=KE)).then_inc(s_dst, 16)

            @block.scalar
            def _(act):
                act.dma_start(net.w_in[:, :, :], net.w[0].rearrange("(k p) n -> p k n", p=P)).then_inc(s_w, 16)
                for j, name in enumerate(("L0_gnn_att_src1", "L0_gnn_att_dst1")):
                    act.dma_start(a_rows[:, j, :], bcast(ext[name].rearrange("h c -> (h c)") if len(ext[name].shape) == 2 else ext[name], 0, P)).then_inc(s_w, 16)

            @block.gpsimd
            def _(pool):
                nc.gpsimd.iota(padding[:, :], pattern=[[0, WIN]], base=0, channel_multiplier=FAR).then_inc(s_padm, 1)
                nc.gpsimd.iota(starts_i[:, :, :], pattern=[[TN, NT], [HALF, 2]], base=0, channel_multiplier=0).then_inc(s_iota, 1)
                nc.gpsimd.iota(node_ids_i[:, :], pattern=[[TN, NT]], base=0, channel_multiplier=1).then_inc(s_iota, 1)
                nc.gpsimd.iota(node_i[:, :, :], pattern=[[0, 2], [1, HALF]], base=0, channel_multiplier=0).then_inc(s_iota, 1)
                nc.gpsimd.iota(ident_i[:, :], pattern=[[1, P]], base=0, channel_multiplier=-1).then_inc(s_iota, 1)

            @block.vector
            def _(dve):
                n = [0]

                def link(ins):
                    n[0] += 1
                    ins.then_inc(s_chain, 1)
                    dve.wait_ge(s_chain, n[0])

                nc.vector.memset(ones_bf[:, :], 1.0).then_inc(s_ones, 1)
                nc.vector.memset(net.ones[:, :], 1.0).then_inc(s_ones, 1)
                nc.vector.memset(net.minus_half[:, :], -0.5)
                nc.vector.memset(lo[0:1, NW:NW + 1], float(E))
                dve.wait_ge(s_iota, 4)
                nc.vector.tensor_copy(net.node_ids[:, :], node_ids_i[:, :])
                nc.vector.tensor_copy(starts[:, :, :], starts_i[:, :, :])
                nc.vector.tensor_copy(net.node[:, :, :], node_i[:, :, :])
                nc.vector.tensor_scalar(net.ident[:, :], ident_i[:, :], 0.0, None, ALU.is_equal).then_inc(s_ones, 1)
                dve.wait_ge(s_dst, 32)
                nc.vector.tensor_copy(next_f[:, :], next_i[:, :])
                link(nc.vector.tensor_copy(dst_f[:, :], dst_i[:, :]))
                for c in range(n_chunks):
                    k0, k1 = c * CK, min(KE, c * CK + CK)
                    if c >= 2:
                        dve.wait_ge(s_cmp_used, c - 1)
                    nc.vector.tensor_tensor(
                        before[:, c % 2, 0:k1 - k0, :], bcast(dst_f[:, k0:k1], 2, NW),
                        bcast(starts[0:TN, :, :].rearrange("p t h -> p (t h)"), 1, k1 - k0), ALU.is_lt).then_inc(s_cmp, 1)
                dve.wait_ge(s_w, 48)
                for a in range(2):
                    for k in range(KT):
                        ins = nc.vector.tensor_tensor_reduce(prod[:, k, :], net.w_in[:, k, :], a_rows[:, a, :], 1.0, 0.0,
                                                             ALU.mult, ALU.add, net.w_att[:, k, a:a + 1])
                    link(ins)
                link(nc.vector.tensor_tensor(falls[:, :], dst_f[:, :], next_f[:, :], ALU.is_gt))
                nc.vector.tensor_reduce(any_fall[:, :], falls[:, :], AX.X, ALU.max).then_inc(s_viol, 1)
                dve.wait_ge(s_lo, 1)
                nc.vector.tensor_copy(net.lo_i[0:1, :], net.bank[0][0:1, 0:NW])
                link(nc.vector.tensor_copy(lo[0:1, 0:NW], net.bank[0][0:1, 0:NW]))
                link(nc.vector.tensor_tensor(over[:, :], lo[0:1, 1:NW + 1], lo[0:1, 0:NW], ALU.subtract))
                link(nc.vector.tensor_reduce(worst[0:1, 0:1], over[:, :], AX.X, ALU.max))
                link(nc.vector.tensor_scalar(worst[0:1, 1:2], worst[0:1, 0:1], float(WIN), None, ALU.is_gt))
                nc.vector.tensor_tensor(net.flag[0:1, 0:1], worst[0:1, 1:2], net.bank[1][0:1, 0:1], ALU.add)

            @block.tensor
            def _(pe):
                pe.wait_ge(s_ones, 3)
                for c in range(n_chunks):
                    pe.wait_ge(s_cmp, c + 1)
                    for k in range(c * CK, min(KE, c * CK + CK)):
                        ins = nc.tensor.matmul(net.bank[0][0:1, 0:NW], ones_bf[:, :], before[:, c % 2, k - c * CK, :],
                                               start=(k == 0), stop=(k == KE - 1))
                    ins.then_inc(s_cmp_used, 1)
                pe.wait_ge(s_viol, 1)
                nc.tensor.matmul(net.bank[1][0:1, 0:1], any_fall[:, :], net.ones[0:TN, 0:1], start=True, stop=True).then_inc(s_lo, 1)


def beside_projection(nc, net, ext, sem, ctx):
    NT = net.NT

    def sb(name, shape, dt=F32):
        return ctx.enter_context(nc.sbuf_tensor(name, shape, dt))

    win_i = sb("win_i", [NT, 2, 2, WIN], I32)
    win_f = sb("win_f", [NT, 2, 2, WIN])
    weights = {j: sb(f"w{j}", [P, KT, D]) for j in (1, 2, 3)}
    names = {1: ("L0_gnn_att_src2", "L0_gnn_att_dst2"), 2: ("L1_gnn_a_src1", "L1_gnn_a_dst1"), 3: ("L1_gnn_a_src2", "L1_gnn_a_dst2")}
    a_rows = sb("a_rows_next", [P, 6, D])
    prod = sb("head_products", [P, KT, D])
    s_w = {j: sem(f"w_weights{j}") for j in (1, 2, 3)}
    s_win = sem("w_win"); s_load = sem("w_load"); s_winf = sem("w_winf"); s_tr = sem("w_tr"); s_prod = sem("w_prod"); s_fold = sem("w_fold")
    tail = PEEL + 2 * ((NT - PEEL - 3) // 2)
    beside = Net()

    def pool():
        pool = nc.gpsimd
        for j in (1, 3, 2):
            pool.dma_start(weights[j][:, :, :], net.w[j].rearrange("(k p) n -> p k n", p=P)).then_inc(s_w[j], 16)
            for i, name in enumerate(names[j]):
                v = ext[name] if len(ext[name].shape) == 1 else ext[name].rearrange("h c -> (h c)")
                pool.dma_start(a_rows[:, 2 * j - 2 + i, :], bcast(v, 0, P)).then_inc(s_w[j], 16)
        with pool.Fori(0, 2 * NT) as w:
            at = pool.value_load(net.lo_i[0:1, bass.ds(w, 1)], min_val=0, max_val=net.E)
            pool.dma_start(net.windows[w], net.edges[:, bass.ds(at, WIN)]).then_inc(s_win, 16)
        pool.wait_ge(s_win, 32 * NT)
        pool.dma_start(win_i[:, :, :, :], net.windows.rearrange("(t h) s e -> t h s e", h=2)).then_inc(s_load, 16)
        pool.wait_ge(s_w[2], 48)
        pool.wait_ge(s_fold, 2)
        pool.tensor_tensor(prod[:, :, :], weights[2][:, :, :], bcast(a_rows[:, 2, :], 1, KT), ALU.mult).then_inc(s_prod, 1)
        pool.tensor_tensor(weights[2][:, :, :], weights[2][:, :, :], bcast(a_rows[:, 3, :], 1, KT), ALU.mult).then_inc(s_prod, 1)

    def dve(s):
        for at, j, n, spare in ((3, 1, 0, prod), (tail, 3, 2, weights[1])):
            if s == at:
                nc.vector.wait_ge(s_w[j], 48)
                if n:
                    nc.vector.wait_ge(s_fold, n)
                for a, out_ in enumerate((spare, weights[j])):
                    for k in range(KT):
                        ins = nc.vector.tensor_tensor_reduce(out_[:, k, :], weights[j][:, k, :], a_rows[:, 2 * j - 2 + a, :], 1.0, 0.0,
                                                             ALU.mult, ALU.add, net.w_att[:, k, net.att_col[j] + a:net.att_col[j] + a + 1])
                    ins.then_inc(s_fold, 1)
        for at, i, x in ((tail + 1, 0, prod), (tail + 2, 1, weights[2])):
            if s == at:
                nc.vector.wait_ge(s_prod, i + 1)
                c = net.att_col[2] + 8 * i
                nc.vector.tensor_reduce(net.w_att[:, :, c:c + 8], x[:, :, :].rearrange("p k (h c) -> p k h c", h=8), AX.X, ALU.add)
        if s == tail + 3:
            nc.vector.wait_ge(s_load, 16)
            nc.vector.tensor_copy(win_f[:, :, :, :], win_i[:, :, :, :]).then_inc(s_winf, 1)
        if s == NT:
            nc.vector.wait_ge(s_tr, 4)
            for h in range(2):
                nc.vector.tensor_copy(net.src_idx[:, :, h], net.bank[0][:, (2 * h) * NT:(2 * h + 1) * NT])
                nc.vector.tensor_tensor(net.dst_rel[:, :, h], net.bank[0][:, (2 * h + 1) * NT:(2 * h + 2) * NT],
                                        net.starts[:, :, h], ALU.subtract)

    def pe(s):
        if s == NT - 1:
            nc.tensor.wait_ge(s_winf, 1)
            for h in range(2):
                for i in range(2):
                    nc.tensor.transpose(net.bank[0][:, (2 * h + i) * NT:(2 * h + i + 1) * NT], win_f[:, h, i, :],
                                        net.ident[0:NT, 0:NT]).then_inc(s_tr, 1)

    beside.pool, beside.dve, beside.pe = pool, dve, pe
    return beside


def layer_phase(nc, net, name, sem, kind, *, heads=1, own=False, table=None, row=None, residual=None, bias=None, out_rows=None, nxt=None, beside=None):
    NT, H = net.NT, heads
    attends = kind != "X"
    AG, TU, PR = {"C": (0, -1, -2)}.get(kind, (1, 0, -1))
    NB = 4 if kind == "D" else 2
    with ExitStack() as ctx:
        def sb(n, shape, dt=F32):
            return ctx.enter_context(nc.sbuf_tensor(f"{name}_{n}", shape, dt))

        def two(n, shape, dt=F32):
            return [sb(f"{n}{i}", shape, dt) for i in range(2)] * (NB // 2)

        def s_(n):
            return sem(f"{name}_{n}")

        bank, bank2 = net.bank, net.bank2
        q_bias = s_("bias")
        if attends:
            XW = D + 8
            bias_row = sb("bias_row", [TN, D])
            idx = [sb(f"idx{i}", [P, 2], I32) for i in range(NB)]
            rows = [sb(f"rows{i}", [P, 2, XW]) for i in range(NB)]
            mine = two("mine", [TN, D]) if own else None
            resid = two("resid", [TN, D]) if residual is not None else None
            onehot = two("onehot", [P, 2, HALF])
            neg = two("neg", [P, 2, HALF])
            masked = two("masked", [P, H, 2, HALF])
            onehot_t = two("onehot_t", [TN, WIN])
            smax = two("smax", [TN, H])
            msum = two("msum", [TN, H])
            nd = two("nd", [TN, 1 + 2 * H])
            us = two("us", [TN, 4]) if own else None
            xself = two("xself", [TN, 1]) if own else None
            e1 = two("e1", [P, 2, H]); e2 = two("e2", [P, 2, H]); e3 = two("e3", [P, 2, H]); e4 = two("e4", [P, 2, H])
            ex = two("ex", [P, 2, H])
            coef = two("coef", [P, 2, HALF]) if H == 1 else None
            scaled = two("scaled", [P, 2, XW]) if H > 1 else None
            onehot_k = two("onehot_k", [P, 2, HALF]) if H > 1 else None
            zsum = two("zsum", [TN, H]); rz = two("rz", [TN, H])
            o1 = two("o1", [TN, D])
            o3 = two("o3", [TN, D]) if kind == "C" else None
            st6 = two("st6", [TN, 2, 6]); mv = two("mv", [TN, 2]); rs = two("rs", [TN, 8])
        o2 = two("o2", [TN, D])
        if nxt is not None:
            n_w, n_heads, n_table = nxt
            NH = 2 * n_heads
            at = net.att_col[n_w]
            t_hi = two("t_hi", [P, KT, TN + 1], F32R); t_lo = two("t_lo", [P, KT, TN + 1], F32R)
            w_hi = sb("w_hi", [P, KT, D + NH], F32R); w_lo = sb("w_lo", [P, KT, D + NH], F32R)
            hrow = two("hrow", [TN, D + NH])

        q_idx = s_("idx"); q_gather = [[s_(f"gather{i}{h}") for h in range(2)] for i in range(NB)]
        q_own, q_res, q_in, q_store, q_hstore = ([s_(f"{n}{i}") for i in range(2)] * (NB // 2) for n in ("own", "res", "in", "store", "hstore"))
        q_masked = s_("masked"); q_mt = s_("mt"); q_nd = s_("nd"); q_g = s_("g"); q_dself = s_("dself"); q_xself = s_("xself")
        q_ndin = s_("ndin"); q_logit = s_("logit"); q_exp = s_("exp"); q_coef = s_("coef"); q_agg = s_("agg")
        q_scaled = s_("scaled"); q_scaled2 = s_("scaled2")
        q_pre = s_("pre"); q_resb = s_("resb"); q_var = s_("var"); q_rstd = s_("rstd"); q_oread = s_("oread"); q_b = s_("b"); q_rz = s_("rz"); q_front = s_("front"); q_neg = s_("neg")
        q_c1 = s_("c1"); q_c2 = s_("c2"); q_out = s_("out"); q_turn = s_("turn"); q_hi = s_("hi"); q_lo = s_("lo")
        q_prod = s_("prod"); q_evac = s_("evac"); q_whi = s_("whi"); q_wlo = s_("wlo"); q_wload = s_("wload")
        q_go = s_("go"); q_go2 = s_("go2")
        c_mid = s_("c_mid"); c_exp = s_("c_exp"); c_sum = s_("c_sum"); c_norm = s_("c_norm"); c_rstd = s_("c_rstd")

        ps_a = bank2(0)
        ps_t = bank2(2)
        ps_h = bank2(4)
        TW = 3 * (TN + 1)
        ps_m = bank2(6) if kind == "C" else bank[7][:, 0:WIN]
        ps_e = net.psum[:, 6:8, WIN:WIN + 2 * H]

        def turned(b):
            return ps_t[:, b, 0:TW].rearrange("p (k n) -> p k n", n=TN + 1)[:, :, 0:TN]

        def q(p, off):
            return (p + off) % NB

        def gathered(t):
            return 16 * (t // NB + 1)

        def past(t, k):
            return not isinstance(t, int) or t >= k

        with nc.Block() as block:
            @block.sync
            def _(sp):
                def step(s, p):
                    t = s + 2
                    if has(t, NT) and own:
                        if past(t, 2):
                            sp.wait_ge(q_pre, t - 1)
                        sp.dma_start(mine[p][:, :], net.tiles(table)[t][:, 0:D]).then_inc(q_own[p], 16)
                    if has(t, NT) and residual is not None:
                        if past(t, 2):
                            sp.wait_ge(q_pre, t - 1)
                        sp.dma_start(resid[p][:, :], net.tiles(residual)[t]).then_inc(q_res[p], 16)
                    if has(t, NT) and not attends:
                        if past(t, 2):
                            sp.wait_ge(q_turn, t - 1)
                        sp.dma_start(o2[p][:, :], net.tiles(table)[t]).then_inc(q_in[p], 16)
                    if has(s, NT) and kind in "BD":
                        sp.wait_ge(q_out, s + 1)
                        sp.dma_start(net.tiles(out_rows)[s], o2[p][:, :]).then_inc(q_store[p], 16)
                    if isinstance(s, int) and s == 2 and nxt is not None and n_w + 1 < 4:
                        sp.wait_ge(q_wlo, 2)
                        sp.dma_start(net.w_in[:, :, :], net.w[n_w + 1].rearrange("(k p) n -> p k n", p=P)).then_inc(q_wload, 16)
                    t = s + PR
                    if has(t, NT) and nxt is not None:
                        sp.wait_ge(q_evac, 2 * t + 2)
                        sp.dma_start(net.tiles(n_table)[t], hrow[q(p, PR)][:, :]).then_inc(q_hstore[q(p, PR)], 16)
                steps(sp, NT, -2, -PR, step, NB)
                if kind in "BD":
                    for d in q_store[:2]:
                        sp.wait_ge(d, 16 * (NT // 2))
                if nxt is not None:
                    for d in q_hstore[:2]:
                        sp.wait_ge(d, 16 * (NT // 2))
                    if n_w + 1 < 4:
                        sp.wait_ge(q_wload, 16)

            @block.gpsimd
            def _(pool):
                def gather(t, p):
                    if past(t, NB):
                        for h in range(2):
                            pool.wait_ge(q_gather[p][h], gathered(t) - 16)
                    nc.gpsimd.tensor_copy(idx[p][:, :], net.src_idx[:, t, :]).then_inc(q_idx, 1)
                    pool.wait_ge(q_idx, t + 1)
                    if past(t, NB):
                        if kind == "C":
                            pool.wait_ge(q_scaled, t - 1)
                            pool.wait_ge(q_scaled2, t - 1)
                        else:
                            pool.wait_ge(q_agg, t + 1 - NB)
                    pool.sem_inc(q_go, 1)
                    for h in range(2):
                        nc.gpsimd.indirect_dma_start(
                            out=rows[p][:, h, 0:row], out_offset=None, in_=table[:, :],
                            in_offset=bass.IndirectOffsetOnAxis(ap=idx[p][:, h:h + 1], axis=0)).then_inc(q_gather[p][h], 16)

                def deviation(t, p):
                    n = [0]
                    r = rs[p]

                    def link(ins):
                        n[0] += 1
                        ins.then_inc(c_rstd, 1)
                        pool.wait_ge(c_rstd, 5 * t + n[0])
                    pool.wait_ge(q_var, t + 1)
                    link(nc.gpsimd.tensor_tensor(r[:, 1:2], r[:, 0:1], net.minus_half[0:TN, :], ALU.pow))
                    link(nc.gpsimd.tensor_tensor(r[:, 2:3], r[:, 1:2], r[:, 1:2], ALU.mult))
                    link(nc.gpsimd.tensor_tensor(r[:, 3:4], r[:, 2:3], r[:, 0:1], ALU.mult))
                    pool.sem_inc(q_go, 1)
                    link(nc.gpsimd.tensor_scalar(r[:, 4:5], r[:, 3:4], -0.5, 1.5, ALU.mult, ALU.add))
                    link(nc.gpsimd.tensor_tensor(r[:, 5:6], r[:, 4:5], r[:, 1:2], ALU.mult))
                    nc.gpsimd.tensor_tensor(r[:, 6:7], mv[p][:, 0:1], r[:, 5:6], ALU.mult).then_inc(q_rstd, 1)

                def step(s, p):
                    if has(s + 2, NT) and kind in "AB":
                        gather(s + 2, p)
                    if has(s + 3, NT) and kind == "D":
                        gather(s + 3, q(p, 3))
                    if isinstance(s, int) and s == -2 and kind in "BCD":
                        pool.wait_ge(q_bias, 16)
                    if has(s, NT) and kind in "BD":
                        deviation(s, p)
                    t = s + 2
                    if has(t, NT) and kind in "BD":
                        pool.wait_ge(q_res[p], 16 * nth(t))
                        nc.gpsimd.tensor_tensor(resid[p][:, :], resid[p][:, :], bias_row[:, :], ALU.add).then_inc(q_resb, 1)
                    t = s + 1
                    if has(t, NT) and kind == "C":
                        pool.wait_ge(q_exp, t + 1)
                        z = q(p, 1)
                        nc.gpsimd.tensor_tensor(scaled[z][:, 1, 0:D].rearrange("p (h c) -> p h c", h=H),
                                                rows[z][:, 1, 0:D].rearrange("p (h c) -> p h c", h=H),
                                                bcast(scaled[z][:, 1, D:D + H], 2, D // H), ALU.mult).then_inc(q_scaled2, 1)
                    if has(s + 3, NT) and kind == "C":
                        gather(s + 3, q(p, 1))
                    if has(s, NT) and kind == "C":
                        pool.wait_ge(q_oread, s + 1)
                        nc.gpsimd.tensor_tensor(o1[p][:, :], o1[p][:, :], bias_row[:, :], ALU.add).then_inc(q_b, 1)
                if beside is not None:
                    beside.pool()
                if attends:
                    steps(pool, NT, -3 if kind in "CD" else -2, 0, step, NB)

            @block.scalar
            def _(act):
                def weights_of(t, p):
                    if own:
                        act.wait_ge(q_dself, t + 1)
                        nc.scalar.activation(xself[p][:, :], us[p][:, 2:3], ACT.Exp).then_inc(q_xself, 1)
                    if kind == "C":
                        if past(t, 2):
                            act.wait_ge(q_agg, t - 1)
                        act.wait_ge(q_masked, t + 1)
                        nc.scalar.copy(onehot_k[p][:, :, :], onehot[p][:, :, :])
                    act.wait_ge(q_logit, t + 1)
                    out_ = ex[p][:, :, :] if H == 1 else scaled[p][:, :, D:D + H]
                    nc.scalar.activation(out_, e4[p][:, :, :], ACT.Exp).then_inc(q_exp, 1)

                def own_parts(t, p):
                    if H == 1:
                        nc.scalar.copy(nd[p][:, 0:2], net.e_own[:, t, :]).then_inc(q_ndin, 1)
                    else:
                        nc.scalar.copy(nd[p][:, 1:1 + H], net.e_dst8[:, t, :]).then_inc(q_ndin, 1)
                    act.wait_ge(q_front, t + 1)
                    nc.scalar.activation(neg[p][:, :, :], onehot[p][:, :, :], ACT.Copy, bias=-BIG, scale=BIG).then_inc(q_neg, 1)

                def finish(t, p):
                    if kind == "A":
                        act.wait_ge(q_pre, t + 1)
                        if past(t, 2):
                            act.wait_ge(q_turn, t - 1)
                        nc.scalar.activation(o2[p][:, :], o1[p][:, :], ACT.Relu).then_inc(q_out, 1)
                    if kind in "BD":
                        act.wait_ge(q_rstd, t + 1)
                        if past(t, 2):
                            act.wait_ge(q_store[p], 16 * (nth(t) - 1))
                            if kind == "B":
                                act.wait_ge(q_turn, t - 1)
                        nc.scalar.activation(o2[p][:, :], o1[p][:, :], ACT.Identity, bias=rs[p][:, 6:7],
                                             scale=rs[p][:, 5:6]).then_inc(q_out, 1)
                    if kind == "C":
                        act.wait_ge(q_b, t + 1)
                        nc.scalar.activation(o3[p][:, :], o1[p][:, :], ACT.Relu, scale=-1.0).then_inc(q_c1, 1)
                        act.wait_ge(q_c1, t + 1)
                        nc.scalar.activation(o3[p][:, :], o3[p][:, :], ACT.Exp, scale=-1.0).then_inc(q_c2, 1)

                def high_parts(t, p):
                    act.wait_ge(q_turn, t + 1)
                    if past(t, 2):
                        act.wait_ge(q_prod, 2 * t - 2)
                    for b in range(2):
                        nc.scalar.copy(t_hi[p][:, 3 * b:3 * b + 3, 0:TN], turned(b)).then_inc(q_hi, 1)

                def keep(t, p):
                    if past(t, 2):
                        act.wait_ge(q_hstore[p], 16 * (nth(t) - 1))
                    act.wait_ge(q_prod, 2 * t + 1)
                    nc.scalar.copy(hrow[p][:, 0:HC], ps_h[0:TN, 0, 0:HC]).then_inc(q_evac, 1)
                    act.wait_ge(q_prod, 2 * t + 2)
                    if n_heads == 1:
                        nc.scalar.copy(net.e_own[:, t, :], ps_h[0:TN, 1, HC:HC + 2])
                    else:
                        nc.scalar.copy(net.e_dst8[:, t, :], ps_h[0:TN, 1, HC + 8:HC + 16])
                    nc.scalar.copy(hrow[p][:, HC:D + NH], ps_h[0:TN, 1, 0:HC + NH]).then_inc(q_evac, 1)

                def step(s, p):
                    if kind == "C" and has(s - 1, NT):
                        finish(s - 1, q(p, -1))
                    if has(s + 2, NT) and attends:
                        own_parts(s + 2, q(p, 2))
                    if has(s + 1, NT) and attends:
                        weights_of(s + 1, q(p, 1))
                    if kind in "BD" and has(s, NT):
                        finish(s, p)
                    if has(s + TU, NT) and nxt is not None:
                        high_parts(s + TU, q(p, TU))
                    if kind == "A" and has(s + 1, NT):
                        finish(s + 1, q(p, 1))
                    if has(s + PR, NT) and nxt is not None:
                        keep(s + PR, q(p, PR))
                if attends:
                    act.dma_start(bias_row[:, :], bcast(bias, 0, TN)).then_inc(q_bias, 16)
                if nxt is not None:
                    nc.scalar.copy(w_hi[:, :, D:D + NH], net.w_att[:, :, at:at + NH])
                    for k in (0, KT // 2):
                        nc.scalar.copy(w_hi[:, k:k + KT // 2, 0:D], net.w_in[:, k:k + KT // 2, :]).then_inc(q_whi, 1)
                steps(act, NT, -2, -PR, step, NB)

            @block.vector
            def _(dve):
                def chain(q, t, per_tile):
                    n = [0]

                    def link(ins):
                        n[0] += 1
                        assert n[0] <= per_tile
                        ins.then_inc(q, 1)
                        dve.wait_ge(q, per_tile * t + n[0])
                    return link

                def front(t, p):
                    nc.vector.tensor_tensor(onehot[p][:, :, :], net.node[:, :, :], bcast(net.dst_rel[:, t, :], 2, HALF),
                                            ALU.is_equal).then_inc(q_front, 1)

                def mask(t, p):
                    for h in range(2):
                        dve.wait_ge(q_gather[p][h], gathered(t))
                    dve.wait_ge(q_neg, t + 1)
                    if past(t, 2):
                        dve.wait_ge(q_mt, t - 1)
                    for hh in range(2):
                        ins = nc.vector.tensor_tensor(masked[p][:, :, hh, :], bcast(neg[p][:, hh, :], 1, H),
                                                      bcast(rows[p][:, hh, D:D + H], 2, HALF), ALU.add)
                    ins.then_inc(q_masked, 1)

                def middle(t, p):
                    link = chain(c_mid, t, 4 if own else 2)
                    dve.wait_ge(q_ndin, t + 1)
                    dve.wait_ge(q_mt, t + 1)
                    e_src, e_dst, top = nd[p][:, 0:1], nd[p][:, 1:1 + H], nd[p][:, 1 + H:1 + 2 * H]
                    if H == 1:
                        m = ps_m[0:TN, :]
                        first = m
                    else:
                        m = ps_m[0:TN, :, :].rearrange("p b (h e) -> p (b h) e", e=WIN)
                        first = ps_m[0:TN, 0, 0:WIN]
                    link(nc.vector.tensor_reduce(smax[p][:, :], m, AX.X, ALU.max))
                    nc.vector.tensor_scalar(onehot_t[p][:, :], first, -BIG / 2, None, ALU.is_gt)
                    if own:
                        link(nc.vector.scalar_tensor_tensor(out=msum[p][:, :], in0=smax[p][:, :], scalar=e_src,
                                                            in1=e_dst, op0=ALU.max, op1=ALU.add))
                    else:
                        link(nc.vector.tensor_tensor(msum[p][:, :], smax[p][:, :], e_dst, ALU.add))
                    nc.vector.scalar_tensor_tensor(out=top, in0=msum[p][:, :], scalar=SLOPE,
                                                   in1=msum[p][:, :], op0=ALU.mult, op1=ALU.max).then_inc(q_nd, 1)
                    if own:
                        link(nc.vector.tensor_tensor(us[p][:, 0:1], e_src, e_dst, ALU.add))
                        link(nc.vector.scalar_tensor_tensor(out=us[p][:, 1:2], in0=us[p][:, 0:1], scalar=SLOPE,
                                                            in1=us[p][:, 0:1], op0=ALU.mult, op1=ALU.max))
                        dve.wait_ge(q_nd, t + 1)
                        nc.vector.tensor_tensor(us[p][:, 2:3], us[p][:, 1:2], top, ALU.subtract).then_inc(q_dself, 1)

                def logits(t, p):
                    link = chain(c_exp, t, 3)
                    dve.wait_ge(q_g, t + 1)
                    link(nc.vector.tensor_tensor(e1[p][:, :, :], rows[p][:, :, D:D + H], ps_e[:, :, 0:H], ALU.add))
                    link(nc.vector.scalar_tensor_tensor(out=e2[p][:, :, :], in0=e1[p][:, :, :], scalar=SLOPE,
                                                        in1=e1[p][:, :, :], op0=ALU.mult, op1=ALU.max))
                    link(nc.vector.tensor_tensor(e3[p][:, :, :], e2[p][:, :, :], ps_e[:, :, H:2 * H], ALU.subtract))
                    nc.vector.tensor_scalar(e4[p][:, :, :], e3[p][:, :, :], 0.0, None, ALU.min).then_inc(q_logit, 1)

                def weigh(t, p):
                    dve.wait_ge(q_exp, t + 1)
                    if H == 1:
                        nc.vector.tensor_tensor(coef[p][:, :, :], onehot[p][:, :, :], bcast(ex[p][:, :, 0], 2, HALF),
                                                ALU.mult).then_inc(q_coef, 1)
                    else:
                        nc.vector.tensor_tensor(scaled[p][:, 0, 0:D].rearrange("p (h c) -> p h c", h=H),
                                                rows[p][:, 0, 0:D].rearrange("p (h c) -> p h c", h=H),
                                                bcast(scaled[p][:, 0, D:D + H], 2, D // H), ALU.mult).then_inc(q_scaled, 1)

                def sums(t, p):
                    if own:
                        dve.wait_ge(q_own[p], 16 * nth(t))
                        dve.wait_ge(q_xself, t + 1)
                    if kind != "C" and past(t, 2):
                        dve.wait_ge(q_out, t - 1)
                    dve.wait_ge(q_agg, t + 1)
                    link = chain(c_sum, t, 1)
                    ins = nc.vector.tensor_scalar(zsum[p][:, :], ps_a[0:TN, 1, HC:HC + H], xself[p][:, 0:1] if own else 1e-16, None, ALU.add)
                    if own:
                        ins = nc.vector.scalar_tensor_tensor(out=o1[p][:, :].rearrange("p (b c) -> p b c", b=2), in0=mine[p][:, :].rearrange("p (b c) -> p b c", b=2),
                                                             scalar=xself[p][:, 0:1], in1=ps_a[0:TN, :, 0:HC], op0=ALU.mult, op1=ALU.add)
                    link(ins)
                    nc.vector.reciprocal(rz[p][:, :], zsum[p][:, :]).then_inc(q_rz, 1)

                def divide(t, p):
                    dve.wait_ge(q_rz, t + 1)
                    if kind == "C":
                        for b in range(2):
                            ins = nc.vector.tensor_tensor(
                                o1[p][:, b * HC:(b + 1) * HC].rearrange("p (h c) -> p h c", h=H // 2),
                                ps_a[0:TN, b, 0:HC].rearrange("p (h c) -> p h c", h=H // 2),
                                bcast(rz[p][:, b * H // 2:(b + 1) * H // 2], 2, D // H), ALU.mult)
                        ins.then_inc(q_oread, 1)
                        return
                    o = o1[p][:, :].rearrange("p (b c) -> p b c", b=2)
                    if kind == "A":
                        if isinstance(t, int) and t == 0:
                            dve.wait_ge(q_bias, 16)
                        more = bias_row
                    else:
                        dve.wait_ge(q_resb, t + 1)
                        more = resid[p]
                    nc.vector.scalar_tensor_tensor(out=o, in0=o if own else ps_a[0:TN, :, 0:HC],
                                                   scalar=rz[p][:, 0:1], in1=more[:, :].rearrange("p (b c) -> p b c", b=2),
                                                   op0=ALU.mult, op1=ALU.add).then_inc(q_pre, 1)

                def moments(t, p):
                    dve.wait_ge(q_pre, t + 1)
                    link = chain(c_norm, t, 2)
                    nc.vector.bn_stats(st6[p][:, 0, :], o1[p][:, 0:HC])
                    link(nc.vector.bn_stats(st6[p][:, 1, :], o1[p][:, HC:D]))
                    dve.sem_inc(q_go2, 1)
                    link(nc.vector.bn_aggr(mv[p][:, :], st6[p][:, :, :]))
                    nc.vector.tensor_scalar(rs[p][:, 0:1], mv[p][:, 1:2], EPS, None, ALU.add)
                    nc.vector.tensor_scalar(mv[p][:, 0:1], mv[p][:, 0:1], -1.0, None, ALU.mult).then_inc(q_var, 1)

                def elu(t, p):
                    dve.wait_ge(q_c2, t + 1)
                    if past(t, 2):
                        dve.wait_ge(q_turn, t - 1)
                    nc.vector.scalar_tensor_tensor(out=o2[p][:, :], in0=o3[p][:, :], scalar=-1.0, in1=o1[p][:, :],
                                                   op0=ALU.add, op1=ALU.max).then_inc(q_out, 1)

                def low_parts(t, p):
                    if past(t, 2):
                        dve.wait_ge(q_prod, 2 * t - 2)
                    for b in range(2):
                        dve.wait_ge(q_hi, 2 * t + 1 + b)
                        nc.vector.tensor_tensor(t_lo[p][:, 3 * b:3 * b + 3, 0:TN], turned(b),
                                                t_hi[p][:, 3 * b:3 * b + 3, 0:TN].bitcast(F32), ALU.subtract).then_inc(q_lo, 1)

                def weights_low():
                    dve.wait_ge(q_whi, 1)
                    nc.vector.tensor_tensor(w_lo[:, :, D:D + NH], net.w_att[:, :, at:at + NH], w_hi[:, :, D:D + NH].bitcast(F32), ALU.subtract)
                    for i, k in enumerate((0, KT // 2)):
                        dve.wait_ge(q_whi, i + 1)
                        nc.vector.tensor_tensor(w_lo[:, k:k + KT // 2, 0:D], net.w_in[:, k:k + KT // 2, :],
                                                w_hi[:, k:k + KT // 2, 0:D].bitcast(F32), ALU.subtract).then_inc(q_wlo, 1)

                def step_last(s, p):
                    if has(s + 1, NT):
                        middle(s + 1, q(p, 1))
                    if has(s + 2, NT):
                        front(s + 2, q(p, 2))
                    if has(s, NT):
                        sums(s, p)
                        divide(s, p)
                    if has(s + 1, NT):
                        logits(s + 1, q(p, 1))
                    if has(s + 2, NT):
                        mask(s + 2, q(p, 2))
                    if has(s + 1, NT):
                        weigh(s + 1, q(p, 1))
                    if has(s, NT):
                        moments(s, p)

                def step(s, p):
                    if has(s + 1, NT) and attends:
                        middle(s + 1, q(p, 1))
                    if has(s + 2, NT) and attends:
                        front(s + 2, q(p, 2))
                    if isinstance(s, int) and s == -2 and nxt is not None:
                        weights_low()
                    if has(s, NT) and kind in "BD":
                        moments(s, p)
                    if has(s + 1, NT) and attends:
                        logits(s + 1, q(p, 1))
                    if kind == "C" and has(s - 1, NT):
                        elu(s - 1, q(p, 1))
                    if has(s + 2, NT) and kind == "C":
                        mask(s + 2, q(p, 2))
                    if has(s + 1, NT) and attends:
                        weigh(s + 1, q(p, 1))
                    if has(s + 2, NT) and attends and kind != "C":
                        mask(s + 2, q(p, 2))
                    if has(s + AG, NT) and attends:
                        sums(s + AG, q(p, AG))
                    if has(s + AG, NT) and kind in "AC":
                        divide(s + AG, q(p, AG))
                    if has(s + TU, NT) and nxt is not None:
                        low_parts(s + TU, q(p, TU))
                    if beside is not None and isinstance(s, int):
                        beside.dve(s)
                    if has(s + AG, NT) and kind == "B":
                        divide(s + AG, q(p, AG))
                steps(dve, NT, -2, 1 - TU, step_last if kind == "D" else step, NB)

            @block.tensor
            def _(pe):
                def mask_t(t, p):
                    pe.wait_ge(q_masked, t + 1)
                    if past(t, 1):
                        pe.wait_ge(q_logit, t)
                    for h in range(H):
                        dst_ = ps_m if H == 1 else ps_m[:, h // 4, (h % 4) * WIN:(h % 4 + 1) * WIN]
                        ins = nc.tensor.transpose(dst_[0:TN, :], masked[p][:, h, :, :].rearrange("p w n -> p (w n)")[:, 0:TN], net.ident[:, :])
                    ins.then_inc(q_mt, 1)

                def spread(t, p):
                    pe.wait_ge(q_nd, t + 1)
                    for w in range(2):
                        a = HALF * w
                        ins = nc.tensor.matmul(ps_e[:, w, :], onehot_t[p][a:a + HN[w], :],
                                               nd[p][a:a + HN[w], 1:1 + 2 * H], start=True, stop=True, skip_group_check=True)
                    ins.then_inc(q_g, 1)

                def aggregate(t, p):
                    if past(t, 1):
                        pe.wait_ge(q_oread if kind == "C" else q_pre, t)
                    if kind == "C":
                        pe.wait_ge(q_scaled, t + 1)
                        pe.wait_ge(q_scaled2, t + 1)
                        for b, n in ((0, HC), (1, HC + H)):
                            for w in range(2):
                                ins = nc.tensor.matmul(ps_a[HALF * w:HALF * w + HN[w], b, 0:n], onehot_k[p][:, w, 0:HN[w]],
                                                       scaled[p][:, w, b * HC:b * HC + n], start=True, stop=True)
                        ins.then_inc(q_agg, 1)
                        return
                    pe.wait_ge(q_coef, t + 1)
                    for b in range(2):
                        for w in range(2):
                            n = slice(HALF * w, HALF * w + HN[w])
                            ins = nc.tensor.matmul(ps_a[n, b, 0:HC], coef[p][:, w, 0:HN[w]], rows[p][:, w, b * HC:(b + 1) * HC],
                                                   start=True, stop=True)
                    for w in range(2):
                        ins = nc.tensor.matmul(ps_a[HALF * w:HALF * w + HN[w], 1, HC:HC + 1], coef[p][:, w, 0:HN[w]], net.ones[:, 0:1],
                                               start=True, stop=True)
                    ins.then_inc(q_agg, 1)

                def turn(t, p):
                    if attends:
                        pe.wait_ge(q_out, t + 1)
                    else:
                        pe.wait_ge(q_in[p], 16 * nth(t))
                    if past(t, 1):
                        pe.wait_ge(q_lo, 2 * t)
                    for k in range(KT):
                        c = (k % 3) * (TN + 1)
                        ins = nc.tensor.transpose(ps_t[:, k // 3, c:c + TN], o2[p][:, k * P:(k + 1) * P], net.ident[0:TN, 0:TN])
                    ins.then_inc(q_turn, 1)

                def product(t, p, k0, k1):
                    if k0 == 0:
                        pe.wait_ge(q_lo, 2 * t + 2)
                        if isinstance(t, int) and t == 0:
                            pe.wait_ge(q_wlo, 2)
                    for b, n in ((0, HC), (1, HC + NH)):
                        if k0 == 0 and past(t, 1):
                            pe.wait_ge(q_evac, 2 * t - 1 + b)
                        for k in range(k0, k1):
                            for a_, b_, first, last in ((t_hi, w_hi, k == 0, False), (t_hi, w_lo, False, False), (t_lo, w_hi, False, k == KT - 1)):
                                ins = nc.tensor.matmul(ps_h[0:TN, b, 0:n], a_[p][:, k, 0:TN], b_[:, k, b * HC:b * HC + n],
                                                       start=first, stop=last)
                        if k1 == KT:
                            ins.then_inc(q_prod, 1)

                def step(s, p):
                    cuts = {"B": (1, 4, 4), "C": (2, 4, 4), "X": (0, 0, 3)}.get(kind, (1, 3, 3))

                    def part(i):
                        k0, k1 = (0, *cuts, KT)[i:i + 2]
                        if k1 > k0 and has(s + PR, NT) and nxt is not None:
                            product(s + PR, q(p, PR), k0, k1)
                    if has(s + 1, NT) and kind in "ABC":
                        mask_t(s + 1, q(p, 1))
                    part(0)
                    if has(s + 1, NT) and attends:
                        spread(s + 1, q(p, 1))
                    if has(s + 2, NT) and kind == "D":
                        mask_t(s + 2, q(p, 2))
                    part(1)
                    if has(s + AG, NT) and attends:
                        aggregate(s + AG, q(p, AG))
                    part(2)
                    if has(s + TU, NT) and nxt is not None:
                        turn(s + TU, q(p, TU))
                    part(3)
                    if beside is not None and isinstance(s, int):
                        beside.pe(s)
                steps(pe, NT, -2 if kind == "D" else -1, -PR, step, NB)


def general_graph(nc, net, sem):
    NT = net.NT
    with ExitStack() as ctx:
        node_i = ctx.enter_context(nc.sbuf_tensor("self_i", [P, NT, 2], I32))
        edge_i = ctx.enter_context(nc.sbuf_tensor("edge_i", [P, NT, 2], I32))
        s_iota = sem("n_iota")
        with nc.Block() as block:
            @block.gpsimd
            def _(pool):
                nc.gpsimd.iota(node_i[:, :, :], pattern=[[TN, NT], [HALF, 2]], base=0, channel_multiplier=1).then_inc(s_iota, 1)
                nc.gpsimd.iota(edge_i[:, :, :], pattern=[[0, NT], [0, 2]], base=0, channel_multiplier=1).then_inc(s_iota, 1)

            @block.vector
            def _(dve):
                dve.wait_ge(s_iota, 2)
                nc.vector.tensor_scalar(net.src_idx[:, :, :], node_i[:, :, :], float(net.N - 1), None, ALU.min)
                nc.vector.tensor_copy(net.dst_rel[:, :, :], edge_i[:, :, :])


def general_sums(nc, net, name, sem, *, heads, own, table, row):
    N, E, NT, H = net.N, net.E, net.NT, heads
    NC = E // TN
    C = D // H
    src_cols = net.src.rearrange("(c e) -> c e", e=TN)
    with ExitStack() as ctx:
        def sb(n, shape, dt=F32):
            return ctx.enter_context(nc.sbuf_tensor(f"{name}_{n}", shape, dt))

        def s_(n):
            return sem(f"{name}_{n}")

        idx = sb("idx", [TN, 1], I32)
        rows = sb("rows", [TN, D + 8])
        s_idx = s_("idx"); s_row = s_("row"); s_store = s_("store"); s_pair = s_("pair"); s_turn = s_("turn")

        with nc.Block() as block:
            @block.sync
            def _(sp):
                with sp.Fori(0, NC) as c:
                    sp.dma_start(idx[:, :], src_cols[c].unsqueeze(1)).then_inc(s_idx, 16)
                    sp.wait_ge(s_row, 16 * c + 16)
                    with nc.allow_non_contiguous_dma(reason="four bytes per edge and head, in the slow path only"):
                        sp.dma_start(net.esrc[0:H, bass.ds(c * TN, TN)].rearrange("h e -> e h"), rows[:, D:D + H]).then_inc(s_store, 16)
                    sp.wait_ge(s_store, 16 * c + 16)
                    sp.sem_inc(s_turn, 1)

            @block.gpsimd
            def _(pool):
                with pool.Fori(0, NC) as c:
                    pool.wait_ge(s_idx, 16 * c + 16)
                    pool.sem_inc(s_pair, 1)
                    nc.gpsimd.indirect_dma_start(out=rows[:, 0:row], out_offset=None, in_=table[:, :],
                                                 in_offset=bass.IndirectOffsetOnAxis(ap=idx[:, 0:1], axis=0)).then_inc(s_row, 16)

    with ExitStack() as ctx:
        name += "s"
        idx = sb("idx", [TN, 1], I32)
        rows = sb("rows", [TN, D + 8])
        mine = sb("mine", [TN, D])
        part = sb("part", [TN, E])
        w = sb("w", [TN, E])
        zeros = sb("zeros", [TN, 8])
        c_ = sb("cells", [TN, 12])
        piece = sb("piece", [TN, TN])
        piece_t = sb("piece_t", [TN, TN])
        res = sb("res", [TN, 3, D])
        acc = net.bank2(0)
        s_to = s_("to"); s_part = s_("part"); s_idx = s_("idx"); s_row = s_("row"); s_own = s_("own"); s_go = s_("go")
        s_chain = s_("chain"); s_m = s_("m"); s_exp = s_("exp"); s_piece = s_("piece"); s_t = s_("t"); s_pt = s_("pt")
        s_mm = s_("mm"); s_res = s_("res"); s_store = s_("store"); s_turn = s_("turn")
        LINKS = 17 + (3 if own else 0)

        with nc.Block() as block:
            @block.sync
            def _(sp):
                with sp.Fori(0, H) as h:
                    sp.dma_start(part[:, :], bcast(net.esrc[h], 0, TN)).then_inc(s_part, 16)
                    with sp.Fori(0, NT) as t:
                        r = h * NT + t
                        sp.dma_start(w[:, :].bitcast(I32), bcast(net.dst, 0, TN)).then_inc(s_to, 16)
                        if own:
                            sp.dma_start(mine[:, :], net.tiles(table)[t][:, 0:D]).then_inc(s_own, 16)
                        with sp.Fori(0, NC) as c:
                            sp.dma_start(idx[:, :], src_cols[c].unsqueeze(1)).then_inc(s_idx, 16)
                            sp.wait_ge(s_mm, r * NC + c + 1)
                            sp.sem_inc(s_turn, 1)
                        sp.wait_ge(s_res, r + 1)
                        sp.dma_start(net.tiles(net.agg)[t][:, bass.ds(h * C, C)], res[:, 2, 0:C]).then_inc(s_store, 16)
                        sp.dma_start(net.tiles(net.agg)[t][:, D:D + 8], zeros[:, :]).then_inc(s_store, 16)
                        sp.wait_ge(s_store, 32 * r + 32)
                        sp.sem_inc(s_turn, 1)

            @block.gpsimd
            def _(pool):
                with pool.Fori(0, H * NT * NC) as k:
                    pool.wait_ge(s_idx, 16 * k + 16)
                    pool.sem_inc(s_go, 1)
                    nc.gpsimd.indirect_dma_start(out=rows[:, 0:row], out_offset=None, in_=table[:, :],
                                                 in_offset=bass.IndirectOffsetOnAxis(ap=idx[:, 0:1], axis=0)).then_inc(s_row, 16)

            @block.scalar
            def _(act):
                with act.Fori(0, H * NT) as r:
                    act.wait_ge(s_m, r + 1)
                    if own:
                        nc.scalar.activation(c_[:, 7:8], c_[:, 6:7], ACT.Exp)
                    nc.scalar.activation(w[:, :], w[:, :], ACT.Exp, bias=c_[:, 4:5]).then_inc(s_exp, 1)

            @block.vector
            def _(dve):
                nc.vector.memset(zeros[:, :], 0.0)
                with dve.Fori(0, H) as h:
                    dve.wait_ge(s_part, 16 * h + 16)
                    dve.sem_inc(s_turn, 1)
                    with dve.Fori(0, NT) as t:
                        r = h * NT + t
                        n = [0]

                        def link(ins):
                            n[0] += 1
                            ins.then_inc(s_chain, 1)
                            dve.wait_ge(s_chain, r * LINKS + n[0])

                        dve.wait_ge(s_to, 16 * r + 16)
                        link(nc.vector.tensor_copy(w[:, :], w[:, :].bitcast(I32)))
                        link(nc.vector.tensor_scalar(w[:, :], w[:, :], net.node_ids[:, bass.ds(t, 1)], None, ALU.is_equal))
                        link(nc.vector.tensor_scalar(w[:, :], w[:, :], -1.0, BIG, ALU.add, ALU.mult))
                        link(nc.vector.tensor_tensor(w[:, :], w[:, :], part[:, :], ALU.add))
                        if H == 1:
                            link(nc.vector.tensor_copy(c_[:, 0:2], net.e_own[:, t, :]))
                        else:
                            link(nc.vector.tensor_copy(c_[:, 1:2], net.e_dst8.rearrange("p t h -> p (t h)")[:, bass.ds(t * 8 + h, 1)]))
                        link(nc.vector.tensor_reduce(c_[:, 2:3], w[:, :], AX.X, ALU.max))
                        if own:
                            link(nc.vector.scalar_tensor_tensor(out=c_[:, 2:3], in0=c_[:, 2:3], scalar=c_[:, 0:1], in1=c_[:, 1:2],
                                                                op0=ALU.max, op1=ALU.add))
                        else:
                            link(nc.vector.tensor_tensor(c_[:, 2:3], c_[:, 2:3], c_[:, 1:2], ALU.add))
                        link(nc.vector.scalar_tensor_tensor(out=c_[:, 3:4], in0=c_[:, 2:3], scalar=SLOPE, in1=c_[:, 2:3],
                                                            op0=ALU.mult, op1=ALU.max))
                        link(nc.vector.tensor_scalar(c_[:, 4:5], c_[:, 3:4], -BIG / 100, -1.0, ALU.max, ALU.mult))
                        if own:
                            link(nc.vector.tensor_tensor(c_[:, 5:6], c_[:, 0:1], c_[:, 1:2], ALU.add))
                            link(nc.vector.scalar_tensor_tensor(out=c_[:, 5:6], in0=c_[:, 5:6], scalar=SLOPE, in1=c_[:, 5:6],
                                                                op0=ALU.mult, op1=ALU.max))
                            link(nc.vector.tensor_tensor(c_[:, 6:7], c_[:, 5:6], c_[:, 4:5], ALU.add))
                        link(nc.vector.tensor_scalar(w[:, :], w[:, :], c_[:, 1:2], None, ALU.add))
                        link(nc.vector.scalar_tensor_tensor(out=w[:, :], in0=w[:, :], scalar=SLOPE, in1=w[:, :], op0=ALU.mult, op1=ALU.max))
                        dve.sem_inc(s_m, 1)
                        dve.wait_ge(s_exp, r + 1)
                        link(nc.vector.tensor_reduce(c_[:, 8:9], w[:, :], AX.X, ALU.add))
                        link(nc.vector.tensor_scalar(c_[:, 9:10], c_[:, 8:9], c_[:, 7:8] if own else 1e-16, None, ALU.add))
                        link(nc.vector.reciprocal(c_[:, 10:11], c_[:, 9:10]))
                        dve.sem_inc(s_turn, 1)
                        with dve.Fori(0, NC) as c:
                            nc.vector.tensor_copy(piece[:, :], w[:, bass.ds(c * TN, TN)]).then_inc(s_piece, 1)
                            dve.wait_ge(s_t, r * NC + c + 1)
                            nc.vector.tensor_copy(piece_t[:, :], net.bank[2][0:TN, 0:TN]).then_inc(s_pt, 1)
                            dve.wait_ge(s_mm, r * NC + c + 1)
                        if own:
                            dve.wait_ge(s_own, 16 * r + 16)
                            link(nc.vector.tensor_scalar(res[:, 0, :], mine[:, :], c_[:, 7:8], None, ALU.mult))
                        else:
                            link(nc.vector.memset(res[:, 0, :], 0.0))
                        o = acc[0:TN, :, 0:C // 2] if H == 1 else acc[0:TN, 0:1, 0:C]
                        nb = 2 if H == 1 else 1
                        link(nc.vector.tensor_tensor(res[:, 1, 0:C].rearrange("p (b c) -> p b c", b=nb), o,
                                                        res[:, 0, 0:C].rearrange("p (b c) -> p b c", b=nb), ALU.add))
                        link(nc.vector.tensor_scalar(res[:, 2, 0:C], res[:, 1, 0:C], c_[:, 10:11], None, ALU.mult))
                        dve.sem_inc(s_res, 1)
                        dve.wait_ge(s_store, 32 * r + 32)
                        assert n[0] == LINKS, n

            @block.tensor
            def _(pe):
                def chunk(k, h, first):
                    pe.wait_ge(s_piece, k + 1)
                    nc.tensor.transpose(net.bank[2][0:TN, 0:TN], piece[:, :], net.ident[0:TN, 0:TN]).then_inc(s_t, 1)
                    pe.wait_ge(s_pt, k + 1)
                    pe.wait_ge(s_row, 16 * k + 16)
                    if H == 1:
                        for b in range(2):
                            ins = nc.tensor.matmul(acc[0:TN, b, 0:HC], piece_t[:, :], rows[:, b * HC:(b + 1) * HC],
                                                   start=first, stop=True, skip_group_check=True)
                    else:
                        ins = nc.tensor.matmul(acc[0:TN, 0, 0:C], piece_t[:, :], rows[:, bass.ds(h * C, C)],
                                               start=first, stop=True, skip_group_check=True)
                    ins.then_inc(s_mm, 1)

                with pe.Fori(0, H) as h:
                    with pe.Fori(0, NT) as t:
                        k = (h * NT + t) * NC
                        chunk(k, h, True)
                        with pe.Fori(1, NC) as c:
                            chunk(k + c, h, False)


def gat_program(nc, ext, out, N, E):
    with ExitStack() as ctx:
        net = Net()
        net.N, net.E, net.NT = N, E, N // TN
        NT = net.NT

        def sb(name, shape, dt=F32):
            return ctx.enter_context(nc.sbuf_tensor(name, shape, dt))

        def dram(name, shape, dt=F32):
            return nc.dram_tensor(name, shape, dt, kind="Internal").ap()

        sems = []

        def sem(name):
            sems.append(nc.alloc_semaphore(name))
            return sems[-1]

        def retire():
            nc.clear_and_free_semaphores(list(sems))
            sems.clear()
            nc.all_engine_barrier()

        net.w = [ext[n] for n in ("L0_gnn_W1", "L0_gnn_W2", "L1_gnn_W1", "L1_gnn_W2")]
        net.w_in = sb("w_in", [P, KT, D])
        net.w_att = sb("w_att", [P, KT, 22])
        net.att_col = [0, 2, 4, 20]
        net.ident = sb("ident", [P, P])
        net.ones = sb("ones", [P, 2])
        net.minus_half = sb("minus_half", [P, 1])
        net.node = sb("node", [P, 2, HALF])
        net.src_idx = sb("src_idx", [P, NT, 2], I32)
        net.dst_rel = sb("dst_rel", [P, NT, 2])
        net.e_own = sb("e_own", [TN, NT, 2])
        net.e_dst8 = sb("e_dst8", [TN, NT, 8])
        net.starts = sb("starts", [P, NT, 2])
        net.lo_i = sb("lo_i", [1, 2 * NT], I32)
        net.flag = sb("flag", [1, 1], I32)
        net.node_ids = sb("node_ids", [TN, NT])
        psum = ctx.enter_context(nc.psum_tensor("psum", [P, 8, OB], F32))
        net.psum = psum
        net.bank = [psum[:, b, :] for b in range(8)]
        net.bank2 = lambda b: psum[:, b:b + 2, :]
        net.edges = dram("edges", [2, E + WIN], I32)
        net.windows = dram("windows", [2 * NT, 2, WIN], I32)
        tables = [dram("h1", [N, D + 2]), dram("h2", [N, D + 2]), dram("h3", [N, D + 16]), dram("h4", [N, D + 2])]
        net.x1 = dram("x1", [N, D])
        net.agg = dram("agg", [N, D + 8])
        net.esrc = dram("esrc", [8, E])
        net.src, net.dst = ext["src"], ext["dst"]
        net.tiles = lambda a: a.rearrange("(t p) d -> t p d", p=TN)
        x = ext["x"]

        prepare(nc, net, ext, sem)
        retire()
        flag = nc.values_load(net.flag[0:1, 0:1], min_val=0, max_val=TN + 1)

        layers = [dict(kind="A", heads=1, own=True, bias=ext["L0_gnn_b1"], nxt=(1, 1, tables[1])),
                  dict(kind="B", heads=1, own=True, bias=ext["L0_gnn_b2"], residual=x, out_rows=net.x1, nxt=(2, 8, tables[2])),
                  dict(kind="C", heads=8, bias=ext["L1_gnn_b1"], nxt=(3, 1, tables[3])),
                  dict(kind="D", heads=1, bias=ext["L1_gnn_b2"], residual=net.x1, out_rows=out)]
        with ExitStack() as beside:
            layer_phase(nc, net, "X", sem, "X", table=x, nxt=(0, 1, tables[0]), beside=beside_projection(nc, net, ext, sem, beside))
        retire()
        with nc.If(flag == 0):
            for layer, table in zip(layers, tables):
                layer_phase(nc, net, layer["kind"], sem, table=table, row=D + layer["heads"], **layer)
                retire()
        with nc.Else():
            for j, (layer, table) in enumerate(zip(layers, tables)):
                kind = layer["kind"]
                general_sums(nc, net, f"s{kind}", sem, heads=layer["heads"], own=layer.get("own", False), table=table,
                             row=D + layer["heads"])
                retire()
                if j == 0:
                    general_graph(nc, net, sem)
                    retire()
                layer_phase(nc, net, f"g{kind}", sem, table=net.agg, row=D + layer["heads"], **layer)
                retire()


_INS = ["x", "src", "dst", "L0_gnn_W1", "L0_gnn_att_src1", "L0_gnn_att_dst1", "L0_gnn_b1", "L0_gnn_W2", "L0_gnn_att_src2",
        "L0_gnn_att_dst2", "L0_gnn_b2", "L1_gnn_W1", "L1_gnn_a_src1", "L1_gnn_a_dst1", "L1_gnn_b1", "L1_gnn_W2",
        "L1_gnn_a_src2", "L1_gnn_a_dst2", "L1_gnn_b2"]


def kernel(**inputs):
    import numpy as _np
    import concourse.bacc as _bacc
    from concourse import mybir as _mybir
    from concourse.bass_utils import run_bass_kernel_spmd as _run

    nc = _bacc.Bacc("TRN2", target_bir_lowering=False, num_devices=1)
    arrays, ext = {}, {}
    for name in _INS:
        a = _np.ascontiguousarray(inputs[name])
        arrays[f"in_{name}"] = a
        ext[name] = nc.dram_tensor(f"in_{name}", a.shape, _mybir.dt.from_np(a.dtype), kind="ExternalInput").ap()
    shape = arrays["in_x"].shape
    out = nc.dram_tensor("out_0", shape, _mybir.dt.float32, kind="ExternalOutput").ap()
    gat_program(nc, ext, out, shape[0], arrays["in_src"].shape[0])
    r = _run(nc, [arrays], core_ids=[0])
    return r.results[0]["out_0"]
```
